# Optimizing a Trainium2 kernel written in Bass

```python
import numpy as np
import jax
import jax.numpy as jnp

def _softmax(x, axis=-1):
    return jax.nn.softmax(x, axis=axis)

def _gelu(x):
    return jax.nn.gelu(x, approximate=True)

def _silu(x):
    return jax.nn.silu(x)

def _sigmoid(x):
    return jax.nn.sigmoid(x)

def _layernorm(x, axis=-1, eps=1e-05):
    m = jnp.mean(x, axis=axis, keepdims=True)
    v = jnp.var(x, axis=axis, keepdims=True)
    return (x - m) / jnp.sqrt(v + eps)

def _scatter_add(tgt, idx, src, axis=0):
    return tgt.at[idx].add(src)

def _segment_sum(src, seg, n):
    return jax.ops.segment_sum(src, seg, n)
kernel_name = 'mk_cond_resid_d4_seqx_r8_16303d'

def setup_inputs(seed: int=0):
    np.random.seed(seed)
    _w = jnp.asarray

    def _rec_inputs():
        import jax
        import jax.numpy as jnp
        _rk = jax.random.key(seed)
        x = -0.000125 + 0.9999 * jax.random.normal(jax.random.fold_in(_rk, 1), (8, 128, 512), jnp.float32)
        _lenS = 128 - jax.random.randint(jax.random.fold_in(_rk, 7), (8,), 0, max(1, 128 // 4) + 1, jnp.int32)
        _lenS2 = 128 - jax.random.randint(jax.random.fold_in(_rk, 8), (8,), 0, max(1, 128 // 4) + 1, jnp.int32)
        condB_codebook = -0.0625 + 0.715345 * jax.random.normal(jax.random.fold_in(_rk, 11), (8,), jnp.float32)
        itok_B_1_7 = jax.random.randint(jax.random.fold_in(_rk, 12), (8,), 1, 8, jnp.int32)
        itok_Bx16_0_63 = jax.random.randint(jax.random.fold_in(_rk, 13), (8, 16), 0, 64, jnp.int32)
        itok_B_207_1644 = jax.random.randint(jax.random.fold_in(_rk, 14), (8,), 207, 1645, jnp.int32)
        condB_coeff = 0.00219231 + 0.0100837 * jax.random.normal(jax.random.fold_in(_rk, 15), (8,), jnp.float32)
        _validS = jnp.arange(128)[None, :] < _lenS[:, None]
        _validS2 = jnp.arange(128)[None, :] < _lenS2[:, None]
        _causal = jnp.tril(jnp.ones((128, 128), dtype=bool))
        mask_Bx4096x4096_ik1 = jnp.where(jnp.ones((8, 512, 512), dtype=bool), 1, 0).astype(jnp.int32)
        return (x, condB_codebook, itok_B_1_7, itok_Bx16_0_63, itok_B_207_1644, condB_coeff, mask_Bx4096x4096_ik1)
    x, condB_codebook, itok_B_1_7, itok_Bx16_0_63, itok_B_207_1644, condB_coeff, mask_Bx4096x4096_ik1 = _rec_inputs()

    def _L0_cond_setup():
        import jax, jax.numpy as jnp
        import numpy as np
        GROUP = 128
        LORA_ALPHA = 32.0
        LORA_RANK = 64
        key = jax.random.key(seed)
        k1, k2, k3, k4 = jax.random.split(key, 4)
        O, I = (512, 512)
        x = jax.random.normal(k1, (4, 256, I), dtype=jnp.float32)
        weight = jax.random.normal(k2, (O, I), dtype=jnp.float32) * 0.02
        wg = weight.reshape(O, I // GROUP, GROUP)
        scale_log = jnp.log(jnp.clip(jnp.max(jnp.abs(wg), axis=2, keepdims=True), 1e-05))
        codebook = jnp.array([-1.0, -0.25, 0.0, 1.0], dtype=jnp.float32)
        lora_A = jax.random.normal(k3, (LORA_RANK, I), dtype=jnp.float32) * 0.02
        lora_B = jax.random.normal(k4, (O, LORA_RANK), dtype=jnp.float32) * 0.02
        return {'x': x, 'weight': weight, 'scale_log': scale_log, 'codebook': codebook, 'lora_A': lora_A, 'lora_B': lora_B}
    _L0_cond_all = _L0_cond_setup()
    _L0_cond_in = {k: v for k, v in _L0_cond_all.items() if k in ('weight', 'scale_log', 'lora_A', 'lora_B')}
    del _L0_cond_all

    def _L1_cond_setup():
        import jax, jax.numpy as jnp
        import numpy as np
        B, S, D_IN, D_OUT = (4, 256, 512, 512)
        N_ADAPTERS, MAX_RANK = (8, 16)
        key = jax.random.key(seed)
        ks = jax.random.split(key, 7)
        x = jax.random.normal(ks[0], (B, S, D_IN), dtype=jnp.float32)
        weight = jax.random.normal(ks[1], (D_OUT, D_IN), dtype=jnp.float32) * (1.0 / np.sqrt(D_IN))
        bias = jax.random.normal(ks[2], (D_OUT,), dtype=jnp.float32) * 0.01
        lora_a_weights = jax.random.normal(ks[3], (N_ADAPTERS, MAX_RANK, D_IN), dtype=jnp.float32) * (1.0 / np.sqrt(D_IN))
        lora_b_weights = jax.random.normal(ks[4], (N_ADAPTERS, D_OUT, MAX_RANK), dtype=jnp.float32) * 0.02
        scaling_factors = jax.random.uniform(ks[5], (N_ADAPTERS,), dtype=jnp.float32, minval=0.5, maxval=2.0)
        adapter_id = jax.random.randint(ks[6], (B,), 0, N_ADAPTERS, dtype=jnp.int64)
        return {'x': x, 'weight': weight, 'bias': bias, 'lora_a_weights': lora_a_weights, 'lora_b_weights': lora_b_weights, 'scaling_factors': scaling_factors, 'adapter_id': adapter_id}
    _L1_cond_all = _L1_cond_setup()
    _L1_cond_in = {k: v for k, v in _L1_cond_all.items() if k in ('weight', 'bias', 'lora_a_weights', 'lora_b_weights', 'scaling_factors')}
    del _L1_cond_all

    def _L2_cond_setup():
        import jax, jax.numpy as jnp
        import numpy as np
        B, S, HID = (4, 128, 512)
        D, HQ, HK = (128, 32, 8)
        PAGES, PSIZE, NPP = (64, 32, 16)
        THETA = 10000.0
        EPS = 1e-06
        SCALE = 1.0 / float(np.sqrt(D))

        def _rmsnorm(t, w):
            var = jnp.mean(t * t, axis=-1, keepdims=True)
            return t * jax.lax.rsqrt(var + EPS) * w

        def _rope(t, pos):
            inv_freq = 1.0 / THETA ** (jnp.arange(0, D, 2, dtype=jnp.float32) / D)
            freqs = pos[..., None].astype(jnp.float32) * inv_freq
            cos = jnp.cos(freqs)[:, :, None, :]
            sin = jnp.sin(freqs)[:, :, None, :]
            t1, t2 = (t[..., :D // 2], t[..., D // 2:])
            return jnp.concatenate([t1 * cos - t2 * sin, t2 * cos + t1 * sin], axis=-1)
        key = jax.random.key(seed)
        ks = jax.random.split(key, 10)
        x = jax.random.normal(ks[0], (B, S, HID), jnp.float32)
        Wq = jax.random.normal(ks[1], (HQ * D, HID), jnp.float32) * 0.02
        Wk = jax.random.normal(ks[2], (HK * D, HID), jnp.float32) * 0.02
        Wv = jax.random.normal(ks[3], (HK * D, HID), jnp.float32) * 0.02
        Wo = jax.random.normal(ks[4], (HID, HQ * D), jnp.float32) * 0.02
        q_norm_w = jax.random.uniform(ks[5], (D,), jnp.float32)
        k_norm_w = jax.random.uniform(ks[6], (D,), jnp.float32)
        k_cache = jax.random.normal(ks[7], (PAGES, PSIZE, HK, D), jnp.float32)
        v_cache = jax.random.normal(ks[8], (PAGES, PSIZE, HK, D), jnp.float32)
        block_table = jnp.arange(B * NPP, dtype=jnp.int32).reshape(B, NPP)
        cache_seqlens = jax.random.randint(ks[9], (B,), 0, 475).astype(jnp.int32)
        return dict(x=x, Wq=Wq, Wk=Wk, Wv=Wv, Wo=Wo, q_norm_w=q_norm_w, k_norm_w=k_norm_w, k_cache=k_cache, v_cache=v_cache, block_table=block_table, cache_seqlens=cache_seqlens)
    _L2_cond_all = _L2_cond_setup()
    _L2_cond_in = {k: v for k, v in _L2_cond_all.items() if k in ('Wq', 'Wk', 'Wv', 'Wo', 'q_norm_w', 'k_norm_w', 'k_cache', 'v_cache')}
    del _L2_cond_all

    def _L3_cond_setup():
        import jax, jax.numpy as jnp
        import numpy as np
        B, S, D_IN, D_OUT = (4, 64, 512, 512)
        key = jax.random.key(seed)
        k1, k2, k3, k4, k5 = jax.random.split(key, 5)
        hidden_states = jax.random.normal(k1, (B, S, D_IN), dtype=jnp.float32)
        W = jax.random.normal(k2, (D_OUT, D_IN), dtype=jnp.float32) * 0.02
        b = jax.random.normal(k3, (D_OUT,), dtype=jnp.float32) * 0.02
        coeff = jax.random.normal(k4, (B,), dtype=jnp.float32) * 0.01
        mask = jax.random.randint(k5, (B, D_IN, D_OUT), 0, 2, dtype=jnp.int32)
        return {'hidden_states': hidden_states, 'W': W, 'b': b, 'coeff': coeff, 'mask': mask}
    _L3_cond_all = _L3_cond_setup()
    _L3_cond_in = {k: v for k, v in _L3_cond_all.items() if k in ('W', 'b')}
    del _L3_cond_all
    return {'x': x, 'condB_codebook': condB_codebook, 'itok_B_1_7': itok_B_1_7, 'itok_Bx16_0_63': itok_Bx16_0_63, 'itok_B_207_1644': itok_B_207_1644, 'condB_coeff': condB_coeff, 'mask_Bx4096x4096_ik1': mask_Bx4096x4096_ik1, 'L0_cond_weight': _L0_cond_in['weight'], 'L0_cond_scale_log': _L0_cond_in['scale_log'], 'L0_cond_lora_A': _L0_cond_in['lora_A'], 'L0_cond_lora_B': _L0_cond_in['lora_B'], 'L1_cond_weight': _L1_cond_in['weight'], 'L1_cond_bias': _L1_cond_in['bias'], 'L1_cond_lora_a_weights': _L1_cond_in['lora_a_weights'], 'L1_cond_lora_b_weights': _L1_cond_in['lora_b_weights'], 'L1_cond_scaling_factors': _L1_cond_in['scaling_factors'], 'L2_cond_Wq': _L2_cond_in['Wq'], 'L2_cond_Wk': _L2_cond_in['Wk'], 'L2_cond_Wv': _L2_cond_in['Wv'], 'L2_cond_Wo': _L2_cond_in['Wo'], 'L2_cond_q_norm_w': _L2_cond_in['q_norm_w'], 'L2_cond_k_norm_w': _L2_cond_in['k_norm_w'], 'L2_cond_k_cache': _L2_cond_in['k_cache'], 'L2_cond_v_cache': _L2_cond_in['v_cache'], 'L3_cond_W': _L3_cond_in['W'], 'L3_cond_b': _L3_cond_in['b']}

def reference(x, condB_codebook, itok_B_1_7, itok_Bx16_0_63, itok_B_207_1644, condB_coeff, mask_Bx4096x4096_ik1, L0_cond_weight, L0_cond_scale_log, L0_cond_lora_A, L0_cond_lora_B, L1_cond_weight, L1_cond_bias, L1_cond_lora_a_weights, L1_cond_lora_b_weights, L1_cond_scaling_factors, L2_cond_Wq, L2_cond_Wk, L2_cond_Wv, L2_cond_Wo, L2_cond_q_norm_w, L2_cond_k_norm_w, L2_cond_k_cache, L2_cond_v_cache, L3_cond_W, L3_cond_b):
    import jax
    import jax.numpy as jnp

    def _L0_cond_ref(x, weight, scale_log, codebook, lora_A, lora_B):
        import jax, jax.numpy as jnp
        import numpy as np
        GROUP = 128
        LORA_ALPHA = 32.0
        LORA_RANK = 64
        O, I = weight.shape
        lora_delta = lora_B @ lora_A * (LORA_ALPHA / LORA_RANK)
        cb = codebook / jnp.clip(jnp.max(jnp.abs(codebook)), 1e-08)
        scale = jnp.exp(scale_log)
        wg = (weight + lora_delta).reshape(O, I // GROUP, GROUP)
        normalized = wg / scale
        thresholds = (cb[:-1] + cb[1:]) * 0.5
        idx = jnp.searchsorted(thresholds, normalized, side='left')
        quantized = cb[idx]
        w = jax.lax.stop_gradient(quantized - normalized) + normalized
        w_q = (w * scale).reshape(O, I)
        w_eff = w_q + lora_delta
        return x @ w_eff.T

    def _L1_cond_ref(x, weight, bias, lora_a_weights, lora_b_weights, scaling_factors, adapter_id):
        import jax, jax.numpy as jnp
        import numpy as np
        B, S, D_IN, D_OUT = (4, 256, 512, 512)
        N_ADAPTERS, MAX_RANK = (8, 16)
        base = jnp.einsum('bsi,oi->bso', x, weight) + bias
        a_sel = lora_a_weights[adapter_id]
        b_sel = lora_b_weights[adapter_id]
        scale = scaling_factors[adapter_id]
        low = jnp.einsum('bsi,bri->bsr', x, a_sel)
        delta = jnp.einsum('bsr,bor->bso', low, b_sel)
        return base + scale[:, None, None] * delta

    def _L2_cond_ref(x, Wq, Wk, Wv, Wo, q_norm_w, k_norm_w, k_cache, v_cache, block_table, cache_seqlens):
        import jax, jax.numpy as jnp
        import numpy as np
        B, S, HID = (4, 128, 512)
        D, HQ, HK = (128, 32, 8)
        PAGES, PSIZE, NPP = (64, 32, 16)
        THETA = 10000.0
        EPS = 1e-06
        SCALE = 1.0 / float(np.sqrt(D))

        def _rmsnorm(t, w):
            var = jnp.mean(t * t, axis=-1, keepdims=True)
            return t * jax.lax.rsqrt(var + EPS) * w

        def _rope(t, pos):
            inv_freq = 1.0 / THETA ** (jnp.arange(0, D, 2, dtype=jnp.float32) / D)
            freqs = pos[..., None].astype(jnp.float32) * inv_freq
            cos = jnp.cos(freqs)[:, :, None, :]
            sin = jnp.sin(freqs)[:, :, None, :]
            t1, t2 = (t[..., :D // 2], t[..., D // 2:])
            return jnp.concatenate([t1 * cos - t2 * sin, t2 * cos + t1 * sin], axis=-1)
        bsz, seqlen, _ = x.shape
        q = jnp.einsum('bsd,ed->bse', x, Wq).reshape(bsz, seqlen, HQ, D)
        k = jnp.einsum('bsd,ed->bse', x, Wk).reshape(bsz, seqlen, HK, D)
        v = jnp.einsum('bsd,ed->bse', x, Wv).reshape(bsz, seqlen, HK, D)
        q = _rmsnorm(q, q_norm_w)
        k = _rmsnorm(k, k_norm_w)
        pos = cache_seqlens[:, None] + jnp.arange(seqlen)[None, :]
        q = _rope(q, pos)
        k = _rope(k, pos)
        L = NPP * PSIZE
        kc = k_cache[block_table].reshape(bsz, L, HK, D)
        vc = v_cache[block_table].reshape(bsz, L, HK, D)
        k_all = jnp.concatenate([kc, k], axis=1)
        v_all = jnp.concatenate([vc, v], axis=1)
        valid_c = jnp.arange(L)[None, :] < cache_seqlens[:, None]
        valid = jnp.concatenate([valid_c, jnp.ones((bsz, seqlen), dtype=bool)], axis=1)
        rep = HQ // HK
        k_all = jnp.repeat(k_all, rep, axis=2)
        v_all = jnp.repeat(v_all, rep, axis=2)
        scores = jnp.einsum('bqhd,bkhd->bhqk', q, k_all) * SCALE
        scores = jnp.where(valid[:, None, None, :], scores, -1e+30)
        probs = jax.nn.softmax(scores, axis=-1)
        o = jnp.einsum('bhqk,bkhd->bqhd', probs, v_all)
        o = o.reshape(bsz, seqlen, HQ * D)
        return jnp.einsum('bse,de->bsd', o, Wo)

    def _L3_cond_ref(hidden_states, W, b, coeff, mask):
        import jax, jax.numpy as jnp
        import numpy as np
        B, S, D_IN, D_OUT = (4, 64, 512, 512)
        output = jnp.einsum('bsi,oi->bso', hidden_states, W) + b
        sign = (2 * mask - 1).astype(hidden_states.dtype)
        diff = jnp.einsum('bsi,bio->bso', hidden_states, sign)
        return output + diff * coeff[:, None, None]
    x = x + _L0_cond_ref(x, L0_cond_weight, L0_cond_scale_log, condB_codebook, L0_cond_lora_A, L0_cond_lora_B)
    x = x + _L1_cond_ref(x, L1_cond_weight, L1_cond_bias, L1_cond_lora_a_weights, L1_cond_lora_b_weights, L1_cond_scaling_factors, itok_B_1_7)
    x = x + _L2_cond_ref(x, L2_cond_Wq, L2_cond_Wk, L2_cond_Wv, L2_cond_Wo, L2_cond_q_norm_w, L2_cond_k_norm_w, L2_cond_k_cache, L2_cond_v_cache, itok_Bx16_0_63, itok_B_207_1644)
    x = x + _L3_cond_ref(x, L3_cond_W, L3_cond_b, condB_coeff, mask_Bx4096x4096_ik1)
    return x

_drawn_inputs = setup_inputs


def setup_inputs(seed=0):
    import zlib

    import numpy as np

    out = dict(_drawn_inputs(seed))
    spreads = {}
    factors = {'L1_cond_bias': 8.0,
     'L1_cond_scaling_factors': 3.489,
     'L2_cond_Wq': 3.242,
     'L2_cond_Wk': 8.0,
     'L2_cond_Wv': 6.292,
     'L2_cond_q_norm_w': 5.611,
     'L2_cond_k_norm_w': 8.0,
     'L2_cond_k_cache': 3.298,
     'L3_cond_b': 17.617}
    for name, (base, spread) in spreads.items():
        noise = np.random.default_rng([zlib.crc32(name.encode()), seed]).standard_normal(out[name].shape)
        drawn = base * np.exp(spread * noise) if base else spread * noise
        out[name] = jnp.asarray(drawn.astype(out[name].dtype))
    for name, factor in factors.items():
        out[name] = (out[name] * factor).astype(out[name].dtype)
    return out
```

```python
import concourse.bass as bass
from concourse import mybir
from contextlib import ExitStack
import numpy as np

FP32 = mybir.dt.float32
F32R = mybir.dt.float32r
I32 = mybir.dt.int32
ALU = mybir.AluOpType
ACT = mybir.ActivationFunctionType
AX = mybir.AxisListType

P = 128
B = 8
D = 512
C = D // P
G = 8
R = 4
PAGE = 32
NPAGE = 16
PAGES = 64
CACHE = NPAGE * PAGE
KT = CACHE // P
KEYS = CACHE + P
JT = KEYS // P
STEPS = G * B
QKV = R * P + 2 * P
REGION = C * QKV + R * D
CHUNKS = 8
CHUNK = REGION // CHUNKS
LEAD = 9
SCALE = 1.0 / float(np.sqrt(P))
EPS = 1e-6
NEG = -1e30
RANK = 16
ADAPTERS = 8
LORA_SCALE = 32.0 / 64.0
MAGIC = 1.5 * 2.0 ** 23
TWO_PI = 2.0 * np.pi
PI_A = 6.28125
PI_B = float(np.float32(0.0019350051879882812))
PI_C = float(np.float32(TWO_PI - PI_A - PI_B))
LN2_A = 0.693359375
LN2_B = float(np.float32(np.log(2.0) - LN2_A))
BELOW_PI = 3.1415925


def wait(engine, semaphore, value):
    if isinstance(value, int) and value <= 0:
        return
    engine.wait_ge(semaphore, value)


def matmul(nc, o, l, r, start, stop):
    return nc.tensor.matmul(o, l, r, start=start, stop=stop)


def passes(nc, o, terms, first=True, last=True):
    for i, (lh, ll, rh, rl) in enumerate(terms):
        matmul(nc, o, lh, rh, first and i == 0, False)
        matmul(nc, o, ll, rh, False, False)
        done = matmul(nc, o, lh, rl, False, last and i == len(terms) - 1)
    return done


def attention(nc, outer, acc, xTs, qA, qB, kA, kB, ident, key_no, seqf, pages, wH, wL, wr, wall, k_cache, v_cache):
    ctx = ExitStack()
    with ctx:
        def sbuf(name, shape, dt=FP32):
            return ctx.enter_context(nc.sbuf_tensor(name, shape, dt))

        def psum(name, shape):
            return ctx.enter_context(nc.psum_tensor(name, shape, FP32))

        def sem(name):
            return ctx.enter_context(nc.semaphore(name))

        xH = sbuf("xH", [P, C, P], F32R)
        xL = sbuf("xL", [P, C, P], F32R)
        k_raw = [sbuf(f"k_raw{i}", [P, KT, P]) for i in range(2)]
        v_raw = [sbuf(f"v_raw{i}", [P, KT, P]) for i in range(2)]
        vH = [sbuf(f"vH{i}", [P, JT, P], F32R) for i in range(2)]
        vL = [sbuf(f"vL{i}", [P, JT, P], F32R) for i in range(2)]
        kH = sbuf("kH", [P, KEYS], F32R)
        kL = sbuf("kL", [P, KEYS], F32R)
        qH = sbuf("qH", [P, R * P], F32R)
        qL = sbuf("qL", [P, R * P], F32R)
        q_u = sbuf("q_u", [P, R, P])
        q_w = sbuf("q_w", [P, R, P])
        q_rot = sbuf("q_rot", [P, R, P])
        kv = sbuf("kv", [P, 2, P])
        k_u = sbuf("k_u", [P, P])
        k_w = sbuf("k_w", [P, P])
        k_s = sbuf("k_s", [P, P])
        k_rot = sbuf("k_rot", [P, P])
        squares = sbuf("squares", [P, R + 1, P])
        sums = sbuf("sums", [P, R + 1])
        mean = sbuf("mean", [P, R + 1])
        halves = sbuf("halves", [P, R + 1])
        rinv = sbuf("rinv", [P, R + 1])
        pos_scale = [sbuf(f"pos_scale{i}", [P, R]) for i in range(2)]
        neg_scale = [sbuf(f"neg_scale{i}", [P, R]) for i in range(2)]
        late = sbuf("late", [P, CACHE])
        new_max = sbuf("new_max", [P, R])
        row_max = sbuf("row_max", [P, R])
        bias = [sbuf(f"bias{i}", [P, R]) for i in range(2)]
        prob = [sbuf(f"prob{i}", [P, R, KEYS]) for i in range(2)]
        den = sbuf("den", [P, R, 2])
        den_sum = sbuf("den_sum", [P, R])
        den_inv = [sbuf(f"den_inv{i}", [P, R]) for i in range(2)]
        ptH = [sbuf(f"ptH{i}", [P, R * P], F32R) for i in range(2)]
        ptL = [sbuf(f"ptL{i}", [P, R * P], F32R) for i in range(2)]
        oH = sbuf("oH", [P, R * P], F32R)
        oL = sbuf("oL", [P, R * P], F32R)
        table_out = sbuf("table_out", [P, 1])

        s_cached = [psum(f"s_cached{i}", [P, CACHE]) for i in range(2)]
        s_new = psum("s_new", [P, R * P])
        turned = [psum(f"turned{i}", [P, R * P]) for i in range(2)]
        p_q = psum("p_q", [P, R * P])
        p_kv = psum("p_kv", [P, R * P])
        p_o = psum("p_o", [P, R * P])

        kv_done, q_done, new_done, cached_done = sem("kv_done"), sem("q_done"), sem("new_done"), sem("cached_done")
        prob_turned, pv_done, out_done = sem("prob_turned"), sem("pv_done"), sem("out_done")
        cache_turned, q_turned, k_turned = sem("cache_turned"), sem("q_turned"), sem("k_turned")
        exp_cached, exp_new, pt_hi, kv_copied, k_sq, q_sq = (sem(x) for x in (
            "exp_cached", "exp_new", "pt_hi", "kv_copied", "k_sq", "q_sq"))
        o_hi, cache_hi, q_hi, k_hi, table_in = (sem(x) for x in ("o_hi", "cache_hi", "q_hi", "k_hi", "table_in"))
        late_ok, new_max_ok, row_max_ok, bias_ok, pt_lo, den_ok, inv_ok = (sem(x) for x in (
            "late_ok", "new_max_ok", "row_max_ok", "bias_ok", "pt_lo", "den_ok", "inv_ok"))
        o_lo, q_parts, sums_ok, mean_ok, cache_lo, q_lo, k_lo, added = (sem(x) for x in (
            "o_lo", "q_parts", "sums_ok", "mean_ok", "cache_lo", "q_lo", "k_lo", "added"))
        x_hi, x_lo, v_hi, v_lo, w_hi, w_lo, normed = (sem(x) for x in (
            "x_hi", "x_lo", "v_hi", "v_lo", "w_hi", "w_lo", "normed"))
        k_parts, k_sum, rinv_ok, scales_ok, k_ready, q_ready, const_ok = (sem(x) for x in (
            "k_parts", "k_sum", "rinv_ok", "scales_ok", "k_ready", "q_ready", "const_ok"))
        pool_passed, dve_passed = sem("pool_passed"), sem("dve_passed")
        w_in = [sem("w_in0"), sem("w_in1")]
        k_in = [sem("k_in0"), sem("k_in1")]
        v_in = [sem("v_in0"), sem("v_in1")]

        def hold(engine, passed, semaphore, value):
            if isinstance(value, int):
                wait(engine, semaphore, value)
                return
            engine.wait_ge(semaphore, value)
            engine.sem_inc(passed, 1)

        def steps(engine, turn):
            turn(-1, 1, False, False, True)
            turn(0, 0, False, True, True)
            turn(1, 1, True, True, True)
            with engine.Fori(1, STEPS // 2 - 1) as i:
                turn(i * 2, 0, True, True, True)
                turn(i * 2 + 1, 1, True, True, True)
            turn(STEPS - 2, 0, True, True, True)
            turn(STEPS - 1, 1, True, True, False)
            turn(STEPS, 0, True, False, False)

        block = ctx.enter_context(nc.Block())

        @block.sync
        def _(sp):
            k_view = k_cache.rearrange("n s h d -> n s (h d)")
            v_view = v_cache.rearrange("n s h d -> n s (h d)")

            def load_pages(m, p):
                b, g = m % B, m // B
                for j in range(NPAGE):
                    page = sp.value_load(pages[0:1, bass.ds(b * NPAGE + j, 1)], min_val=0, max_val=PAGES - 1)
                    rows = slice(PAGE * (j % 4), PAGE * (j % 4 + 1))
                    if j == 0:
                        wait(sp, cache_turned, m - 1)
                    sp.dma_start(k_raw[p][rows, j // 4, :],
                                 k_view[bass.ds(page, 1), :, bass.ds(g * P, P)].rearrange("o s d -> (o s) d")
                                 ).then_inc(k_in[p], 16)
                    if j == 0:
                        wait(sp, v_lo, m - 1)
                    sp.dma_start(v_raw[p][rows, j // 4, :],
                                 v_view[bass.ds(page, 1), :, bass.ds(g * P, P)].rearrange("o s d -> (o s) d")
                                 ).then_inc(v_in[p], 16)

            def load_weights(m, p):
                wait(sp, w_lo, m - (LEAD + 1))
                sp.dma_start(wr[p][:, :], wall[bass.ds(m % (G * CHUNKS), 1), :, :].rearrange("o p n -> (o p) n")
                             ).then_inc(w_in[p], 16)

            def turn(n, p):
                load_pages(n + 2, p)
                load_weights(n + LEAD + 1, (p + LEAD + 1) % 2)

            load_weights(LEAD, LEAD % 2)
            load_pages(0, 0)
            load_pages(1, 1)
            turn(0, 0)
            with sp.Fori(0, (STEPS - 4) // 2) as i:
                turn(i * 2 + 1, 1)
                turn(i * 2 + 2, 0)
            load_pages(STEPS - 1, 1)
            for p in range(2):
                sp.wait_ge(k_in[p], 16 * NPAGE * STEPS // 2)
                sp.wait_ge(v_in[p], 16 * NPAGE * STEPS // 2)

        @block.gpsimd
        def _(pool):
            Gp = nc.gpsimd
            Gp.memset(halves[:, :], -0.5).then_inc(const_ok, 1)
            pool.wait_ge(const_ok, 1)

            def rounded(o, full):
                return Gp.tensor_scalar(o, full, 1.0, 1.0, ALU.mult, ALU.mult)

            def turn(n, p, ends, works, begins):
                q = 1 - p
                m = n + 1
                if begins:
                    cols = bass.ds((m % B) * P, P)
                    hold(pool, pool_passed, q_done, m)
                    Gp.tensor_copy(xH[:, :, :], xTs[:, :, cols]).then_inc(x_hi, 1)
                    hold(pool, pool_passed, x_hi, m + 1)
                    Gp.tensor_tensor(xL[:, :, :], xTs[:, :, cols], xH[:, :, :].bitcast(FP32), ALU.subtract
                                     ).then_inc(x_lo, 1)
                if works:
                    hold(pool, pool_passed, v_in[p], 16 * NPAGE * (n // 2 + 1))
                    if not isinstance(n, int) or n >= 2:
                        hold(pool, pool_passed, pv_done, (n - 1) * JT)
                    hold(pool, pool_passed, kv_copied, n + 1)
                    rounded(vH[p][:, 0:KT, :], v_raw[p][:, :, :]).then_inc(v_hi, 1)
                    rounded(vH[p][:, KT, :], kv[:, 1, :]).then_inc(v_hi, 1)
                    hold(pool, pool_passed, v_hi, (n + 1) * 2)
                    Gp.tensor_tensor(vL[p][:, KT, :], kv[:, 1, :], vH[p][:, KT, :].bitcast(FP32), ALU.subtract)
                    Gp.tensor_tensor(vL[p][:, 0:KT, :], v_raw[p][:, :, :], vH[p][:, 0:KT, :].bitcast(FP32),
                                     ALU.subtract).then_inc(v_lo, 1)
                    if not isinstance(n, int) or n < STEPS - 2:
                        at = bass.ds(((n + LEAD) % (2 * CHUNKS)) * CHUNK, CHUNK)
                        w = (p + LEAD) % 2
                        hold(pool, pool_passed, w_in[w], w_count(n, p))
                        hold(pool, pool_passed, q_done, n + 1)
                        if not isinstance(n, int) or n >= 2:
                            hold(pool, pool_passed, out_done, n - 1)
                        Gp.tensor_copy(wH[:, at], wr[w][:, :]).then_inc(w_hi, 1)
                        hold(pool, pool_passed, w_hi, n + 1)
                        Gp.tensor_tensor(wL[:, at], wr[w][:, :], wH[:, at].bitcast(FP32), ALU.subtract
                                         ).then_inc(w_lo, 1)
                    hold(pool, pool_passed, inv_ok, n + 1)
                    for h in range(R):
                        last = Gp.tensor_scalar(prob[p][:, h, :], prob[p][:, h, :], den_inv[p][:, h:h + 1], 1.0,
                                                ALU.mult, ALU.mult)
                    last.then_inc(normed, 1)
                if begins:
                    row = bass.ds(m % B, 1)
                    hold(pool, pool_passed, kv_copied, m + 1)
                    a = kA[:, row, :].rearrange("p o d -> p (o d)")
                    b_ = kB[:, row, :].rearrange("p o d -> p (o d)")
                    Gp.tensor_tensor(k_u[:, :], kv[:, 0, :], a, ALU.mult).then_inc(k_parts, 1)
                    Gp.tensor_tensor(k_w[:, 0:64], kv[:, 0, 64:P], b_[:, 0:64], ALU.mult).then_inc(k_parts, 1)
                    Gp.tensor_tensor(k_w[:, 64:P], kv[:, 0, 0:64], b_[:, 64:P], ALU.mult).then_inc(k_parts, 1)
                    hold(pool, pool_passed, k_parts, (m + 1) * 3)
                    Gp.tensor_tensor(k_s[:, :], k_u[:, :], k_w[:, :], ALU.add).then_inc(k_sum, 1)
                    hold(pool, pool_passed, q_parts, m + 1)
                    hold(pool, pool_passed, q_turned, m)
                    Gp.tensor_tensor(q_rot[:, :, :], q_u[:, :, :], q_w[:, :, :], ALU.add).then_inc(q_ready, 1)
                    hold(pool, pool_passed, mean_ok, m + 1)
                    Gp.tensor_tensor(rinv[:, :], mean[:, :], halves[:, :], ALU.pow).then_inc(rinv_ok, 1)
                    hold(pool, pool_passed, rinv_ok, m + 1)
                    hold(pool, pool_passed, k_sum, m + 1)
                    hold(pool, pool_passed, k_turned, m)
                    Gp.tensor_scalar(k_rot[:, :], k_s[:, :], rinv[:, R:R + 1], 1.0, ALU.mult, ALU.mult).then_inc(k_ready, 1)
                    Gp.tensor_scalar(pos_scale[q][:, :], rinv[:, 0:R], SCALE, 1.0, ALU.mult, ALU.mult)
                    Gp.tensor_scalar(neg_scale[q][:, :], rinv[:, 0:R], -SCALE, 1.0, ALU.mult, ALU.mult).then_inc(scales_ok, 1)

            def w_count(n, p):
                return 16 * (n // 2 + 1)

            steps(pool, turn)

        @block.scalar
        def _(act):
            A = nc.scalar
            A.activation(table_out[:, :], ident[:, 0:1], ACT.Exp).then_inc(table_in, 1)

            def turn(n, p, ends, works, begins):
                q = 1 - p
                m = n + 1

                def prob_part(j):
                    act.wait_ge(prob_turned, (n - 1) * JT + j + 1)
                    wait(act, pv_done, (n - 1) * JT + max(j - 1, 0))
                    A.copy(ptH[j % 2][:, :], turned[j % 2][:, :]).then_inc(pt_hi, 1)

                for h in range(R):
                    if works:
                        act.wait_ge(bias_ok, n * R + h + 1)
                        if h == 0:
                            wait(act, prob_turned, (n - 1) * JT)
                            wait(act, den_ok, n)
                        A.activation(prob[p][:, h, 0:CACHE], s_cached[h % 2][:, :], ACT.Exp,
                                     bias=bias[p][:, h:h + 1], scale=pos_scale[p][:, h:h + 1],
                                     accum_out=den[:, h, 0:1]).then_inc(exp_cached, 1)
                        A.activation(prob[p][:, h, CACHE:KEYS], s_new[:, h * P:(h + 1) * P], ACT.Exp,
                                     bias=bias[p][:, h:h + 1], scale=pos_scale[p][:, h:h + 1],
                                     accum_out=den[:, h, 1:2]).then_inc(exp_new, 1)
                    if ends:
                        prob_part(h)
                if ends:
                    prob_part(R)
                if begins:
                    act.wait_ge(kv_done, m + 1)
                    wait(act, v_lo, m)
                    wait(act, k_sum, m)
                    A.copy(kv[:, :, :], p_kv[:, 0:2 * P].rearrange("p (a d) -> p a d", a=2)).then_inc(kv_copied, 1)
                    wait(act, sums_ok, m)
                    act.wait_ge(kv_copied, m + 1)
                    A.activation(squares[:, R, :], kv[:, 0, :], ACT.Square).then_inc(k_sq, 1)
                if ends:
                    act.wait_ge(pv_done, n * JT)
                    wait(act, out_done, n - 1)
                    A.copy(oH[:, :], p_o[:, :]).then_inc(o_hi, 1)
                if begins:
                    act.wait_ge(q_parts, m + 1)
                    A.activation(squares[:, 0:R, :], p_q[:, :].rearrange("p (h d) -> p h d", h=R), ACT.Square
                                 ).then_inc(q_sq, 1)
                    act.wait_ge(cache_turned, m + 1)
                    wait(act, cached_done, m * R)
                    A.copy(kH[:, 0:CACHE], turned[1][:, :]).then_inc(cache_hi, 1)
                    act.wait_ge(q_turned, m + 1)
                    A.copy(qH[:, :], turned[0][:, :]).then_inc(q_hi, 1)
                    act.wait_ge(k_turned, m + 1)
                    A.copy(kH[:, CACHE:KEYS], p_kv[:, 2 * P:3 * P]).then_inc(k_hi, 1)

            steps(act, turn)

        @block.vector
        def _(dve):
            V = nc.vector

            def rest(o, full, high):
                return V.tensor_tensor(o, full, high.bitcast(FP32), ALU.subtract)

            def turn(n, p, ends, works, begins):
                q = 1 - p
                m = n + 1

                def prob_part(j):
                    dve.wait_ge(pt_hi, (n - 1) * JT + j + 1)
                    rest(ptL[j % 2][:, :], turned[j % 2][:, :], ptH[j % 2][:, :]).then_inc(pt_lo, 1)

                if works:
                    wait(dve, row_max_ok, n * R)
                    V.tensor_scalar(late[:, :], key_no[:, :], seqf[:, bass.ds(n % B, 1)], NEG, ALU.is_ge, ALU.mult
                                    ).then_inc(late_ok, 1)
                    dve.wait_ge(new_done, n + 1)
                    V.tensor_reduce(new_max[:, :], s_new[:, :].rearrange("p (h k) -> p h k", h=R), AX.X, ALU.max
                                    ).then_inc(new_max_ok, 1)
                    hold(dve, dve_passed, late_ok, n + 1)
                    hold(dve, dve_passed, new_max_ok, n + 1)
                    hold(dve, dve_passed, scales_ok, n + 1)
                for h in range(R):
                    if works:
                        hold(dve, dve_passed, cached_done, n * R + h + 1)
                        V.tensor_tensor_reduce(out=s_cached[h % 2][:, :], in0=s_cached[h % 2][:, :], in1=late[:, :],
                                               scale=1.0, scalar=new_max[:, h:h + 1], op0=ALU.add, op1=ALU.max,
                                               accum_out=row_max[:, h:h + 1]).then_inc(row_max_ok, 1)
                        dve.wait_ge(row_max_ok, n * R + h + 1)
                        V.tensor_tensor(bias[p][:, h:h + 1], row_max[:, h:h + 1], neg_scale[p][:, h:h + 1], ALU.mult
                                        ).then_inc(bias_ok, 1)
                    if ends:
                        prob_part(h)
                if works:
                    dve.wait_ge(exp_new, (n + 1) * R)
                    V.tensor_tensor(den_sum[:, :], den[:, :, 0], den[:, :, 1], ALU.add).then_inc(den_ok, 1)
                    dve.wait_ge(den_ok, n + 1)
                    V.reciprocal(den_inv[p][:, :], den_sum[:, :]).then_inc(inv_ok, 1)
                if ends:
                    prob_part(R)
                    dve.wait_ge(o_hi, n)
                    rest(oL[:, :], p_o[:, :], oH[:, :]).then_inc(o_lo, 1)
                if begins:
                    row = bass.ds(m % B, 1)
                    heads = p_q[:, :].rearrange("p (h d) -> p h d", h=R)
                    dve.wait_ge(q_done, m + 1)
                    wait(dve, q_ready, m)
                    V.tensor_tensor(q_w[:, :, 0:64], heads[:, :, 64:P], qB[:, row, 0:64].broadcast_to([P, R, 64]),
                                    ALU.mult)
                    V.tensor_tensor(q_w[:, :, 64:P], heads[:, :, 0:64], qB[:, row, 64:P].broadcast_to([P, R, 64]),
                                    ALU.mult)
                    V.tensor_tensor(q_u[:, :, :], heads, qA[:, row, :].broadcast_to([P, R, P]), ALU.mult
                                    ).then_inc(q_parts, 1)
                    dve.wait_ge(k_sq, m + 1)
                    dve.wait_ge(q_sq, m + 1)
                    V.tensor_reduce(sums[:, :], squares[:, :, :], AX.X, ALU.add).then_inc(sums_ok, 1)
                    dve.wait_ge(sums_ok, m + 1)
                    wait(dve, rinv_ok, m)
                    V.tensor_scalar(mean[:, :], sums[:, :], 1.0 / P, EPS, ALU.mult, ALU.add).then_inc(mean_ok, 1)
                    dve.wait_ge(cache_hi, m + 1)
                    rest(kL[:, 0:CACHE], turned[1][:, :], kH[:, 0:CACHE]).then_inc(cache_lo, 1)
                    dve.wait_ge(q_hi, m + 1)
                    rest(qL[:, :], turned[0][:, :], qH[:, :]).then_inc(q_lo, 1)
                    dve.wait_ge(k_hi, m + 1)
                    rest(kL[:, CACHE:KEYS], p_kv[:, 2 * P:3 * P], kH[:, CACHE:KEYS]).then_inc(k_lo, 1)
                if ends:
                    a = acc[:, bass.ds((n - 1) % B, 1), :].rearrange("p o d -> p (o d)")
                    dve.wait_ge(out_done, n)
                    wait(dve, added, n - 1)
                    V.tensor_tensor(a, p_o[:, :], a, ALU.add).then_inc(added, 1)

            steps(dve, turn)

        @block.tensor
        def _(pe):
            def mm(o, l, r, start, stop):
                return matmul(nc, o, l, r, start, stop)

            def turn(n, p, ends, works, begins):
                q = 1 - p
                m = n + 1

                def new_scores():
                    pe.wait_ge(q_lo, n + 1)
                    pe.wait_ge(cache_lo, n + 1)
                    pe.wait_ge(k_lo, n + 1)
                    wait(pe, exp_new, n * R)
                    for h in range(R):
                        s = slice(h * P, (h + 1) * P)
                        last = passes(nc, s_new[:, s], [(qH[:, s], qL[:, s], kH[:, CACHE:KEYS], kL[:, CACHE:KEYS])])
                    last.then_inc(new_done, 1)

                def cached_scores(h):
                    if not (isinstance(n, int) and n == 0 and h < 2):
                        pe.wait_ge(exp_cached, n * R + h - 1)
                    s = slice(h * P, (h + 1) * P)
                    passes(nc, s_cached[h % 2][:, :], [(qH[:, s], qL[:, s], kH[:, 0:CACHE], kL[:, 0:CACHE])]
                           ).then_inc(cached_done, 1)

                def turn_probs(j):
                    if j == 0:
                        pe.wait_ge(normed, n)
                    if j < 2:
                        wait(pe, q_lo, n if not works else n + 1)
                        wait(pe, cache_lo, n if not works else n + 1)
                    else:
                        pe.wait_ge(pt_lo, (n - 1) * JT + j - 1)
                    for h in range(R):
                        last = nc.tensor.transpose(turned[j % 2][:, h * P:(h + 1) * P],
                                                   prob[q][:, h, j * P:(j + 1) * P], ident[:, :])
                    last.then_inc(prob_turned, 1)

                def times_values(j):
                    pe.wait_ge(pt_lo, (n - 1) * JT + j + 1)
                    if j == 0:
                        pe.wait_ge(v_lo, n)
                        wait(pe, added, n - 1)
                    passes(nc, p_o[:, :], [(vH[q][:, j, :], vL[q][:, j, :], ptH[j % 2][:, :], ptL[j % 2][:, :])],
                           first=j == 0, last=j == JT - 1).then_inc(pv_done, 1)

                def project_kv():
                    pe.wait_ge(x_lo, m + 1)
                    wait(pe, w_lo, n)
                    wait(pe, k_lo, m)
                    base = ((m // B) % 2) * REGION
                    for i in range(C):
                        at = bass.ds(base + i * QKV + R * P, 2 * P)
                        last = passes(nc, p_kv[:, 0:2 * P], [(xH[:, i, :], xL[:, i, :], wH[:, at], wL[:, at])],
                                      first=i == 0, last=i == C - 1)
                    last.then_inc(kv_done, 1)

                def project_q(half):
                    base = ((m // B) % 2) * REGION
                    if half == 0:
                        wait(pe, q_parts, m)
                        wait(pe, q_sq, m)
                    for i in (0, 1) if half == 0 else (2, 3):
                        at = bass.ds(base + i * QKV, R * P)
                        last = passes(nc, p_q[:, :], [(xH[:, i, :], xL[:, i, :], wH[:, at], wL[:, at])],
                                      first=i == 0, last=i == C - 1)
                    if half == 1:
                        last.then_inc(q_done, 1)

                def project_out(heads):
                    if heads[0] == 0:
                        pe.wait_ge(o_lo, n)
                    base = (((n - 1) // B) % 2) * REGION + C * QKV
                    for h in heads:
                        s = slice(h * P, (h + 1) * P)
                        at = bass.ds(base + h * D, D)
                        last = passes(nc, p_o[:, :], [(oH[:, s], oL[:, s], wH[:, at], wL[:, at])],
                                      first=h == 0, last=h == R - 1)
                    if heads[-1] == R - 1:
                        last.then_inc(out_done, 1)

                def turn_cached_keys():
                    pe.wait_ge(k_in[q], 16 * NPAGE * (m // 2 + 1))
                    if ends:
                        pe.wait_ge(pt_lo, (n - 1) * JT + 4)
                    elif works:
                        pe.wait_ge(cache_lo, n + 1)
                    for t in range(KT):
                        last = nc.tensor.transpose(turned[1][:, t * P:(t + 1) * P], k_raw[q][:, t, :], ident[:, :])
                    last.then_inc(cache_turned, 1)

                def turn_queries():
                    pe.wait_ge(q_ready, m + 1)
                    if ends:
                        pe.wait_ge(pt_lo, n * JT)
                    elif works:
                        pe.wait_ge(q_lo, n + 1)
                    for h in range(R):
                        last = nc.tensor.transpose(turned[0][:, h * P:(h + 1) * P], q_rot[:, h, :], ident[:, :])
                    last.then_inc(q_turned, 1)

                def turn_new_keys():
                    pe.wait_ge(k_ready, m + 1)
                    pe.wait_ge(kv_copied, m + 1)
                    nc.tensor.transpose(p_kv[:, 2 * P:3 * P], k_rot[:, :], ident[:, :]).then_inc(k_turned, 1)

                if works:
                    new_scores()
                    cached_scores(0)
                if ends:
                    turn_probs(0)
                if works:
                    cached_scores(1)
                if ends:
                    turn_probs(1)
                    times_values(0)
                if works:
                    cached_scores(2)
                if ends:
                    turn_probs(2)
                    times_values(1)
                if works:
                    cached_scores(3)
                if ends:
                    turn_probs(3)
                    times_values(2)
                    turn_probs(4)
                if begins:
                    project_kv()
                if ends:
                    times_values(3)
                if begins:
                    project_q(0)
                if ends:
                    times_values(4)
                if begins:
                    project_q(1)
                if ends:
                    project_out((0, 1, 2))
                if begins:
                    turn_cached_keys()
                if ends:
                    project_out((3,))
                if begins:
                    turn_queries()
                    turn_new_keys()

            steps(pe, turn)


def last_layer(nc, acc, ident, cfs, mask, w3T, bias3, out):
    ctx = ExitStack()
    with ctx:
        def sbuf(name, shape, dt=FP32):
            return ctx.enter_context(nc.sbuf_tensor(name, shape, dt))

        def psum(name, shape):
            return ctx.enter_context(nc.psum_tensor(name, shape, FP32))

        def sem(name):
            return ctx.enter_context(nc.semaphore(name))

        w3 = sbuf("w3", [P, C, D])
        bi3 = sbuf("bi3", [P, D])
        mk = [sbuf(f"mk{i}", [P, C, D], I32) for i in range(2)]
        sg = sbuf("sg", [P, C, D])
        wc = sbuf("wc", [P, C, D])
        wcH = [sbuf(f"wcH{i}", [P, C, D], F32R) for i in range(2)]
        wcL = [sbuf(f"wcL{i}", [P, C, D], F32R) for i in range(2)]
        row = [sbuf(f"row{i}", [P, D]) for i in range(2)]
        tH = [sbuf(f"tH{i}", [P, C * P], F32R) for i in range(2)]
        tL = [sbuf(f"tL{i}", [P, C * P], F32R) for i in range(2)]
        rb = [sbuf(f"rb{i}", [P, D]) for i in range(2)]
        yo = [sbuf(f"yo{i}", [P, D]) for i in range(2)]
        pT = [psum(f"pT{i}", [P, D]) for i in range(2)]
        pO = [psum(f"pO{i}", [P, D]) for i in range(2)]
        cin, m_in = sem("cin"), [sem("m_in0"), sem("m_in1")]
        row_ok, sg_ok, wc_ok, wc_hi, wc_lo = (sem(x) for x in ("row_ok", "sg_ok", "wc_ok", "wc_hi", "wc_lo"))
        t_done, t_hi, t_lo, rb_ok, y_done, y_out = (sem(x) for x in ("t_done3", "t_hi", "t_lo", "rb_ok", "y_done3", "y_out3"))
        stored = [sem("stored0"), sem("stored1")]
        block = ctx.enter_context(nc.Block())

        @block.sync
        def _(sp):
            sp.dma_start(w3[:, :, :], w3T).then_inc(cin, 16)
            sp.dma_start(bi3[:, :], bias3.rearrange("(o n) -> o n", o=1).broadcast_to([P, D])).then_inc(cin, 16)

            def load(b):
                wait(sp, sg_ok, b - 1)
                sp.dma_start(mk[b % 2][:, :, :], mask[b].rearrange("(c p) o -> p c o", p=P)).then_inc(m_in[b % 2], 16)

            load(0)
            load(1)
            for b in range(B):
                if b + 2 < B:
                    load(b + 2)
                sp.wait_ge(y_out, b + 1)
                sp.dma_start(out[b], yo[b % 2][:, :]).then_inc(stored[b % 2], 16)
            for p in range(2):
                sp.wait_ge(stored[p], 16 * B // 2)

        @block.scalar
        def _(act):
            A = nc.scalar

            def copy_row(b):
                wait(act, t_done, b - 1)
                A.copy(row[b % 2][:, :], acc[:, b, :]).then_inc(row_ok, 1)

            def signs(b):
                act.wait_ge(m_in[b % 2], 16 * (b // 2 + 1))
                wait(act, wc_ok, b)
                A.activation(sg[:, :, :], mk[b % 2][:, :, :], ACT.Identity, bias=cfs[:, 2, b:b + 1],
                             scale=cfs[:, 1, b:b + 1]).then_inc(sg_ok, 1)

            copy_row(0)
            signs(0)
            for b in range(B):
                act.wait_ge(wc_ok, b + 1)
                wait(act, y_done, b - 1)
                A.copy(wcH[b % 2][:, :, :], wc[:, :, :]).then_inc(wc_hi, 1)
                act.wait_ge(t_done, b + 1)
                A.copy(tH[b % 2][:, :], pT[b % 2][:, :]).then_inc(t_hi, 1)
                if b + 1 < B:
                    copy_row(b + 1)
                    signs(b + 1)

        @block.gpsimd
        def _(pool):
            pool.wait_ge(cin, 32)
            for b in range(B):
                wait(pool, y_out, b - 1)
                nc.gpsimd.tensor_tensor(rb[b % 2][:, :], acc[:, b, :], bi3[:, :], ALU.add).then_inc(rb_ok, 1)
                pool.wait_ge(wc_hi, b + 1)
                nc.gpsimd.tensor_tensor(wcL[b % 2][:, 0, :], wc[:, 0, :], wcH[b % 2][:, 0, :].bitcast(FP32),
                                        ALU.subtract).then_inc(wc_lo, 1)

        @block.vector
        def _(dve):
            V = nc.vector

            def finish(b):
                dve.wait_ge(y_done, b + 1)
                dve.wait_ge(rb_ok, b + 1)
                wait(dve, stored[b % 2], 16 * (b // 2))
                nc.vector.tensor_tensor(yo[b % 2][:, :], pO[b % 2][:, :], rb[b % 2][:, :], ALU.add).then_inc(y_out, 1)

            dve.wait_ge(cin, 32)
            for b in range(B):
                dve.wait_ge(sg_ok, b + 1)
                wait(dve, wc_lo, 2 * b)
                V.tensor_tensor(wc[:, :, :], sg[:, :, :], w3[:, :, :], ALU.add).then_inc(wc_ok, 1)
                dve.wait_ge(wc_hi, b + 1)
                V.tensor_tensor(wcL[b % 2][:, 1:C, :], wc[:, 1:C, :], wcH[b % 2][:, 1:C, :].bitcast(FP32),
                                ALU.subtract).then_inc(wc_lo, 1)
                dve.wait_ge(t_hi, b + 1)
                V.tensor_tensor(tL[b % 2][:, :], pT[b % 2][:, :], tH[b % 2][:, :].bitcast(FP32), ALU.subtract
                                ).then_inc(t_lo, 1)
                if b >= 1:
                    finish(b - 1)
            finish(B - 1)

        @block.tensor
        def _(pe):
            def turn(b):
                pe.wait_ge(row_ok, b + 1)
                wait(pe, t_lo, b - 1)
                for i in range(C):
                    last = nc.tensor.transpose(pT[b % 2][:, i * P:(i + 1) * P], row[b % 2][:, i * P:(i + 1) * P],
                                               ident[:, :])
                last.then_inc(t_done, 1)

            turn(0)
            for b in range(B):
                if b + 1 < B:
                    turn(b + 1)
                pe.wait_ge(t_lo, b + 1)
                pe.wait_ge(wc_lo, 2 * (b + 1))
                wait(pe, y_out, b - 1)
                passes(nc, pO[b % 2][:, :], [(tH[b % 2][:, i * P:(i + 1) * P], tL[b % 2][:, i * P:(i + 1) * P],
                                              wcH[b % 2][:, i, :], wcL[b % 2][:, i, :]) for i in range(C)]
                       ).then_inc(y_done, 1)


def program(nc, x, xT, seqlens, adapter, table, coeff, mask, codebook, w0, scale_log, loraA, loraBT,
            w1T, bias1, a1T, b1, scaling, wall, wqn, wkn, k_cache, v_cache, w3T, bias3, invf, out):
    outer = ExitStack()
    names = [0]

    def sbuf(ctx, name, shape, dt=FP32):
        return ctx.enter_context(nc.sbuf_tensor(name, shape, dt))

    def psum(ctx, name, shape, dt=FP32):
        return ctx.enter_context(nc.psum_tensor(name, shape, dt))

    def semaphore(ctx, name):
        return ctx.enter_context(nc.semaphore(name))

    def counted(ctx, *all_names):
        return [semaphore(ctx, n) for n in all_names]

    class Chain:

        def __init__(self, engine, sem):
            self.engine, self.sem, self.n = engine, sem, 0

        def __call__(self, instruction):
            self.n += 1
            instruction.then_inc(self.sem, 1)
            self.engine.wait_ge(self.sem, self.n)

    def mm(o, l, r, start, stop):
        return nc.tensor.matmul(o, l, r, start=start, stop=stop)

    def product(o, terms):
        n = len(terms)
        for i, (lh, ll, rh, rl) in enumerate(terms):
            mm(o, lh, rh, i == 0, False)
            mm(o, ll, rh, False, False)
            last = mm(o, lh, rl, False, i == n - 1)
        return last

    with outer:
        acc = sbuf(outer, "acc", [P, B, D])
        xTs = sbuf(outer, "xTs", [P, C, B * P])
        qA = sbuf(outer, "qA", [P, B, P])
        qB = sbuf(outer, "qB", [P, B, P])
        kA = sbuf(outer, "kA", [P, B, P])
        kB = sbuf(outer, "kB", [P, B, P])
        ident = sbuf(outer, "ident", [P, P])
        key_no = sbuf(outer, "key_no", [P, CACHE])
        seqf = sbuf(outer, "seqf", [P, B])
        pages = sbuf(outer, "pages", [1, B * NPAGE], I32)
        cfs = sbuf(outer, "cfs", [P, 3, B])
        weights = ExitStack()
        wH = sbuf(weights, "wH", [P, 2 * REGION], F32R)
        wL = sbuf(weights, "wL", [P, 2 * REGION], F32R)
        wr = [sbuf(weights, f"wr{i}", [P, CHUNK]) for i in range(2)]

        prep = ExitStack()
        with prep:
            c1 = prep
            w0TH = sbuf(c1, "w0TH", [P, C, D], F32R)
            w0TL = sbuf(c1, "w0TL", [P, C, D], F32R)
            sel = sbuf(c1, "sel", [P, B])
            setup = ExitStack()
            with setup:
                c = setup
                W = sbuf(c, "W", [P, C, D])
                DL = sbuf(c, "DL", [P, C, D])
                NR = sbuf(c, "NR", [P, C, D])
                QA = sbuf(c, "QA", [P, C, D])
                QB = sbuf(c, "QB", [P, C, D])
                GT = sbuf(c, "GT", [P, C, D], I32)
                lA = sbuf(c, "lA", [64, D])
                lB = sbuf(c, "lB", [64, D])
                sl = sbuf(c, "sl", [P, C, C])
                ex = sbuf(c, "ex", [P, 6, C * C])
                exi = sbuf(c, "exi", [P, C * C], I32)
                cb = sbuf(c, "cb", [P, 8])
                cbt = sbuf(c, "cbt", [P, 6, 8])
                seqi = sbuf(c, "seqi", [P, B], I32)
                toki = sbuf(c, "toki", [P, 1], I32)
                rowi = sbuf(c, "rowi", [P, 2], I32)
                rowf = sbuf(c, "rowf", [P, 2])
                adi = sbuf(c, "adi", [P, B], I32)
                adf = sbuf(c, "adf", [P, 3, B])
                scl = sbuf(c, "scl", [P, 1])
                pos = sbuf(c, "pos", [P, B])
                tokf = sbuf(c, "tokf", [P, 1])
                keyi = sbuf(c, "keyi", [P, CACHE], I32)
                pgf = sbuf(c, "pgf", [1, 2, B * NPAGE])
                invs = sbuf(c, "invs", [P, 64])
                nwq = sbuf(c, "nwq", [P, P])
                nwk = sbuf(c, "nwk", [P, P])
                nn = sbuf(c, "nn", [P, 2, 64])
                fr = sbuf(c, "fr", [P, B, 64])
                kk = sbuf(c, "kk", [P, B, 64])
                ra = sbuf(c, "ra", [P, B, 64])
                sn = sbuf(c, "sn", [P, B, 64])
                cs = sbuf(c, "cs", [P, B, 64])
                pD = [psum(c, f"pD{i}", [P, D]) for i in range(4)]
                (in_w, in_lora, in_x, in_small, in_idx, iota_ok, ident_ok, delta_ok, dv, pl, ac, sin_ready, cos_ready, sc_ok,
                 tabs, seq_ok, w_tr, w_hi, w_lo, w_eff, trig_in) = counted(
                    c, "in_w", "in_lora", "in_x", "in_small", "in_idx", "iota_ok", "ident_ok", "delta_ok", "dv", "pl", "ac",
                    "sin_ready", "cos_ready", "sc_ok", "tabs", "seq_ok", "w_tr", "w_hi", "w_lo", "w_eff", "trig_in")
                block = c.enter_context(nc.Block())

                def row(ap, n):
                    return ap.rearrange("(o n) -> o n", o=1).broadcast_to([P, n])

                @block.sync
                def _(sp):
                    sp.dma_start(lA[:, :], loraA).then_inc(in_lora, 16)
                    sp.dma_start(lB[:, :], loraBT).then_inc(in_lora, 16)
                    sp.dma_start(W[:, :, :], w0.rearrange("(t p) i -> p t i", p=P)).then_inc(in_w, 16)
                    sp.dma_start(sl[:, :, :], scale_log.rearrange("(t p) g o -> p t (g o)", p=P)).then_inc(in_w, 16)
                    sp.dma_start(cb[:, :], row(codebook, 8)).then_inc(in_w, 16)
                    sp.dma_start(seqi[:, :], row(seqlens, B)).then_inc(in_idx, 16)
                    sp.dma_start(adi[:, :], row(adapter, B)).then_inc(in_idx, 16)
                    sp.dma_start(invs[:, :], row(invf, 64)).then_inc(in_idx, 16)
                    sp.dma_start(nwq[:, :], row(wqn, P)).then_inc(in_idx, 16)
                    sp.dma_start(nwk[:, :], row(wkn, P)).then_inc(in_idx, 16)
                    sp.dma_start(cfs[:, 0, :], row(coeff, B)).then_inc(in_idx, 16)
                    sp.dma_start(pages[:, :], table.rearrange("(o b) n -> o (b n)", o=1)).then_inc(in_idx, 16)
                    for a in range(ADAPTERS):
                        sp.dma_start(scl[a * RANK:(a + 1) * RANK, :],
                                     scaling[a:a + 1].rearrange("(o n) -> o n", o=1).broadcast_to([RANK, 1])
                                     ).then_inc(in_idx, 16)
                    sp.dma_start(acc[:, :, :], x.rearrange("b s d -> s b d")).then_inc(in_x, 16)
                    sp.dma_start(xTs[:, :, :], xT).then_inc(in_x, 16)
                    sp.wait_ge(in_x, 32)

                IDX = 16 * (7 + ADAPTERS)

                @block.gpsimd
                def _(pool):
                    do = Chain(pool, pl)
                    do(nc.gpsimd.memset(ident[:, :], 0.0))
                    nc.gpsimd.affine_select(out=ident[:, :], in_=ident[:, :], compare_op=ALU.not_equal, fill=1.0,
                                            base=0, pattern=[[-1, P]], channel_multiplier=1).then_inc(ident_ok, 1)
                    nc.gpsimd.iota(toki[:, :], pattern=[[0, 1]], base=0, channel_multiplier=1).then_inc(iota_ok, 1)
                    nc.gpsimd.iota(keyi[:, :], pattern=[[1, CACHE]], base=0, channel_multiplier=0).then_inc(iota_ok, 1)

                @block.scalar
                def _(act):
                    act.wait_ge(trig_in, 1)
                    nc.scalar.activation(sn[:, :, :], ra[:, :, :], ACT.Sin).then_inc(sin_ready, 1)
                    act.wait_ge(trig_in, 2)
                    nc.scalar.activation(cs[:, :, :], ra[:, :, :], ACT.Sin).then_inc(cos_ready, 1)
                    for i in range(C):
                        act.wait_ge(w_tr, i + 1)
                        nc.scalar.copy(w0TH[:, i, :], pD[i][:, :]).then_inc(w_hi, 1)

                @block.tensor
                def _(pe):
                    pe.wait_ge(in_lora, 32)
                    for i in range(C):
                        mm(pD[i][:, :], lB[:, i * P:(i + 1) * P], lA[:, :], True, True).then_inc(delta_ok, 1)
                    pe.wait_ge(w_eff, 1)
                    pe.wait_ge(ident_ok, 1)
                    for i in range(C):
                        for t in range(C):
                            last = nc.tensor.transpose(pD[i][:, t * P:(t + 1) * P], W[:, t, i * P:(i + 1) * P],
                                                       ident[:, :])
                        last.then_inc(w_tr, 1)

                @block.vector
                def _(dve):
                    do = Chain(dve, dv)
                    V = nc.vector
                    dve.wait_ge(in_idx, IDX)
                    dve.wait_ge(iota_ok, 2)
                    do(V.tensor_copy(seqf[:, :], seqi[:, :]))
                    do(V.tensor_copy(tokf[:, :], toki[:, :]))
                    do(V.tensor_copy(key_no[:, :], keyi[:, :]))
                    do(V.tensor_scalar(pos[:, :], seqf[:, :], tokf[:, 0:1], None, ALU.add))
                    do(V.tensor_scalar(cfs[:, 1, :], cfs[:, 0, :], 2.0, None, ALU.mult))
                    do(V.tensor_scalar(cfs[:, 2, :], cfs[:, 0, :], -1.0, None, ALU.mult))
                    do(V.tensor_scalar(pgf[:, 0, :], pages[:, :], 0.0, float(PAGES), ALU.is_lt, ALU.mult))
                    do(V.tensor_tensor(pgf[:, 1, :], pgf[:, 0, :], pages[:, :], ALU.add))
                    do(V.tensor_scalar(pages[:, :], pgf[:, 1, :], 0.0, float(PAGES - 1), ALU.max, ALU.min))
                    do(V.tensor_scalar(rowi[:, 0:1], toki[:, :], 4, None, ALU.arith_shift_right))
                    do(V.tensor_copy(rowf[:, 0:1], rowi[:, 0:1]))
                    do(V.tensor_scalar(adf[:, 0, :], adi[:, :], 0.0, float(ADAPTERS), ALU.is_lt, ALU.mult))
                    do(V.tensor_tensor(adf[:, 1, :], adf[:, 0, :], adi[:, :], ALU.add))
                    do(V.tensor_scalar(adf[:, 2, :], adf[:, 1, :], 0.0, float(ADAPTERS - 1), ALU.max, ALU.min))
                    do(V.tensor_scalar(sel[:, :], adf[:, 2, :], rowf[:, 0:1], scl[:, 0:1], ALU.is_equal, ALU.mult))
                    do(V.tensor_tensor(fr[:, :, :], invs[:, :].rearrange("p (o f) -> p o f", o=1).broadcast_to([P, B, 64]),
                                       pos[:, :].rearrange("p (b o) -> p b o", o=1).broadcast_to([P, B, 64]), ALU.mult))
                    for turn, shift in ((0.0, 0.0), (0.25, float(np.float32(np.pi / 2)))):
                        do(V.tensor_scalar(kk[:, :, :], fr[:, :, :], float(1.0 / TWO_PI), turn, ALU.mult, ALU.add))
                        do(V.tensor_scalar(kk[:, :, :], kk[:, :, :], MAGIC, None, ALU.add))
                        do(V.tensor_scalar(kk[:, :, :], kk[:, :, :], MAGIC, None, ALU.subtract))
                        if turn:
                            dve.wait_ge(sin_ready, 1)
                        do(V.scalar_tensor_tensor(ra[:, :, :], kk[:, :, :], -PI_A, fr[:, :, :], ALU.mult, ALU.add))
                        do(V.scalar_tensor_tensor(ra[:, :, :], kk[:, :, :], -PI_B, ra[:, :, :], ALU.mult, ALU.add))
                        do(V.scalar_tensor_tensor(ra[:, :, :], kk[:, :, :], -PI_C, ra[:, :, :], ALU.mult, ALU.add))
                        if turn:
                            do(V.tensor_scalar(ra[:, :, :], ra[:, :, :], shift, None, ALU.add))
                        V.tensor_scalar(ra[:, :, :], ra[:, :, :], BELOW_PI, -BELOW_PI, ALU.min, ALU.max
                                        ).then_inc(trig_in, 1)
                    dve.wait_ge(in_w, 48)
                    do(V.tensor_reduce(cbt[:, 0, 0:1], cb[:, :], AX.X, ALU.max, apply_absolute_value=True))
                    do(V.tensor_scalar(cbt[:, 0, 0:1], cbt[:, 0, 0:1], 1e-8, None, ALU.max))
                    do(V.reciprocal(cbt[:, 0, 1:2], cbt[:, 0, 0:1]))
                    do(V.tensor_scalar(cbt[:, 1, :], cb[:, :], cbt[:, 0, 1:2], None, ALU.mult))
                    do(V.tensor_tensor(cbt[:, 2, 0:7], cbt[:, 1, 0:7], cbt[:, 1, 1:8], ALU.add))
                    do(V.tensor_scalar(cbt[:, 2, 0:7], cbt[:, 2, 0:7], 0.5, None, ALU.mult))
                    do(V.tensor_tensor(cbt[:, 3, 0:7], cbt[:, 1, 1:8], cbt[:, 1, 0:7], ALU.subtract))
                    s_in = sl[:, :, :].rearrange("p t g -> p (t g)")
                    S, K, F, Y, Z, IV = (ex[:, i, :] for i in range(6))
                    do(V.tensor_scalar(S, s_in, 88.0, -87.0, ALU.min, ALU.max))
                    do(V.tensor_scalar(K, S, float(np.log2(np.e)), None, ALU.mult))
                    do(V.tensor_scalar(K, K, MAGIC, None, ALU.add))
                    do(V.tensor_scalar(K, K, MAGIC, None, ALU.subtract))
                    do(V.scalar_tensor_tensor(F, K, -LN2_A, S, ALU.mult, ALU.add))
                    do(V.scalar_tensor_tensor(F, K, -LN2_B, F, ALU.mult, ALU.add))
                    do(V.tensor_scalar(Y, F, 1.0 / 5040.0, None, ALU.mult))
                    for cf in (720.0, 120.0, 24.0, 6.0, 2.0, 1.0):
                        do(V.scalar_tensor_tensor(Y, Y, 1.0 / cf, F, ALU.add, ALU.mult))
                    do(V.tensor_scalar(Y, Y, 1.0, None, ALU.add))
                    do(V.tensor_scalar(exi[:, :], K, 127.0, None, ALU.add))
                    do(V.tensor_scalar(exi[:, :], exi[:, :], 23, None, ALU.logical_shift_left))
                    do(V.tensor_tensor(Z, Y, exi[:, :].bitcast(FP32), ALU.mult))
                    do(V.reciprocal(IV, Z))
                    dve.wait_ge(delta_ok, C)
                    for t in range(C):
                        do(V.tensor_scalar(DL[:, t, :], pD[t][:, :], LORA_SCALE, None, ALU.mult))
                    do(V.tensor_tensor(W[:, :, :], W[:, :, :], DL[:, :, :], ALU.add))
                    wide = [P, C * C, P]
                    g3 = "p t (g i) -> p (t g) i"
                    inv_b = IV.rearrange("p (n o) -> p n o", o=1).broadcast_to(wide)
                    sc_b = Z.rearrange("p (n o) -> p n o", o=1).broadcast_to(wide)
                    do(V.tensor_tensor(NR[:, :, :].rearrange(g3, g=C), W[:, :, :].rearrange(g3, g=C), inv_b, ALU.mult))

                    def leaf(o, i):
                        do(V.tensor_scalar(o[:, :, :], NR[:, :, :], cbt[:, 2, i:i + 1], cbt[:, 3, i:i + 1],
                                           ALU.is_gt, ALU.mult))
                        do(V.tensor_scalar(o[:, :, :], o[:, :, :], cbt[:, 1, i:i + 1], None, ALU.add))

                    def above(i):
                        do(V.tensor_scalar(GT[:, :, :], NR[:, :, :], cbt[:, 2, i:i + 1], None, ALU.is_gt))

                    leaf(QA, 0)
                    leaf(QB, 2)
                    above(1)
                    do(V.copy_predicated(QA[:, :, :], GT[:, :, :], QB[:, :, :]))
                    leaf(QB, 4)
                    leaf(W, 6)
                    above(5)
                    do(V.copy_predicated(QB[:, :, :], GT[:, :, :], W[:, :, :]))
                    above(3)
                    do(V.copy_predicated(QA[:, :, :], GT[:, :, :], QB[:, :, :]))
                    do(V.tensor_tensor(QA[:, :, :], QA[:, :, :], NR[:, :, :], ALU.subtract))
                    do(V.tensor_tensor(QA[:, :, :], QA[:, :, :], NR[:, :, :], ALU.add))
                    do(V.tensor_tensor(QA[:, :, :].rearrange(g3, g=C), QA[:, :, :].rearrange(g3, g=C), sc_b, ALU.mult))
                    V.tensor_tensor(W[:, :, :], QA[:, :, :], DL[:, :, :], ALU.add).then_inc(w_eff, 1)
                    dve.wait_ge(cos_ready, 1)
                    do(V.tensor_scalar(nn[:, 0, :], nwq[:, 64:P], -1.0, None, ALU.mult))
                    do(V.tensor_scalar(nn[:, 1, :], nwk[:, 64:P], -1.0, None, ALU.mult))
                    for A_t, B_t, nw, neg in ((qA, qB, nwq, nn[:, 0, :]), (kA, kB, nwk, nn[:, 1, :])):
                        for o, trig, w in ((A_t[:, :, 0:64], cs, nw[:, 0:64]), (A_t[:, :, 64:P], cs, nw[:, 64:P]),
                                           (B_t[:, :, 0:64], sn, neg), (B_t[:, :, 64:P], sn, nw[:, 0:64])):
                            do(V.tensor_tensor(o, trig[:, :, :],
                                               w.rearrange("p (o f) -> p o f", o=1).broadcast_to([P, B, 64]), ALU.mult))
                    for i in range(C):
                        dve.wait_ge(w_hi, i + 1)
                        V.tensor_tensor(w0TL[:, i, :], pD[i][:, :], w0TH[:, i, :].bitcast(FP32), ALU.subtract
                                        ).then_inc(w_lo, 1)

            dense = ExitStack()
            with dense:
                c = dense
                w1r = sbuf(c, "w1r", [P, C, D])
                a1r = sbuf(c, "a1r", [P, C, P])
                b1r = sbuf(c, "b1r", [P, D])
                bi1 = sbuf(c, "bi1", [P, D])
                w1H = sbuf(c, "w1H", [P, C, D], F32R)
                w1L = sbuf(c, "w1L", [P, C, D], F32R)
                a1H = sbuf(c, "a1H", [P, C, P], F32R)
                a1L = sbuf(c, "a1L", [P, C, P], F32R)
                b1H = sbuf(c, "b1H", [P, D], F32R)
                b1L = sbuf(c, "b1L", [P, D], F32R)
                xsH = [sbuf(c, f"xsH{i}", [P, C, P], F32R) for i in range(2)]
                xsL = [sbuf(c, f"xsL{i}", [P, C, P], F32R) for i in range(2)]
                lo_f = sbuf(c, "lo_f", [P, P])
                loH = sbuf(c, "loH", [P, P], F32R)
                loL = sbuf(c, "loL", [P, P], F32R)
                ys = [sbuf(c, f"ys{i}", [P, D]) for i in range(2)]
                yn = sbuf(c, "yn", [P, D])
                pY = [psum(c, f"pY{i}", [P, D]) for i in range(2)]
                pX = [psum(c, f"pX{i}", [P, D]) for i in range(2)]
                pL = psum(c, "pL", [P, P])
                (w1_in, w1_hi, w1_lo, xs_hi, xs_lo, low_done, low_f, low_hi, low_lo, y_done, y_out, y_mid, acc_in,
                 t_done, t_out, c_in0, c_in1, c_hi, c_lo, act_passed) = counted(
                    c, "w1_in", "w1_hi", "w1_lo", "xs_hi", "xs_lo", "low_done", "low_f", "low_hi", "low_lo", "y_done",
                    "y_out", "y_mid", "acc_in", "t_done", "t_out", "c_in0", "c_in1", "c_hi", "c_lo", "act_passed")
                c_in = [c_in0, c_in1]
                block = c.enter_context(nc.Block())

                def rows(engine, body, first, last):
                    while first % 2:
                        body(first, first % B, first % 2)
                        first += 1
                    end = last + 1 - (last + 1 - first) % 2
                    with engine.Fori(0, (end - first) // 2) as i:
                        for p in range(2):
                            body(i * 2 + (first + p), i * 2 + (first + p) % B, p)
                    for n in range(end, last + 1):
                        body(n, n % B, n % 2)

                @block.sync
                def _(sp):
                    sp.dma_start(w1r[:, :, :], w1T).then_inc(w1_in, 16)
                    sp.dma_start(a1r[:, :, :], a1T).then_inc(w1_in, 16)
                    sp.dma_start(b1r[:, :], b1).then_inc(w1_in, 16)
                    sp.dma_start(bi1[:, :], bias1.rearrange("(o n) -> o n", o=1).broadcast_to([P, D])
                                 ).then_inc(w1_in, 16)
                    for m in range(LEAD):
                        wait(sp, c_lo, m - 1)
                        sp.dma_start(wr[m % 2][:, :], wall[m]).then_inc(c_in[m % 2], 16)
                    sp.wait_ge(w1_in, 64)

                @block.gpsimd
                def _(pool):
                    pool.wait_ge(w1_in, 64)
                    nc.gpsimd.tensor_copy(w1H[:, :, :], w1r[:, :, :]).then_inc(w1_hi, 1)
                    nc.gpsimd.tensor_copy(a1H[:, :, :], a1r[:, :, :]).then_inc(w1_hi, 1)
                    nc.gpsimd.tensor_copy(b1H[:, :], b1r[:, :]).then_inc(w1_hi, 1)
                    pool.wait_ge(w1_hi, 3)
                    nc.gpsimd.tensor_tensor(w1L[:, :, :], w1r[:, :, :], w1H[:, :, :].bitcast(FP32), ALU.subtract
                                            ).then_inc(w1_lo, 1)
                    nc.gpsimd.tensor_tensor(a1L[:, :, :], a1r[:, :, :], a1H[:, :, :].bitcast(FP32), ALU.subtract
                                            ).then_inc(w1_lo, 1)
                    nc.gpsimd.tensor_tensor(b1L[:, :], b1r[:, :], b1H[:, :].bitcast(FP32), ALU.subtract
                                            ).then_inc(w1_lo, 1)
                    for m in range(LEAD):
                        at = slice(m * CHUNK, (m + 1) * CHUNK)
                        pool.wait_ge(c_in[m % 2], 16 * (m // 2 + 1))
                        nc.gpsimd.tensor_copy(wH[:, at], wr[m % 2][:, :]).then_inc(c_hi, 1)
                        pool.wait_ge(c_hi, m + 1)
                        nc.gpsimd.tensor_tensor(wL[:, at], wr[m % 2][:, :], wH[:, at].bitcast(FP32), ALU.subtract
                                                ).then_inc(c_lo, 1)

                @block.scalar
                def _(act):
                    def hold(sem, value):
                        if isinstance(value, int) and value <= 0:
                            return
                        act.wait_ge(sem, value)
                        if not isinstance(value, int):
                            act.sem_inc(act_passed, 1)

                    def split_row(n, b, p):
                        hold(y_done, n - 1)
                        if not isinstance(n, int) or n >= B:
                            hold(t_out, n - (B - 1))
                        nc.scalar.copy(xsH[p][:, :, :], xTs[:, :, bass.ds(b * P, P)]).then_inc(xs_hi, 1)

                    def finish_row(n, b, p):
                        hold(y_out, n + 1)
                        nc.scalar.copy(acc[:, bass.ds(b, 1), :].rearrange("p o n -> p (o n)"), ys[p][:, :]
                                       ).then_inc(acc_in, 1)
                        hold(t_done, n + 1)
                        nc.scalar.copy(xTs[:, :, bass.ds(b * P, P)], pX[p][:, :].rearrange("p (c t) -> p c t", c=C)
                                       ).then_inc(t_out, 1)

                    split_row(0, 0, 0)
                    split_row(1, 1, 1)
                    for n in (0, 1):
                        finish_row(n, n, n)
                        split_row(n + 2, n + 2, n)

                    def body0(n, b, p):
                        finish_row(n, b, p)
                        hold(y_done, n + 1)
                        nc.scalar.copy(xsH[p][:, :, :], xTs[:, :, bass.ds((b + 2) * P, P)]).then_inc(xs_hi, 1)
                    rows(act, body0, 2, 5)
                    for n in (6, 7):
                        finish_row(n, n, n % 2)
                        split_row(n + 2, n + 2 - B, n % 2)

                    def body1(n, b, p):
                        finish_row(n, b, p)
                        hold(y_done, n + 1)
                        hold(t_out, n - 5)
                        nc.scalar.copy(xsH[p][:, :, :], xTs[:, :, bass.ds((b + 2) * P, P)]).then_inc(xs_hi, 1)
                    rows(act, body1, 8, 13)
                    for n in (14, 15):
                        finish_row(n, n - B, n % 2)

                @block.vector
                def _(dve):
                    V = nc.vector

                    def low_part(n, b, p):
                        dve.wait_ge(xs_hi, n + 1)
                        V.tensor_tensor(xsL[p][:, :, :], xTs[:, :, bass.ds(b * P, P)], xsH[p][:, :, :].bitcast(FP32),
                                        ALU.subtract).then_inc(xs_lo, 1)

                    def adapter_part(n, b, p):
                        k = n - B
                        dve.wait_ge(low_done, k + 1)
                        V.tensor_scalar(lo_f[:, :], pL[:, :], sel[:, bass.ds(b, 1)], None, ALU.mult).then_inc(low_f, 1)
                        dve.wait_ge(low_f, k + 1)
                        if not isinstance(n, int) or k >= 1:
                            dve.wait_ge(y_done, n)
                        V.tensor_copy(loH[:, :], lo_f[:, :]).then_inc(low_hi, 1)
                        dve.wait_ge(low_hi, k + 1)
                        V.tensor_tensor(loL[:, :], lo_f[:, :], loH[:, :].bitcast(FP32), ALU.subtract
                                        ).then_inc(low_lo, 1)

                    def sum_row(n, b, p):
                        a = acc[:, bass.ds(b, 1), :].rearrange("p o n -> p (o n)")
                        dve.wait_ge(y_done, n + 1)
                        wait(dve, t_done, n - 1)
                        wait(dve, acc_in, n - 1)
                        if isinstance(n, int) and n < B or not isinstance(n, int) and phase[0] == 0:
                            V.tensor_tensor(ys[p][:, :], pY[p][:, :], a, ALU.add).then_inc(y_out, 1)
                        else:
                            V.tensor_tensor(yn[:, :], pY[p][:, :], a, ALU.add).then_inc(y_mid, 1)
                            dve.wait_ge(y_mid, n - B + 1)
                            V.tensor_tensor(ys[p][:, :], yn[:, :], bi1[:, :], ALU.add).then_inc(y_out, 1)

                    phase = [0]
                    low_part(0, 0, 0)
                    low_part(1, 1, 1)
                    for n in (0, 1):
                        sum_row(n, n, n)
                        low_part(n + 2, n + 2, n)

                    def body0(n, b, p):
                        sum_row(n, b, p)
                        low_part(n + 2, b + 2, p)
                    rows(dve, body0, 2, 5)
                    sum_row(6, 6, 0)
                    low_part(8, 0, 0)
                    sum_row(7, 7, 1)
                    adapter_part(8, 0, 0)
                    low_part(9, 1, 1)
                    phase[0] = 1

                    def body1(n, b, p):
                        sum_row(n, b, p)
                        adapter_part(n + 1, b + 1, 1 - p)
                        low_part(n + 2, b + 2, p)
                    rows(dve, body1, 8, 13)
                    sum_row(14, 6, 0)
                    adapter_part(15, 7, 1)
                    sum_row(15, 7, 1)

                @block.tensor
                def _(pe):
                    def produce(n, b, p, layer):
                        pe.wait_ge(xs_lo, n + 1)
                        wait(pe, y_out, n - 1)
                        if layer == 0:
                            product(pY[p][:, :], [(xsH[p][:, i, :], xsL[p][:, i, :], w0TH[:, i, :], w0TL[:, i, :])
                                                  for i in range(C)]).then_inc(y_done, 1)
                            return
                        k = n - B
                        wait(pe, low_f, k)
                        product(pL[:, :], [(a1H[:, i, :], a1L[:, i, :], xsH[p][:, i, :], xsL[p][:, i, :])
                                           for i in range(C)]).then_inc(low_done, 1)
                        for i in range(C):
                            mm(pY[p][:, :], xsH[p][:, i, :], w1H[:, i, :], i == 0, False)
                            mm(pY[p][:, :], xsL[p][:, i, :], w1H[:, i, :], False, False)
                            mm(pY[p][:, :], xsH[p][:, i, :], w1L[:, i, :], False, False)
                        pe.wait_ge(low_lo, k + 1)
                        mm(pY[p][:, :], loH[:, :], b1H[:, :], False, False)
                        mm(pY[p][:, :], loL[:, :], b1H[:, :], False, False)
                        mm(pY[p][:, :], loH[:, :], b1L[:, :], False, True).then_inc(y_done, 1)

                    def turn(n, b, p):
                        pe.wait_ge(y_out, n + 1)
                        wait(pe, t_out, n - 1)
                        for i in range(C):
                            last = nc.tensor.transpose(pX[p][:, i * P:(i + 1) * P], ys[p][:, i * P:(i + 1) * P],
                                                       ident[:, :])
                        last.then_inc(t_done, 1)

                    produce(0, 0, 0, 0)
                    produce(1, 1, 1, 0)
                    for n in (0, 1):
                        turn(n, n, n)
                        produce(n + 2, n + 2, n, 0)

                    def body0(n, b, p):
                        turn(n, b, p)
                        produce(n + 2, b, p, 0)
                    rows(pe, body0, 2, 5)
                    pe.wait_ge(w1_lo, 3)
                    for n in (6, 7):
                        turn(n, n, n % 2)
                        produce(n + 2, n, n % 2, 1)

                    def body1(n, b, p):
                        turn(n, b, p)
                        produce(n + 2, b, p, 1)
                    rows(pe, body1, 8, 13)
                    turn(14, 6, 0)
                    turn(15, 7, 1)

        attention(nc, outer, acc, xTs, qA, qB, kA, kB, ident, key_no, seqf, pages, wH, wL, wr, wall, k_cache, v_cache)
        weights.close()
        last_layer(nc, acc, ident, cfs, mask, w3T, bias3, out)


def kernel(**inputs):
    import numpy as _np
    import concourse.bacc as _bacc
    from concourse import mybir as _mybir
    from concourse.bass_utils import run_bass_kernel_spmd as _run

    given = {k: _np.asarray(v) for k, v in inputs.items()}

    def columns(w):
        return w.T.reshape(C, P, w.shape[0]).transpose(1, 0, 2)

    wq, wk, wv = (columns(given[f"L2_cond_W{n}"]) for n in "qkv")
    wo = given["L2_cond_Wo"].T.reshape(G, R, P, D).transpose(0, 2, 1, 3)
    heads = []
    for g in range(G):
        qkv = _np.concatenate([wq[:, :, g * R * P:(g + 1) * R * P], wk[:, :, g * P:(g + 1) * P],
                               wv[:, :, g * P:(g + 1) * P]], axis=2).reshape(P, C * QKV)
        whole = _np.concatenate([qkv, wo[g].reshape(P, R * D)], axis=1)
        heads.append(whole.reshape(P, CHUNKS, CHUNK).transpose(1, 0, 2))
    inv_freq = (1.0 / _np.float32(10000.0) ** (_np.arange(0, P, 2, dtype=_np.float32) / _np.float32(P))
                ).astype(_np.float32)
    layout = {
        "x": given["x"],
        "xT": given["x"].reshape(B * P, D).T.reshape(C, P, B * P).transpose(1, 0, 2),
        "seqlens": given["itok_B_207_1644"],
        "adapter": given["itok_B_1_7"],
        "table": given["itok_Bx16_0_63"],
        "coeff": given["condB_coeff"],
        "mask": given["mask_Bx4096x4096_ik1"],
        "codebook": given["condB_codebook"],
        "w0": given["L0_cond_weight"],
        "scale_log": given["L0_cond_scale_log"],
        "loraA": given["L0_cond_lora_A"],
        "loraBT": given["L0_cond_lora_B"].T,
        "w1T": columns(given["L1_cond_weight"]),
        "bias1": given["L1_cond_bias"],
        "a1T": columns(given["L1_cond_lora_a_weights"].reshape(P, D)),
        "b1": given["L1_cond_lora_b_weights"].transpose(0, 2, 1).reshape(P, D),
        "scaling": given["L1_cond_scaling_factors"],
        "wall": _np.concatenate(heads, axis=0),
        "wqn": given["L2_cond_q_norm_w"],
        "wkn": given["L2_cond_k_norm_w"],
        "k_cache": given["L2_cond_k_cache"],
        "v_cache": given["L2_cond_v_cache"],
        "w3T": columns(given["L3_cond_W"]),
        "bias3": given["L3_cond_b"],
        "invf": inv_freq,
    }
    nc = _bacc.Bacc("TRN2", target_bir_lowering=False, num_devices=1, dynamic_dma_scratch_size=1024)
    arrays, args = {}, {}
    for name, a in layout.items():
        a = _np.ascontiguousarray(a)
        arrays[f"in_{name}"] = a
        args[name] = nc.dram_tensor(f"in_{name}", a.shape, _mybir.dt.from_np(a.dtype), kind="ExternalInput").ap()
    args["out"] = nc.dram_tensor("out", (B, P, D), _mybir.dt.from_np(_np.dtype("float32")),
                                 kind="ExternalOutput").ap()
    program(nc, **args)
    r = _run(nc, [arrays], core_ids=[0])
    return r.results[0]["out"]
```

```python
import concourse.bass as bass
from concourse import mybir
from contextlib import ExitStack
import numpy as np

FP32 = mybir.dt.float32
F32R = mybir.dt.float32r
I32 = mybir.dt.int32
ALU = mybir.AluOpType
ACT = mybir.ActivationFunctionType
AX = mybir.AxisListType

P = 128
B = 8
D = 512
C = D // P
G = 8
R = 4
PAGE = 32
NPAGE = 16
PAGES = 64
CACHE = NPAGE * PAGE
KT = CACHE // P
KEYS = CACHE + P
JT = KEYS // P
STEPS = G * B
QKV = R * P + 2 * P
REGION = C * QKV + R * D
CHUNKS = 8
CHUNK = REGION // CHUNKS
LEAD = 9
SCALE = 1.0 / float(np.sqrt(P))
EPS = 1e-6
NEG = -1e30
RANK = 16
ADAPTERS = 8
LORA_SCALE = 32.0 / 64.0
MAGIC = 1.5 * 2.0 ** 23
TWO_PI = 2.0 * np.pi
PI_A = 6.28125
PI_B = float(np.float32(0.0019350051879882812))
PI_C = float(np.float32(TWO_PI - PI_A - PI_B))
LN2_A = 0.693359375
LN2_B = float(np.float32(np.log(2.0) - LN2_A))
BELOW_PI = 3.1415925
HALF = KEYS // 2
HUGE = 2.0 ** 93
LOWEST = -3.4e38
BANK = [0, 1, 0, 1, 1]


def wait(engine, semaphore, value):
    if isinstance(value, int) and value <= 0:
        return
    engine.wait_ge(semaphore, value)


def matmul(nc, o, l, r, start, stop):
    return nc.tensor.matmul(o, l, r, start=start, stop=stop)


def passes(nc, o, terms, first=True, last=True):
    for i, (lh, ll, rh, rl) in enumerate(terms):
        matmul(nc, o, lh, rh, first and i == 0, False)
        matmul(nc, o, ll, rh, False, False)
        done = matmul(nc, o, lh, rl, False, last and i == len(terms) - 1)
    return done


def attention(nc, acc, xTH, xTL, qA, qB, kA, kB, ident, key_no, late_from, pages, wH, wL, wr, wall, kv_cache):
    ctx = ExitStack()
    with ctx:
        def sbuf(name, shape, dt=FP32):
            return ctx.enter_context(nc.sbuf_tensor(name, shape, dt))

        def psum(name, shape):
            return ctx.enter_context(nc.psum_tensor(name, shape, FP32))

        def sem(name):
            return ctx.enter_context(nc.semaphore(name))

        xH = sbuf("xH", [P, C, P], F32R)
        xL = sbuf("xL", [P, C, P], F32R)
        kv_raw = [sbuf(f"kv_raw{i}", [P, KT, 2, P]) for i in range(2)]
        vH = [sbuf(f"vH{i}", [P, JT, P], F32R) for i in range(2)]
        vL = [sbuf(f"vL{i}", [P, JT, P], F32R) for i in range(2)]
        kH = sbuf("kH", [P, KEYS], F32R)
        kL = sbuf("kL", [P, KEYS], F32R)
        qH = sbuf("qH", [P, R * P], F32R)
        qL = sbuf("qL", [P, R * P], F32R)
        q_u = sbuf("q_u", [P, R, P])
        q_w = sbuf("q_w", [P, R, P])
        kv = sbuf("kv", [P, 2, P])
        k_u = sbuf("k_u", [P, P])
        k_w = sbuf("k_w", [P, P])
        k_rot = sbuf("k_rot", [P, P])
        q_sums = sbuf("q_sums", [P, R])
        k_sum = sbuf("k_sum", [P, 1])
        q_mean = sbuf("q_mean", [P, R])
        k_mean = sbuf("k_mean", [P, 1])
        halves = sbuf("halves", [P, R])
        k_inv = sbuf("k_inv", [P, 1])
        q_inv = [sbuf(f"q_inv{i}", [P, R]) for i in range(2)]
        late = sbuf("late", [P, 2, HALF])
        row_max = sbuf("row_max", [P, R])
        bias = [sbuf(f"bias{i}", [P, R]) for i in range(2)]
        prob = [sbuf(f"prob{i}", [P, R, KEYS]) for i in range(2)]
        den = [sbuf(f"den{i}", [P, R]) for i in range(2)]
        den_inv = [sbuf(f"den_inv{i}", [P, R]) for i in range(2)]
        ptH = [sbuf(f"ptH{i}", [P, R * P], F32R) for i in range(2)]
        ptL = [sbuf(f"ptL{i}", [P, R * P], F32R) for i in range(2)]
        oH = sbuf("oH", [P, R * P], F32R)
        oL = sbuf("oL", [P, R * P], F32R)
        table_out = sbuf("table_out", [P, 1])

        scores = [psum(f"scores{i}", [P, 2, 512]) for i in range(2)]
        turned = [psum(f"turned{i}", [P, R * P]) for i in range(2)]
        p_q = psum("p_q", [P, R * P])
        p_o = psum("p_o", [P, R * P])

        kv_done, q_done, scored = sem("kv_done"), sem("q_done"), sem("scored")
        prob_turned, pv_done, out_done = sem("prob_turned"), sem("pv_done"), sem("out_done")
        cache_turned, q_turned, k_turned = sem("cache_turned"), sem("q_turned"), sem("k_turned")
        x_ready = sem("x_ready")
        late_ok, exp_done, pt_hi, kv_copied, k_sq, q_sq = (sem(x) for x in (
            "late_ok", "exp_done", "pt_hi", "kv_copied", "k_sq", "q_sq"))
        o_hi, cache_hi, q_hi, k_hi, table_in, w_hi = (sem(x) for x in (
            "o_hi", "cache_hi", "q_hi", "k_hi", "table_in", "w_hi"))
        row_max_ok, bias_ok, pt_lo, inv_ok = (sem(x) for x in ("row_max_ok", "bias_ok", "pt_lo", "inv_ok"))
        o_lo, q_parts, sums_ok, cache_lo, q_lo, k_lo, added = (sem(x) for x in (
            "o_lo", "q_parts", "sums_ok", "cache_lo", "q_lo", "k_lo", "added"))
        v_hi, v_lo, w_lo, normed, k_parts, k_added = (sem(x) for x in (
            "v_hi", "v_lo", "w_lo", "normed", "k_parts", "k_added"))
        k_mean_ok, k_inv_ok, q_mean_ok, q_inv_ok, k_ready, q_ready, const_ok = (sem(x) for x in (
            "k_mean_ok", "k_inv_ok", "q_mean_ok", "q_inv_ok", "k_ready", "q_ready", "const_ok"))
        act_passed, pool_passed, dve_passed = sem("act_passed"), sem("pool_passed"), sem("dve_passed")
        w_in = sem("w_in")
        kv_in = [sem("kv_in0"), sem("kv_in1")]

        def hold(engine, passed, semaphore, value):
            if isinstance(value, int):
                wait(engine, semaphore, value)
                return
            engine.wait_ge(semaphore, value)
            engine.sem_inc(passed, 1)

        def steps(engine, turn):
            turn(-1, 1, False, False, False, True)
            turn(0, 0, False, False, True, True)
            turn(1, 1, False, True, True, True)
            with engine.Fori(1, STEPS // 2 - 1) as i:
                turn(i * 2, 0, True, True, True, True)
                turn(i * 2 + 1, 1, True, True, True, True)
            turn(STEPS - 2, 0, True, True, True, True)
            turn(STEPS - 1, 1, True, True, True, False)
            turn(STEPS, 0, True, True, False, False)
            turn(STEPS + 1, 1, True, False, False, False)

        block = ctx.enter_context(nc.Block())

        @block.sync
        def _(sp):
            heads_of_pages = kv_cache.rearrange("n g s d -> (n g) s d")

            def load_pages(m, p):
                b, g = m % B, m // B
                _, numbers = nc.values_load_multi_w_load_instructions(
                    pages[0:1, bass.ds(b * NPAGE, NPAGE)], engines=(mybir.EngineType.SP,), min_val=0,
                    max_val=PAGES - 1, skip_runtime_bounds_check_because="they were clamped to the cache on the chip")
                wait(sp, cache_turned, m - 1)
                wait(sp, v_lo, m - 1)
                for j in range(NPAGE):
                    rows = slice(PAGE * (j % 4), PAGE * (j % 4 + 1))
                    sp.dma_start(kv_raw[p][rows, j // 4, :, :],
                                 heads_of_pages[bass.ds(numbers[j] * G + g, 1), :, :].rearrange(
                                     "o s (a d) -> (o s) a d", a=2)).then_inc(kv_in[p], 16)

            def load_weights(m):
                wait(sp, w_lo, m - LEAD)
                sp.dma_start(wr[:, :], wall[bass.ds(m % (G * CHUNKS), 1), :, :].rearrange("o p n -> (o p) n")
                             ).then_inc(w_in, 16)

            def turn(n, p):
                load_pages(n + 2, p)
                load_weights(n + LEAD + 1)

            load_weights(LEAD)
            load_pages(0, 0)
            load_pages(1, 1)
            turn(0, 0)
            with sp.Fori(0, (STEPS - 4) // 2) as i:
                turn(i * 2 + 1, 1)
                turn(i * 2 + 2, 0)
            load_pages(STEPS - 1, 1)
            for p in range(2):
                sp.wait_ge(kv_in[p], 16 * NPAGE * STEPS // 2)

        @block.gpsimd
        def _(pool):
            Gp = nc.gpsimd
            Gp.memset(halves[:, :], -0.5).then_inc(const_ok, 1)
            pool.wait_ge(const_ok, 1)

            def rounded(o, full):
                return Gp.tensor_scalar(o, full, 1.0, 1.0, ALU.mult, ALU.mult)

            def turn(n, p, outs, ends, works, begins):
                q = 1 - p
                m = n + 1
                if works:
                    hold(pool, pool_passed, kv_copied, n + 1)
                    if outs:
                        hold(pool, pool_passed, pv_done, (n - 1) * JT)
                    hold(pool, pool_passed, kv_in[p], 16 * NPAGE * (n // 2 + 1))
                    rounded(vH[p][:, KT, :], kv[:, 1, :]).then_inc(v_hi, 1)
                    rounded(vH[p][:, 0:KT, :], kv_raw[p][:, :, 1, :]).then_inc(v_hi, 1)
                    hold(pool, pool_passed, v_hi, (n + 1) * 2)
                    Gp.tensor_tensor(vL[p][:, KT, :], kv[:, 1, :], vH[p][:, KT, :].bitcast(FP32), ALU.subtract)
                    Gp.tensor_tensor(vL[p][:, 0:KT, :], kv_raw[p][:, :, 1, :], vH[p][:, 0:KT, :].bitcast(FP32),
                                     ALU.subtract).then_inc(v_lo, 1)
                    if not isinstance(n, int) or n < STEPS - 2:
                        at = bass.ds(((n + LEAD) % (2 * CHUNKS)) * CHUNK, CHUNK)
                        hold(pool, pool_passed, w_hi, n + 1)
                        Gp.tensor_tensor(wL[:, at], wr[:, :], wH[:, at].bitcast(FP32), ALU.subtract
                                         ).then_inc(w_lo, 1)
                    for h in range(R):
                        hold(pool, pool_passed, inv_ok, n * R + h + 1)
                        last = Gp.tensor_scalar(prob[p][:, h, :], prob[p][:, h, :], den_inv[p][:, h:h + 1], 1.0,
                                                ALU.mult, ALU.mult)
                    last.then_inc(normed, 1)
                if begins:
                    row = bass.ds(m % B, 1)
                    hold(pool, pool_passed, q_parts, m + 1)
                    Gp.tensor_tensor(q_u[:, :, :], q_u[:, :, :], q_w[:, :, :], ALU.add).then_inc(q_ready, 1)
                    hold(pool, pool_passed, k_sq, m + 1)
                    Gp.tensor_scalar(k_mean[:, :], k_sum[:, :], 1.0 / P, EPS, ALU.mult, ALU.add).then_inc(k_mean_ok, 1)
                    a = kA[:, row, :].rearrange("p o d -> p (o d)")
                    b_ = kB[:, row, :].rearrange("p o d -> p (o d)")
                    Gp.tensor_tensor(k_u[:, :], kv[:, 0, :], a, ALU.mult).then_inc(k_parts, 1)
                    Gp.tensor_tensor(k_w[:, 0:64], kv[:, 0, 64:P], b_[:, 0:64], ALU.mult).then_inc(k_parts, 1)
                    Gp.tensor_tensor(k_w[:, 64:P], kv[:, 0, 0:64], b_[:, 64:P], ALU.mult).then_inc(k_parts, 1)
                    hold(pool, pool_passed, k_mean_ok, m + 1)
                    Gp.tensor_tensor(k_inv[:, :], k_mean[:, :], halves[:, 0:1], ALU.pow).then_inc(k_inv_ok, 1)
                    hold(pool, pool_passed, k_parts, (m + 1) * 3)
                    Gp.tensor_tensor(k_u[:, :], k_u[:, :], k_w[:, :], ALU.add).then_inc(k_added, 1)
                    hold(pool, pool_passed, k_added, m + 1)
                    hold(pool, pool_passed, k_inv_ok, m + 1)
                    hold(pool, pool_passed, k_turned, m)
                    Gp.tensor_scalar(k_rot[:, :], k_u[:, :], k_inv[:, 0:1], 1.0, ALU.mult, ALU.mult
                                     ).then_inc(k_ready, 1)
                    hold(pool, pool_passed, sums_ok, m + 1)
                    Gp.tensor_scalar(q_mean[:, :], q_sums[:, :], 1.0, P * EPS, ALU.mult, ALU.add).then_inc(q_mean_ok, 1)
                    hold(pool, pool_passed, q_mean_ok, m + 1)
                    Gp.tensor_tensor(q_inv[q][:, :], q_mean[:, :], halves[:, :], ALU.pow).then_inc(q_inv_ok, 1)

            steps(pool, turn)

        @block.scalar
        def _(act):
            A = nc.scalar
            A.activation(table_out[:, :], ident[:, 0:1], ACT.Exp).then_inc(table_in, 1)

            def place_row(m):
                cols = bass.ds((m % B) * P, P)
                hold(act, act_passed, kv_done, m)
                A.copy(xH[:, :, :], xTH[:, :, cols].bitcast(FP32))
                A.copy(xL[:, :, :], xTL[:, :, cols]).then_inc(x_ready, 1)

            def turn(n, p, outs, ends, works, begins):
                q = 1 - p
                m = n + 1

                def prob_part(s, parity, j):
                    act.wait_ge(prob_turned, s * JT + j + 1)
                    wait(act, pv_done, s * JT + j - 1)
                    A.copy(ptH[(parity + j) % 2][:, :], turned[BANK[j]][:, :]).then_inc(pt_hi, 1)

                def soft(h):
                    act.wait_ge(bias_ok, n * R + h + 1)
                    if h == 0:
                        wait(act, prob_turned, (n - 1) * JT)
                    A.activation(prob[p][:, h, :].rearrange("p (a k) -> p a k", a=2), scores[h % 2][:, :, 0:HALF],
                                 ACT.Exp, bias=bias[p][:, h:h + 1], scale=q_inv[p][:, h:h + 1],
                                 accum_out=den[p][:, h:h + 1]).then_inc(exp_done, 1)

                if works:
                    soft(0)
                    if not isinstance(n, int) or n < STEPS - 2:
                        at = bass.ds(((n + LEAD) % (2 * CHUNKS)) * CHUNK, CHUNK)
                        hold(act, act_passed, w_in, 16 * (n + 1))
                        A.copy(wH[:, at], wr[:, :]).then_inc(w_hi, 1)
                    soft(1)
                    soft(2)
                if ends:
                    prob_part(n - 1, q, 2)
                if works:
                    soft(3)
                if ends:
                    prob_part(n - 1, q, 3)
                if begins:
                    act.wait_ge(kv_done, m + 1)
                    wait(act, v_lo, m)
                    wait(act, k_added, m)
                    A.copy(kv[:, :, :], turned[0][:, 0:2 * P].rearrange("p (a d) -> p a d", a=2)).then_inc(kv_copied, 1)
                    wait(act, k_mean_ok, m)
                    act.wait_ge(kv_copied, m + 1)
                    A.activation(k_w[:, :], kv[:, 0, :], ACT.Square, accum_out=k_sum[:, :]).then_inc(k_sq, 1)
                if ends:
                    prob_part(n - 1, q, 4)
                if begins:
                    act.wait_ge(cache_turned, m + 1)
                    wait(act, scored, m * R)
                    A.copy(kH[:, 0:CACHE], turned[0][:, :]).then_inc(cache_hi, 1)
                    act.wait_ge(q_ready, m + 1)
                    A.activation(q_w[:, :, :], p_q[:, :].rearrange("p (h d) -> p h d", h=R), ACT.Square
                                 ).then_inc(q_sq, 1)
                    act.wait_ge(q_turned, m + 1)
                    A.copy(qH[:, :], turned[1][:, :]).then_inc(q_hi, 1)
                    act.wait_ge(k_turned, m + 1)
                    A.copy(kH[:, CACHE:KEYS], p_q[:, 0:P]).then_inc(k_hi, 1)
                    hold(act, act_passed, row_max_ok, m * R)
                    A.activation(late[:, :, :], key_no[:, :, :], ACT.Relu, bias=late_from[:, bass.ds(m % B, 1)],
                                 scale=HUGE).then_inc(late_ok, 1)
                    if not isinstance(m, int) or m + 1 < STEPS:
                        place_row(m + 1)
                if ends:
                    act.wait_ge(pv_done, n * JT)
                    wait(act, out_done, n - 1)
                    A.copy(oH[:, :], p_o[:, :]).then_inc(o_hi, 1)
                if works:
                    prob_part(n, p, 0)
                    prob_part(n, p, 1)

            place_row(0)
            steps(act, turn)

        @block.vector
        def _(dve):
            V = nc.vector

            def rest(o, full, high):
                return V.tensor_tensor(o, full, high.bitcast(FP32), ALU.subtract)

            def turn(n, p, outs, ends, works, begins):
                q = 1 - p
                m = n + 1

                def prob_part(s, parity, j):
                    dve.wait_ge(pt_hi, s * JT + j + 1)
                    t = (parity + j) % 2
                    rest(ptL[t][:, :], turned[BANK[j]][:, :], ptH[t][:, :]
                         ).then_inc(pt_lo, 1)

                def masked_max(h):
                    s = scores[h % 2][:, :, 0:HALF]
                    hold(dve, dve_passed, scored, n * R + h + 1)
                    V.tensor_tensor_reduce(out=s, in0=s, in1=late[:, :, :], scale=1.0, scalar=LOWEST,
                                           op0=ALU.subtract, op1=ALU.max, accum_out=row_max[:, h:h + 1]
                                           ).then_inc(row_max_ok, 1)
                    dve.wait_ge(row_max_ok, n * R + h + 1)
                    V.scalar_tensor_tensor(bias[p][:, h:h + 1], row_max[:, h:h + 1], -1.0, q_inv[p][:, h:h + 1],
                                           ALU.mult, ALU.mult).then_inc(bias_ok, 1)

                def inverse(h):
                    dve.wait_ge(exp_done, n * R + h + 1)
                    V.reciprocal(den_inv[p][:, h:h + 1], den[p][:, h:h + 1]).then_inc(inv_ok, 1)

                if works:
                    hold(dve, dve_passed, late_ok, n + 1)
                    hold(dve, dve_passed, q_inv_ok, n + 1)
                    masked_max(0)
                    masked_max(1)
                    inverse(0)
                if outs:
                    a = acc[:, bass.ds((n - 2) % B, 1), :].rearrange("p o d -> p (o d)")
                    dve.wait_ge(out_done, n - 1)
                    V.tensor_tensor(a, p_o[:, :], a, ALU.add).then_inc(added, 1)
                if works:
                    masked_max(2)
                    inverse(1)
                if ends:
                    prob_part(n - 1, q, 2)
                if works:
                    masked_max(3)
                    inverse(2)
                if ends:
                    prob_part(n - 1, q, 3)
                if works:
                    inverse(3)
                if begins:
                    row = bass.ds(m % B, 1)
                    heads = p_q[:, :].rearrange("p (h d) -> p h d", h=R)
                    dve.wait_ge(q_done, m + 1)
                    wait(dve, q_turned, m)
                    V.tensor_tensor(q_w[:, :, 0:64], heads[:, :, 64:P], qB[:, row, 0:64].broadcast_to([P, R, 64]),
                                    ALU.mult)
                    V.tensor_tensor(q_w[:, :, 64:P], heads[:, :, 0:64], qB[:, row, 64:P].broadcast_to([P, R, 64]),
                                    ALU.mult)
                    V.tensor_tensor(q_u[:, :, :], heads, qA[:, row, :].broadcast_to([P, R, P]), ALU.mult
                                    ).then_inc(q_parts, 1)
                if ends:
                    prob_part(n - 1, q, 4)
                if begins:
                    dve.wait_ge(cache_hi, m + 1)
                    rest(kL[:, 0:CACHE], turned[0][:, :], kH[:, 0:CACHE]).then_inc(cache_lo, 1)
                    dve.wait_ge(q_sq, m + 1)
                    wait(dve, q_mean_ok, m)
                    V.tensor_reduce(q_sums[:, :], q_w[:, :, :], AX.X, ALU.add).then_inc(sums_ok, 1)
                    dve.wait_ge(q_hi, m + 1)
                    rest(qL[:, :], turned[1][:, :], qH[:, :]).then_inc(q_lo, 1)
                    dve.wait_ge(k_hi, m + 1)
                    rest(kL[:, CACHE:KEYS], p_q[:, 0:P], kH[:, CACHE:KEYS]).then_inc(k_lo, 1)
                if ends:
                    dve.wait_ge(o_hi, n)
                    rest(oL[:, :], p_o[:, :], oH[:, :]).then_inc(o_lo, 1)
                if works:
                    prob_part(n, p, 0)
                    prob_part(n, p, 1)

            steps(dve, turn)

        @block.tensor
        def _(pe):
            def turn(n, p, outs, ends, works, begins):
                q = 1 - p
                m = n + 1

                def score(h):
                    if h == 0:
                        pe.wait_ge(q_lo, n + 1)
                        pe.wait_ge(cache_lo, n + 1)
                        pe.wait_ge(k_lo, n + 1)
                    if not (isinstance(n, int) and n == 0 and h < 2):
                        pe.wait_ge(exp_done, n * R + h - 1)
                    s = slice(h * P, (h + 1) * P)
                    for a in range(2):
                        k = slice(a * HALF, (a + 1) * HALF)
                        last = passes(nc, scores[h % 2][:, a, 0:HALF], [(qH[:, s], qL[:, s], kH[:, k], kL[:, k])])
                    last.then_inc(scored, 1)

                def turn_probs(s, buffer, j):
                    if j == 0:
                        pe.wait_ge(normed, s + 1)
                    if j == 0 and begins:
                        pe.wait_ge(cache_lo, s + 2)
                    elif j == 1 and begins:
                        pe.wait_ge(q_lo, s + 2)
                    elif j < 2:
                        pe.wait_ge(pt_lo, s * JT)
                    else:
                        pe.wait_ge(pt_lo, s * JT + (j if j == JT - 1 else j - 1))
                    for h in range(R):
                        last = nc.tensor.transpose(turned[BANK[j]][:, h * P:(h + 1) * P],
                                                   prob[buffer][:, h, j * P:(j + 1) * P], ident[:, :])
                    last.then_inc(prob_turned, 1)

                def times_values(j):
                    s = n - 1
                    pe.wait_ge(pt_lo, s * JT + j + 1)
                    if j == 0:
                        pe.wait_ge(v_lo, n)
                        wait(pe, added, n - 1)
                    t = (q + j) % 2
                    passes(nc, p_o[:, :], [(vH[q][:, j, :], vL[q][:, j, :], ptH[t][:, :], ptL[t][:, :])],
                           first=j == 0, last=j == JT - 1).then_inc(pv_done, 1)

                def project_kv():
                    base = ((m // B) % 2) * REGION
                    if ends:
                        pe.wait_ge(pt_lo, (n - 1) * JT + 3)
                    elif works:
                        pe.wait_ge(cache_lo, n + 1)
                    for i in range(C):
                        at = bass.ds(base + i * QKV + R * P, 2 * P)
                        last = passes(nc, turned[0][:, 0:2 * P], [(xH[:, i, :], xL[:, i, :], wH[:, at], wL[:, at])],
                                      first=i == 0, last=i == C - 1)
                    last.then_inc(kv_done, 1)

                def project_q():
                    base = ((m // B) % 2) * REGION
                    pe.wait_ge(x_ready, m + 1)
                    wait(pe, w_lo, n)
                    wait(pe, k_lo, m)
                    for i in range(C):
                        at = bass.ds(base + i * QKV, R * P)
                        last = passes(nc, p_q[:, :], [(xH[:, i, :], xL[:, i, :], wH[:, at], wL[:, at])],
                                      first=i == 0, last=i == C - 1)
                    last.then_inc(q_done, 1)

                def project_out(heads):
                    if heads[0] == 0:
                        pe.wait_ge(o_lo, n - 1)
                    base = (((n - 2) // B) % 2) * REGION + C * QKV
                    for h in heads:
                        s = slice(h * P, (h + 1) * P)
                        at = bass.ds(base + h * D, D)
                        last = passes(nc, p_o[:, :], [(oH[:, s], oL[:, s], wH[:, at], wL[:, at])],
                                      first=h == 0, last=h == R - 1)
                    if heads[-1] == R - 1:
                        last.then_inc(out_done, 1)

                def turn_cached_keys():
                    pe.wait_ge(kv_in[q], 16 * NPAGE * (m // 2 + 1))
                    pe.wait_ge(kv_copied, m + 1)
                    for t in range(KT):
                        last = nc.tensor.transpose(turned[0][:, t * P:(t + 1) * P], kv_raw[q][:, t, 0, :], ident[:, :])
                    last.then_inc(cache_turned, 1)

                def turn_queries():
                    pe.wait_ge(q_ready, m + 1)
                    if ends:
                        pe.wait_ge(pt_lo, n * JT)
                    elif works:
                        pe.wait_ge(q_lo, n + 1)
                    for h in range(R):
                        last = nc.tensor.transpose(turned[1][:, h * P:(h + 1) * P], q_u[:, h, :], ident[:, :])
                    last.then_inc(q_turned, 1)

                def turn_new_keys():
                    pe.wait_ge(k_ready, m + 1)
                    pe.wait_ge(q_sq, m + 1)
                    nc.tensor.transpose(p_q[:, 0:P], k_rot[:, :], ident[:, :]).then_inc(k_turned, 1)

                if works:
                    score(0)
                if outs:
                    project_out((0, 1))
                if works:
                    score(1)
                if outs:
                    project_out((2, 3))
                if works:
                    score(2)
                if ends:
                    times_values(0)
                    turn_probs(n - 1, q, 2)
                if works:
                    score(3)
                if ends:
                    times_values(1)
                    turn_probs(n - 1, q, 3)
                if begins:
                    project_q()
                    project_kv()
                if ends:
                    times_values(2)
                    turn_probs(n - 1, q, 4)
                    times_values(3)
                if begins:
                    turn_cached_keys()
                    turn_queries()
                if ends:
                    times_values(4)
                if begins:
                    turn_new_keys()
                if works:
                    turn_probs(n, p, 0)
                    turn_probs(n, p, 1)

            steps(pe, turn)


def last_layer(nc, acc, ident, cfs, mask, w3T, bias3, out):
    ctx = ExitStack()
    with ctx:
        def sbuf(name, shape, dt=FP32):
            return ctx.enter_context(nc.sbuf_tensor(name, shape, dt))

        def psum(name, shape):
            return ctx.enter_context(nc.psum_tensor(name, shape, FP32))

        def sem(name):
            return ctx.enter_context(nc.semaphore(name))

        w3 = sbuf("w3", [P, C, D])
        bi3 = sbuf("bi3", [P, D])
        mk = [sbuf(f"mk{i}", [P, C, D], I32) for i in range(2)]
        sg = sbuf("sg", [P, C, D])
        wc = sbuf("wc", [P, C, D])
        wcH = [sbuf(f"wcH{i}", [P, C, D], F32R) for i in range(2)]
        wcL = [sbuf(f"wcL{i}", [P, C, D], F32R) for i in range(2)]
        row = [sbuf(f"row{i}", [P, D]) for i in range(2)]
        tH = [sbuf(f"tH{i}", [P, C * P], F32R) for i in range(2)]
        tL = [sbuf(f"tL{i}", [P, C * P], F32R) for i in range(2)]
        rb = [sbuf(f"rb{i}", [P, D]) for i in range(2)]
        yo = [sbuf(f"yo{i}", [P, D]) for i in range(2)]
        pT = [psum(f"pT{i}", [P, D]) for i in range(2)]
        pO = [psum(f"pO{i}", [P, D]) for i in range(2)]
        cin, m_in = sem("cin"), [sem("m_in0"), sem("m_in1")]
        row_ok, sg_ok, wc_ok, wc_hi, wc_lo = (sem(x) for x in ("row_ok", "sg_ok", "wc_ok", "wc_hi", "wc_lo"))
        t_done, t_hi, t_lo, rb_ok, y_done, y_out = (sem(x) for x in ("t_done3", "t_hi", "t_lo", "rb_ok", "y_done3", "y_out3"))
        stored = [sem("stored0"), sem("stored1")]
        block = ctx.enter_context(nc.Block())

        @block.sync
        def _(sp):
            sp.dma_start(w3[:, :, :], w3T).then_inc(cin, 16)
            sp.dma_start(bi3[:, :], bias3.rearrange("(o n) -> o n", o=1).broadcast_to([P, D])).then_inc(cin, 16)

            def load(b):
                wait(sp, sg_ok, b - 1)
                sp.dma_start(mk[b % 2][:, :, :], mask[b].rearrange("(c p) o -> p c o", p=P)).then_inc(m_in[b % 2], 16)

            load(0)
            load(1)
            for b in range(B):
                if b + 2 < B:
                    load(b + 2)
                sp.wait_ge(y_out, b + 1)
                sp.dma_start(out[b], yo[b % 2][:, :]).then_inc(stored[b % 2], 16)
            for p in range(2):
                sp.wait_ge(stored[p], 16 * B // 2)

        @block.scalar
        def _(act):
            A = nc.scalar

            def copy_row(b):
                wait(act, t_done, b - 1)
                A.copy(row[b % 2][:, :], acc[:, b, :]).then_inc(row_ok, 1)

            def signs(b):
                act.wait_ge(m_in[b % 2], 16 * (b // 2 + 1))
                wait(act, wc_ok, b)
                A.activation(sg[:, :, :], mk[b % 2][:, :, :], ACT.Identity, bias=cfs[:, 2, b:b + 1],
                             scale=cfs[:, 1, b:b + 1]).then_inc(sg_ok, 1)

            copy_row(0)
            signs(0)
            for b in range(B):
                act.wait_ge(wc_ok, b + 1)
                wait(act, y_done, b - 1)
                A.copy(wcH[b % 2][:, :, :], wc[:, :, :]).then_inc(wc_hi, 1)
                act.wait_ge(t_done, b + 1)
                A.copy(tH[b % 2][:, :], pT[b % 2][:, :]).then_inc(t_hi, 1)
                if b + 1 < B:
                    copy_row(b + 1)
                    signs(b + 1)

        @block.gpsimd
        def _(pool):
            pool.wait_ge(cin, 32)
            for b in range(B):
                wait(pool, y_out, b - 1)
                nc.gpsimd.tensor_tensor(rb[b % 2][:, :], acc[:, b, :], bi3[:, :], ALU.add).then_inc(rb_ok, 1)
                pool.wait_ge(wc_hi, b + 1)
                nc.gpsimd.tensor_tensor(wcL[b % 2][:, 0, :], wc[:, 0, :], wcH[b % 2][:, 0, :].bitcast(FP32),
                                        ALU.subtract).then_inc(wc_lo, 1)

        @block.vector
        def _(dve):
            V = nc.vector

            def finish(b):
                dve.wait_ge(y_done, b + 1)
                dve.wait_ge(rb_ok, b + 1)
                wait(dve, stored[b % 2], 16 * (b // 2))
                nc.vector.tensor_tensor(yo[b % 2][:, :], pO[b % 2][:, :], rb[b % 2][:, :], ALU.add).then_inc(y_out, 1)

            dve.wait_ge(cin, 32)
            for b in range(B):
                dve.wait_ge(sg_ok, b + 1)
                wait(dve, wc_lo, 2 * b)
                V.tensor_tensor(wc[:, :, :], sg[:, :, :], w3[:, :, :], ALU.add).then_inc(wc_ok, 1)
                dve.wait_ge(wc_hi, b + 1)
                V.tensor_tensor(wcL[b % 2][:, 1:C, :], wc[:, 1:C, :], wcH[b % 2][:, 1:C, :].bitcast(FP32),
                                ALU.subtract).then_inc(wc_lo, 1)
                dve.wait_ge(t_hi, b + 1)
                V.tensor_tensor(tL[b % 2][:, :], pT[b % 2][:, :], tH[b % 2][:, :].bitcast(FP32), ALU.subtract
                                ).then_inc(t_lo, 1)
                if b >= 1:
                    finish(b - 1)
            finish(B - 1)

        @block.tensor
        def _(pe):
            def turn(b):
                pe.wait_ge(row_ok, b + 1)
                wait(pe, t_lo, b - 1)
                for i in range(C):
                    last = nc.tensor.transpose(pT[b % 2][:, i * P:(i + 1) * P], row[b % 2][:, i * P:(i + 1) * P],
                                               ident[:, :])
                last.then_inc(t_done, 1)

            turn(0)
            for b in range(B):
                if b + 1 < B:
                    turn(b + 1)
                pe.wait_ge(t_lo, b + 1)
                pe.wait_ge(wc_lo, 2 * (b + 1))
                wait(pe, y_out, b - 1)
                passes(nc, pO[b % 2][:, :], [(tH[b % 2][:, i * P:(i + 1) * P], tL[b % 2][:, i * P:(i + 1) * P],
                                              wcH[b % 2][:, i, :], wcL[b % 2][:, i, :]) for i in range(C)]
                       ).then_inc(y_done, 1)


def program(nc, x, xT, seqlens, adapter, table, coeff, mask, codebook, w0, scale_log, loraA, loraBT,
            w1T, bias1, a1T, b1, scaling, wall, wqn, wkn, kv_cache, w3T, bias3, invf, out):
    outer = ExitStack()
    names = [0]

    def sbuf(ctx, name, shape, dt=FP32):
        return ctx.enter_context(nc.sbuf_tensor(name, shape, dt))

    def psum(ctx, name, shape, dt=FP32):
        return ctx.enter_context(nc.psum_tensor(name, shape, dt))

    def semaphore(ctx, name):
        return ctx.enter_context(nc.semaphore(name))

    def counted(ctx, *all_names):
        return [semaphore(ctx, n) for n in all_names]

    class Chain:

        def __init__(self, engine, sem):
            self.engine, self.sem, self.n = engine, sem, 0

        def __call__(self, instruction):
            self.n += 1
            instruction.then_inc(self.sem, 1)
            self.engine.wait_ge(self.sem, self.n)

    def mm(o, l, r, start, stop):
        return nc.tensor.matmul(o, l, r, start=start, stop=stop)

    def product(o, terms):
        n = len(terms)
        for i, (lh, ll, rh, rl) in enumerate(terms):
            mm(o, lh, rh, i == 0, False)
            mm(o, ll, rh, False, False)
            last = mm(o, lh, rl, False, i == n - 1)
        return last

    with outer:
        acc = sbuf(outer, "acc", [P, B, D])
        xTH = sbuf(outer, "xTH", [P, C, B * P], F32R)
        xTL = sbuf(outer, "xTL", [P, C, B * P])
        xTs = xTH[:, :, :].bitcast(FP32)
        qA = sbuf(outer, "qA", [P, B, P])
        qB = sbuf(outer, "qB", [P, B, P])
        kA = sbuf(outer, "kA", [P, B, P])
        kB = sbuf(outer, "kB", [P, B, P])
        ident = sbuf(outer, "ident", [P, P])
        key_no = sbuf(outer, "key_no", [P, 2, HALF])
        late_from = sbuf(outer, "late_from", [P, B])
        pages = sbuf(outer, "pages", [1, B * NPAGE], I32)
        cfs = sbuf(outer, "cfs", [P, 3, B])
        weights = ExitStack()
        wH = sbuf(weights, "wH", [P, 2 * REGION], F32R)
        wL = sbuf(weights, "wL", [P, 2 * REGION], F32R)
        wr0 = sbuf(weights, "wr0", [P, CHUNK])

        prep = ExitStack()
        with prep:
            c1 = prep
            w0TH = sbuf(c1, "w0TH", [P, C, D], F32R)
            w0TL = sbuf(c1, "w0TL", [P, C, D], F32R)
            sel = sbuf(c1, "sel", [P, B])
            setup = ExitStack()
            with setup:
                c = setup
                W = sbuf(c, "W", [P, C, D])
                NR = sbuf(c, "NR", [P, C, D])
                QA = sbuf(c, "QA", [P, C, D])
                DL, QB = (xTL[:, :, i * D:(i + 1) * D] for i in range(2))
                seqf = sbuf(c, "seqf", [P, B])
                GT = sbuf(c, "GT", [P, C, D], I32)
                lA = sbuf(c, "lA", [64, D])
                lB = sbuf(c, "lB", [64, D])
                sl = sbuf(c, "sl", [P, C, C])
                ex = sbuf(c, "ex", [P, 6, C * C])
                exi = sbuf(c, "exi", [P, C * C], I32)
                cb = sbuf(c, "cb", [P, 8])
                cbt = sbuf(c, "cbt", [P, 6, 8])
                seqi = sbuf(c, "seqi", [P, B], I32)
                toki = sbuf(c, "toki", [P, 1], I32)
                rowi = sbuf(c, "rowi", [P, 2], I32)
                rowf = sbuf(c, "rowf", [P, 2])
                adi = sbuf(c, "adi", [P, B], I32)
                adf = sbuf(c, "adf", [P, 3, B])
                scl = sbuf(c, "scl", [P, 1])
                pos = sbuf(c, "pos", [P, B])
                tokf = sbuf(c, "tokf", [P, 1])
                keyi = sbuf(c, "keyi", [P, CACHE], I32)
                pgf = sbuf(c, "pgf", [1, 2, B * NPAGE])
                invs = sbuf(c, "invs", [P, 64])
                nwq = sbuf(c, "nwq", [P, P])
                nwk = sbuf(c, "nwk", [P, P])
                nn = sbuf(c, "nn", [P, 2, 64])
                fr = sbuf(c, "fr", [P, B, 64])
                kk = sbuf(c, "kk", [P, B, 64])
                ra = sbuf(c, "ra", [P, B, 64])
                sn = sbuf(c, "sn", [P, B, 64])
                cs = sbuf(c, "cs", [P, B, 64])
                pD = [psum(c, f"pD{i}", [P, D]) for i in range(4)]
                (in_w, in_lora, in_x, in_small, in_idx, iota_ok, ident_ok, delta_ok, dv, pl, ac, sin_ready, cos_ready, sc_ok,
                 tabs, seq_ok, w_tr, w_hi, w_lo, w_eff, trig_in) = counted(
                    c, "in_w", "in_lora", "in_x", "in_small", "in_idx", "iota_ok", "ident_ok", "delta_ok", "dv", "pl", "ac",
                    "sin_ready", "cos_ready", "sc_ok", "tabs", "seq_ok", "w_tr", "w_hi", "w_lo", "w_eff", "trig_in")
                block = c.enter_context(nc.Block())

                def row(ap, n):
                    return ap.rearrange("(o n) -> o n", o=1).broadcast_to([P, n])

                @block.sync
                def _(sp):
                    sp.dma_start(lA[:, :], loraA).then_inc(in_lora, 16)
                    sp.dma_start(lB[:, :], loraBT).then_inc(in_lora, 16)
                    sp.dma_start(W[:, :, :], w0.rearrange("(t p) i -> p t i", p=P)).then_inc(in_w, 16)
                    sp.dma_start(sl[:, :, :], scale_log.rearrange("(t p) g o -> p t (g o)", p=P)).then_inc(in_w, 16)
                    sp.dma_start(cb[:, :], row(codebook, 8)).then_inc(in_w, 16)
                    sp.dma_start(seqi[:, :], row(seqlens, B)).then_inc(in_idx, 16)
                    sp.dma_start(adi[:, :], row(adapter, B)).then_inc(in_idx, 16)
                    sp.dma_start(invs[:, :], row(invf, 64)).then_inc(in_idx, 16)
                    sp.dma_start(nwq[:, :], row(wqn, P)).then_inc(in_idx, 16)
                    sp.dma_start(nwk[:, :], row(wkn, P)).then_inc(in_idx, 16)
                    sp.dma_start(cfs[:, 0, :], row(coeff, B)).then_inc(in_idx, 16)
                    sp.dma_start(pages[:, :], table.rearrange("(o b) n -> o (b n)", o=1)).then_inc(in_idx, 16)
                    for a in range(ADAPTERS):
                        sp.dma_start(scl[a * RANK:(a + 1) * RANK, :],
                                     scaling[a:a + 1].rearrange("(o n) -> o n", o=1).broadcast_to([RANK, 1])
                                     ).then_inc(in_idx, 16)
                    sp.dma_start(acc[:, :, :], x.rearrange("b s d -> s b d")).then_inc(in_x, 16)
                    sp.dma_start(xTs[:, :, :], xT).then_inc(in_x, 16)
                    sp.wait_ge(in_x, 32)

                IDX = 16 * (7 + ADAPTERS)

                @block.gpsimd
                def _(pool):
                    do = Chain(pool, pl)
                    do(nc.gpsimd.memset(ident[:, :], 0.0))
                    nc.gpsimd.affine_select(out=ident[:, :], in_=ident[:, :], compare_op=ALU.not_equal, fill=1.0,
                                            base=0, pattern=[[-1, P]], channel_multiplier=1).then_inc(ident_ok, 1)
                    nc.gpsimd.iota(toki[:, :], pattern=[[0, 1]], base=0, channel_multiplier=1).then_inc(iota_ok, 1)
                    nc.gpsimd.iota(keyi[:, :], pattern=[[1, CACHE]], base=0, channel_multiplier=0).then_inc(iota_ok, 1)

                @block.scalar
                def _(act):
                    act.wait_ge(trig_in, 1)
                    nc.scalar.activation(sn[:, :, :], ra[:, :, :], ACT.Sin).then_inc(sin_ready, 1)
                    act.wait_ge(trig_in, 2)
                    nc.scalar.activation(cs[:, :, :], ra[:, :, :], ACT.Sin).then_inc(cos_ready, 1)
                    for i in range(C):
                        act.wait_ge(w_tr, i + 1)
                        nc.scalar.copy(w0TH[:, i, :], pD[i][:, :]).then_inc(w_hi, 1)

                @block.tensor
                def _(pe):
                    pe.wait_ge(in_lora, 32)
                    for i in range(C):
                        mm(pD[i][:, :], lB[:, i * P:(i + 1) * P], lA[:, :], True, True).then_inc(delta_ok, 1)
                    pe.wait_ge(w_eff, 1)
                    pe.wait_ge(ident_ok, 1)
                    for i in range(C):
                        for t in range(C):
                            last = nc.tensor.transpose(pD[i][:, t * P:(t + 1) * P], W[:, t, i * P:(i + 1) * P],
                                                       ident[:, :])
                        last.then_inc(w_tr, 1)

                @block.vector
                def _(dve):
                    do = Chain(dve, dv)
                    V = nc.vector
                    dve.wait_ge(in_idx, IDX)
                    dve.wait_ge(iota_ok, 2)
                    do(V.tensor_copy(seqf[:, :], seqi[:, :]))
                    do(V.tensor_copy(tokf[:, :], toki[:, :]))
                    k_flat = key_no[:, :, :].rearrange("p a k -> p (a k)")
                    do(V.memset(k_flat[:, CACHE:KEYS], -2.0 ** 32))
                    do(V.tensor_copy(k_flat[:, 0:CACHE], keyi[:, :]))
                    do(V.tensor_scalar(late_from[:, :], seqf[:, :], -HUGE, 0.5 * HUGE, ALU.mult, ALU.add))
                    do(V.tensor_scalar(pos[:, :], seqf[:, :], tokf[:, 0:1], None, ALU.add))
                    do(V.tensor_scalar(cfs[:, 1, :], cfs[:, 0, :], 2.0, None, ALU.mult))
                    do(V.tensor_scalar(cfs[:, 2, :], cfs[:, 0, :], -1.0, None, ALU.mult))
                    do(V.tensor_scalar(pgf[:, 0, :], pages[:, :], 0.0, float(PAGES), ALU.is_lt, ALU.mult))
                    do(V.tensor_tensor(pgf[:, 1, :], pgf[:, 0, :], pages[:, :], ALU.add))
                    do(V.tensor_scalar(pages[:, :], pgf[:, 1, :], 0.0, float(PAGES - 1), ALU.max, ALU.min))
                    do(V.tensor_scalar(rowi[:, 0:1], toki[:, :], 4, None, ALU.arith_shift_right))
                    do(V.tensor_copy(rowf[:, 0:1], rowi[:, 0:1]))
                    do(V.tensor_scalar(adf[:, 0, :], adi[:, :], 0.0, float(ADAPTERS), ALU.is_lt, ALU.mult))
                    do(V.tensor_tensor(adf[:, 1, :], adf[:, 0, :], adi[:, :], ALU.add))
                    do(V.tensor_scalar(adf[:, 2, :], adf[:, 1, :], 0.0, float(ADAPTERS - 1), ALU.max, ALU.min))
                    do(V.tensor_scalar(sel[:, :], adf[:, 2, :], rowf[:, 0:1], scl[:, 0:1], ALU.is_equal, ALU.mult))
                    do(V.tensor_tensor(fr[:, :, :], invs[:, :].rearrange("p (o f) -> p o f", o=1).broadcast_to([P, B, 64]),
                                       pos[:, :].rearrange("p (b o) -> p b o", o=1).broadcast_to([P, B, 64]), ALU.mult))
                    for turn, shift in ((0.0, 0.0), (0.25, float(np.float32(np.pi / 2)))):
                        do(V.tensor_scalar(kk[:, :, :], fr[:, :, :], float(1.0 / TWO_PI), turn, ALU.mult, ALU.add))
                        do(V.tensor_scalar(kk[:, :, :], kk[:, :, :], MAGIC, None, ALU.add))
                        do(V.tensor_scalar(kk[:, :, :], kk[:, :, :], MAGIC, None, ALU.subtract))
                        if turn:
                            dve.wait_ge(sin_ready, 1)
                        do(V.scalar_tensor_tensor(ra[:, :, :], kk[:, :, :], -PI_A, fr[:, :, :], ALU.mult, ALU.add))
                        do(V.scalar_tensor_tensor(ra[:, :, :], kk[:, :, :], -PI_B, ra[:, :, :], ALU.mult, ALU.add))
                        do(V.scalar_tensor_tensor(ra[:, :, :], kk[:, :, :], -PI_C, ra[:, :, :], ALU.mult, ALU.add))
                        if turn:
                            do(V.tensor_scalar(ra[:, :, :], ra[:, :, :], shift, None, ALU.add))
                        V.tensor_scalar(ra[:, :, :], ra[:, :, :], BELOW_PI, -BELOW_PI, ALU.min, ALU.max
                                        ).then_inc(trig_in, 1)
                    dve.wait_ge(in_w, 48)
                    do(V.tensor_reduce(cbt[:, 0, 0:1], cb[:, :], AX.X, ALU.max, apply_absolute_value=True))
                    do(V.tensor_scalar(cbt[:, 0, 0:1], cbt[:, 0, 0:1], 1e-8, None, ALU.max))
                    do(V.reciprocal(cbt[:, 0, 1:2], cbt[:, 0, 0:1]))
                    do(V.tensor_scalar(cbt[:, 1, :], cb[:, :], cbt[:, 0, 1:2], None, ALU.mult))
                    do(V.tensor_tensor(cbt[:, 2, 0:7], cbt[:, 1, 0:7], cbt[:, 1, 1:8], ALU.add))
                    do(V.tensor_scalar(cbt[:, 2, 0:7], cbt[:, 2, 0:7], 0.5, None, ALU.mult))
                    do(V.tensor_tensor(cbt[:, 3, 0:7], cbt[:, 1, 1:8], cbt[:, 1, 0:7], ALU.subtract))
                    s_in = sl[:, :, :].rearrange("p t g -> p (t g)")
                    S, K, F, Y, Z, IV = (ex[:, i, :] for i in range(6))
                    do(V.tensor_scalar(S, s_in, 88.0, -87.0, ALU.min, ALU.max))
                    do(V.tensor_scalar(K, S, float(np.log2(np.e)), None, ALU.mult))
                    do(V.tensor_scalar(K, K, MAGIC, None, ALU.add))
                    do(V.tensor_scalar(K, K, MAGIC, None, ALU.subtract))
                    do(V.scalar_tensor_tensor(F, K, -LN2_A, S, ALU.mult, ALU.add))
                    do(V.scalar_tensor_tensor(F, K, -LN2_B, F, ALU.mult, ALU.add))
                    do(V.tensor_scalar(Y, F, 1.0 / 5040.0, None, ALU.mult))
                    for cf in (720.0, 120.0, 24.0, 6.0, 2.0, 1.0):
                        do(V.scalar_tensor_tensor(Y, Y, 1.0 / cf, F, ALU.add, ALU.mult))
                    do(V.tensor_scalar(Y, Y, 1.0, None, ALU.add))
                    do(V.tensor_scalar(exi[:, :], K, 127.0, None, ALU.add))
                    do(V.tensor_scalar(exi[:, :], exi[:, :], 23, None, ALU.logical_shift_left))
                    do(V.tensor_tensor(Z, Y, exi[:, :].bitcast(FP32), ALU.mult))
                    do(V.reciprocal(IV, Z))
                    dve.wait_ge(delta_ok, C)
                    for t in range(C):
                        do(V.tensor_scalar(DL[:, t, :], pD[t][:, :], LORA_SCALE, None, ALU.mult))
                    do(V.tensor_tensor(W[:, :, :], W[:, :, :], DL[:, :, :], ALU.add))
                    wide = [P, C * C, P]
                    g3 = "p t (g i) -> p (t g) i"
                    inv_b = IV.rearrange("p (n o) -> p n o", o=1).broadcast_to(wide)
                    sc_b = Z.rearrange("p (n o) -> p n o", o=1).broadcast_to(wide)
                    do(V.tensor_tensor(NR[:, :, :].rearrange(g3, g=C), W[:, :, :].rearrange(g3, g=C), inv_b, ALU.mult))

                    def leaf(o, i):
                        do(V.tensor_scalar(o[:, :, :], NR[:, :, :], cbt[:, 2, i:i + 1], cbt[:, 3, i:i + 1],
                                           ALU.is_gt, ALU.mult))
                        do(V.tensor_scalar(o[:, :, :], o[:, :, :], cbt[:, 1, i:i + 1], None, ALU.add))

                    def above(i):
                        do(V.tensor_scalar(GT[:, :, :], NR[:, :, :], cbt[:, 2, i:i + 1], None, ALU.is_gt))

                    leaf(QA, 0)
                    leaf(QB, 2)
                    above(1)
                    do(V.copy_predicated(QA[:, :, :], GT[:, :, :], QB[:, :, :]))
                    leaf(QB, 4)
                    leaf(W, 6)
                    above(5)
                    do(V.copy_predicated(QB[:, :, :], GT[:, :, :], W[:, :, :]))
                    above(3)
                    do(V.copy_predicated(QA[:, :, :], GT[:, :, :], QB[:, :, :]))
                    do(V.tensor_tensor(QA[:, :, :], QA[:, :, :], NR[:, :, :], ALU.subtract))
                    do(V.tensor_tensor(QA[:, :, :], QA[:, :, :], NR[:, :, :], ALU.add))
                    do(V.tensor_tensor(QA[:, :, :].rearrange(g3, g=C), QA[:, :, :].rearrange(g3, g=C), sc_b, ALU.mult))
                    V.tensor_tensor(W[:, :, :], QA[:, :, :], DL[:, :, :], ALU.add).then_inc(w_eff, 1)
                    dve.wait_ge(cos_ready, 1)
                    do(V.tensor_scalar(nn[:, 0, :], nwq[:, 64:P], -1.0, None, ALU.mult))
                    do(V.tensor_scalar(nn[:, 1, :], nwk[:, 64:P], -1.0, None, ALU.mult))
                    for A_t, B_t, nw, neg in ((qA, qB, nwq, nn[:, 0, :]), (kA, kB, nwk, nn[:, 1, :])):
                        for o, trig, w in ((A_t[:, :, 0:64], cs, nw[:, 0:64]), (A_t[:, :, 64:P], cs, nw[:, 64:P]),
                                           (B_t[:, :, 0:64], sn, neg), (B_t[:, :, 64:P], sn, nw[:, 0:64])):
                            do(V.tensor_tensor(o, trig[:, :, :],
                                               w.rearrange("p (o f) -> p o f", o=1).broadcast_to([P, B, 64]), ALU.mult))
                    for i in range(C):
                        dve.wait_ge(w_hi, i + 1)
                        V.tensor_tensor(w0TL[:, i, :], pD[i][:, :], w0TH[:, i, :].bitcast(FP32), ALU.subtract
                                        ).then_inc(w_lo, 1)

            dense = ExitStack()
            with dense:
                c = dense
                w1r = sbuf(c, "w1r", [P, C, D])
                a1r = sbuf(c, "a1r", [P, C, P])
                b1r = sbuf(c, "b1r", [P, D])
                bi1 = sbuf(c, "bi1", [P, D])
                w1H = sbuf(c, "w1H", [P, C, D], F32R)
                w1L = sbuf(c, "w1L", [P, C, D], F32R)
                a1H = sbuf(c, "a1H", [P, C, P], F32R)
                a1L = sbuf(c, "a1L", [P, C, P], F32R)
                b1H = sbuf(c, "b1H", [P, D], F32R)
                b1L = sbuf(c, "b1L", [P, D], F32R)
                wr = [wr0, sbuf(c, "wr1", [P, CHUNK])]
                xsH = [sbuf(c, f"xsH{i}", [P, C, P], F32R) for i in range(2)]
                xsL = [sbuf(c, f"xsL{i}", [P, C, P], F32R) for i in range(2)]
                lo_f = sbuf(c, "lo_f", [P, P])
                loH = sbuf(c, "loH", [P, P], F32R)
                loL = sbuf(c, "loL", [P, P], F32R)
                ys = [sbuf(c, f"ys{i}", [P, D]) for i in range(2)]
                yn = sbuf(c, "yn", [P, D])
                pY = [psum(c, f"pY{i}", [P, D]) for i in range(2)]
                pX = [psum(c, f"pX{i}", [P, D]) for i in range(2)]
                pL = psum(c, "pL", [P, P])
                (w1_in, w1_hi, w1_lo, xs_hi, xs_lo, low_done, low_f, low_hi, low_lo, y_done, y_out, y_mid, acc_in,
                 t_done, t_out, t_low, c_in0, c_in1, c_hi, c_lo, act_passed) = counted(
                    c, "w1_in", "w1_hi", "w1_lo", "xs_hi", "xs_lo", "low_done", "low_f", "low_hi", "low_lo", "y_done",
                    "y_out", "y_mid", "acc_in", "t_done", "t_out", "t_low", "c_in0", "c_in1", "c_hi", "c_lo", "act_passed")
                c_in = [c_in0, c_in1]
                block = c.enter_context(nc.Block())

                def rows(engine, body, first, last):
                    while first % 2:
                        body(first, first % B, first % 2)
                        first += 1
                    end = last + 1 - (last + 1 - first) % 2
                    with engine.Fori(0, (end - first) // 2) as i:
                        for p in range(2):
                            body(i * 2 + (first + p), i * 2 + (first + p) % B, p)
                    for n in range(end, last + 1):
                        body(n, n % B, n % 2)

                @block.sync
                def _(sp):
                    sp.dma_start(w1r[:, :, :], w1T).then_inc(w1_in, 16)
                    sp.dma_start(a1r[:, :, :], a1T).then_inc(w1_in, 16)
                    sp.dma_start(b1r[:, :], b1).then_inc(w1_in, 16)
                    sp.dma_start(bi1[:, :], bias1.rearrange("(o n) -> o n", o=1).broadcast_to([P, D])
                                 ).then_inc(w1_in, 16)
                    for m in range(LEAD):
                        wait(sp, c_lo, m - 1)
                        sp.dma_start(wr[m % 2][:, :], wall[m]).then_inc(c_in[m % 2], 16)
                    sp.wait_ge(w1_in, 64)

                @block.gpsimd
                def _(pool):
                    pool.wait_ge(w1_in, 64)
                    nc.gpsimd.tensor_copy(w1H[:, :, :], w1r[:, :, :]).then_inc(w1_hi, 1)
                    nc.gpsimd.tensor_copy(a1H[:, :, :], a1r[:, :, :]).then_inc(w1_hi, 1)
                    nc.gpsimd.tensor_copy(b1H[:, :], b1r[:, :]).then_inc(w1_hi, 1)
                    pool.wait_ge(w1_hi, 3)
                    nc.gpsimd.tensor_tensor(w1L[:, :, :], w1r[:, :, :], w1H[:, :, :].bitcast(FP32), ALU.subtract
                                            ).then_inc(w1_lo, 1)
                    nc.gpsimd.tensor_tensor(a1L[:, :, :], a1r[:, :, :], a1H[:, :, :].bitcast(FP32), ALU.subtract
                                            ).then_inc(w1_lo, 1)
                    nc.gpsimd.tensor_tensor(b1L[:, :], b1r[:, :], b1H[:, :].bitcast(FP32), ALU.subtract
                                            ).then_inc(w1_lo, 1)
                    for m in range(LEAD):
                        at = slice(m * CHUNK, (m + 1) * CHUNK)
                        pool.wait_ge(c_in[m % 2], 16 * (m // 2 + 1))
                        nc.gpsimd.tensor_copy(wH[:, at], wr[m % 2][:, :]).then_inc(c_hi, 1)
                        pool.wait_ge(c_hi, m + 1)
                        nc.gpsimd.tensor_tensor(wL[:, at], wr[m % 2][:, :], wH[:, at].bitcast(FP32), ALU.subtract
                                                ).then_inc(c_lo, 1)

                @block.scalar
                def _(act):
                    def hold(sem, value):
                        if isinstance(value, int) and value <= 0:
                            return
                        act.wait_ge(sem, value)
                        if not isinstance(value, int):
                            act.sem_inc(act_passed, 1)

                    def split_row(n, b, p):
                        hold(y_done, n - 1)
                        if not isinstance(n, int) or n >= B:
                            hold(t_out, n - (B - 1))
                        nc.scalar.copy(xsH[p][:, :, :], xTs[:, :, bass.ds(b * P, P)]).then_inc(xs_hi, 1)

                    def finish_row(n, b, p, layer):
                        hold(y_out, n + 1)
                        nc.scalar.copy(acc[:, bass.ds(b, 1), :].rearrange("p o n -> p (o n)"), ys[p][:, :]
                                       ).then_inc(acc_in, 1)
                        hold(t_done, n + 1)
                        to = xTs if layer == 0 else xTH
                        nc.scalar.copy(to[:, :, bass.ds(b * P, P)], pX[p][:, :].rearrange("p (c t) -> p c t", c=C)
                                       ).then_inc(t_out, 1)

                    split_row(0, 0, 0)
                    split_row(1, 1, 1)
                    for n in (0, 1):
                        finish_row(n, n, n, 0)
                        split_row(n + 2, n + 2, n)

                    def body0(n, b, p):
                        finish_row(n, b, p, 0)
                        hold(y_done, n + 1)
                        nc.scalar.copy(xsH[p][:, :, :], xTs[:, :, bass.ds((b + 2) * P, P)]).then_inc(xs_hi, 1)
                    rows(act, body0, 2, 5)
                    for n in (6, 7):
                        finish_row(n, n, n % 2, 0)
                        split_row(n + 2, n + 2 - B, n % 2)

                    def body1(n, b, p):
                        finish_row(n, b, p, 1)
                        hold(y_done, n + 1)
                        hold(t_out, n - 5)
                        nc.scalar.copy(xsH[p][:, :, :], xTs[:, :, bass.ds((b + 2) * P, P)]).then_inc(xs_hi, 1)
                    rows(act, body1, 8, 13)
                    for n in (14, 15):
                        finish_row(n, n - B, n % 2, 1)

                @block.vector
                def _(dve):
                    V = nc.vector

                    def low_part(n, b, p):
                        dve.wait_ge(xs_hi, n + 1)
                        V.tensor_tensor(xsL[p][:, :, :], xTs[:, :, bass.ds(b * P, P)], xsH[p][:, :, :].bitcast(FP32),
                                        ALU.subtract).then_inc(xs_lo, 1)

                    def adapter_part(n, b, p):
                        k = n - B
                        dve.wait_ge(low_done, k + 1)
                        V.tensor_scalar(lo_f[:, :], pL[:, :], sel[:, bass.ds(b, 1)], None, ALU.mult).then_inc(low_f, 1)
                        dve.wait_ge(low_f, k + 1)
                        if not isinstance(n, int) or k >= 1:
                            dve.wait_ge(y_done, n)
                        V.tensor_copy(loH[:, :], lo_f[:, :]).then_inc(low_hi, 1)
                        dve.wait_ge(low_hi, k + 1)
                        V.tensor_tensor(loL[:, :], lo_f[:, :], loH[:, :].bitcast(FP32), ALU.subtract
                                        ).then_inc(low_lo, 1)

                    def sum_row(n, b, p, layer):
                        a = acc[:, bass.ds(b, 1), :].rearrange("p o n -> p (o n)")
                        dve.wait_ge(y_done, n + 1)
                        wait(dve, t_done, n - 1)
                        wait(dve, acc_in, n - 1)
                        if layer == 0:
                            V.tensor_tensor(ys[p][:, :], pY[p][:, :], a, ALU.add).then_inc(y_out, 1)
                        else:
                            V.tensor_tensor(yn[:, :], pY[p][:, :], a, ALU.add).then_inc(y_mid, 1)
                            dve.wait_ge(y_mid, n - B + 1)
                            V.tensor_tensor(ys[p][:, :], yn[:, :], bi1[:, :], ALU.add).then_inc(y_out, 1)

                    def turned_low(n, b, p):
                        dve.wait_ge(t_out, n + 1)
                        cols = bass.ds(b * P, P)
                        V.tensor_tensor(xTL[:, :, cols], pX[p][:, :].rearrange("p (c t) -> p c t", c=C),
                                        xTH[:, :, cols].bitcast(FP32), ALU.subtract).then_inc(t_low, 1)

                    low_part(0, 0, 0)
                    low_part(1, 1, 1)
                    for n in (0, 1):
                        sum_row(n, n, n, 0)
                        low_part(n + 2, n + 2, n)

                    def body0(n, b, p):
                        sum_row(n, b, p, 0)
                        low_part(n + 2, b + 2, p)
                    rows(dve, body0, 2, 5)
                    sum_row(6, 6, 0, 0)
                    low_part(8, 0, 0)
                    sum_row(7, 7, 1, 0)
                    adapter_part(8, 0, 0)
                    low_part(9, 1, 1)
                    sum_row(8, 0, 0, 1)
                    adapter_part(9, 1, 1)
                    low_part(10, 2, 0)

                    def body1(n, b, p):
                        sum_row(n, b, p, 1)
                        turned_low(n - 1, b - 1, 1 - p)
                        adapter_part(n + 1, b + 1, 1 - p)
                        low_part(n + 2, b + 2, p)
                    rows(dve, body1, 9, 13)
                    sum_row(14, 6, 0, 1)
                    turned_low(13, 5, 1)
                    adapter_part(15, 7, 1)
                    sum_row(15, 7, 1, 1)
                    turned_low(14, 6, 0)
                    turned_low(15, 7, 1)

                @block.tensor
                def _(pe):
                    def produce(n, b, p, layer):
                        pe.wait_ge(xs_lo, n + 1)
                        wait(pe, y_out, n - 1)
                        if layer == 0:
                            product(pY[p][:, :], [(xsH[p][:, i, :], xsL[p][:, i, :], w0TH[:, i, :], w0TL[:, i, :])
                                                  for i in range(C)]).then_inc(y_done, 1)
                            return
                        k = n - B
                        wait(pe, low_f, k)
                        product(pL[:, :], [(a1H[:, i, :], a1L[:, i, :], xsH[p][:, i, :], xsL[p][:, i, :])
                                           for i in range(C)]).then_inc(low_done, 1)
                        for i in range(C):
                            mm(pY[p][:, :], xsH[p][:, i, :], w1H[:, i, :], i == 0, False)
                            mm(pY[p][:, :], xsL[p][:, i, :], w1H[:, i, :], False, False)
                            mm(pY[p][:, :], xsH[p][:, i, :], w1L[:, i, :], False, False)
                        pe.wait_ge(low_lo, k + 1)
                        mm(pY[p][:, :], loH[:, :], b1H[:, :], False, False)
                        mm(pY[p][:, :], loL[:, :], b1H[:, :], False, False)
                        mm(pY[p][:, :], loH[:, :], b1L[:, :], False, True).then_inc(y_done, 1)

                    def turn(n, b, p, layer):
                        pe.wait_ge(y_out, n + 1)
                        wait(pe, t_out, n - 1)
                        if not isinstance(n, int) and layer == 1 or isinstance(n, int) and n > B + 1:
                            pe.wait_ge(t_low, n - (B + 1))
                        for i in range(C):
                            last = nc.tensor.transpose(pX[p][:, i * P:(i + 1) * P], ys[p][:, i * P:(i + 1) * P],
                                                       ident[:, :])
                        last.then_inc(t_done, 1)

                    produce(0, 0, 0, 0)
                    produce(1, 1, 1, 0)
                    for n in (0, 1):
                        turn(n, n, n, 0)
                        produce(n + 2, n + 2, n, 0)

                    def body0(n, b, p):
                        turn(n, b, p, 0)
                        produce(n + 2, b, p, 0)
                    rows(pe, body0, 2, 5)
                    pe.wait_ge(w1_lo, 3)
                    for n in (6, 7):
                        turn(n, n, n % 2, 0)
                        produce(n + 2, n, n % 2, 1)

                    def body1(n, b, p):
                        turn(n, b, p, 1)
                        produce(n + 2, b, p, 1)
                    body1(8, 0, 0)
                    body1(9, 1, 1)
                    rows(pe, body1, 10, 13)
                    turn(14, 6, 0, 1)
                    turn(15, 7, 1, 1)

        attention(nc, acc, xTH, xTL, qA, qB, kA, kB, ident, key_no, late_from, pages, wH, wL, wr0, wall,
                  kv_cache)
        weights.close()
        last_layer(nc, acc, ident, cfs, mask, w3T, bias3, out)


def kernel(**inputs):
    import numpy as _np
    import concourse.bacc as _bacc
    from concourse import mybir as _mybir
    from concourse.bass_utils import run_bass_kernel_spmd as _run

    given = {k: _np.asarray(v) for k, v in inputs.items()}

    def columns(w):
        return w.T.reshape(C, P, w.shape[0]).transpose(1, 0, 2)

    wq, wk, wv = (columns(given[f"L2_cond_W{n}"]) for n in "qkv")
    wo = given["L2_cond_Wo"].T.reshape(G, R, P, D).transpose(0, 2, 1, 3)
    heads = []
    for g in range(G):
        qkv = _np.concatenate([wq[:, :, g * R * P:(g + 1) * R * P], wk[:, :, g * P:(g + 1) * P],
                               wv[:, :, g * P:(g + 1) * P]], axis=2).reshape(P, C * QKV)
        whole = _np.concatenate([qkv, wo[g].reshape(P, R * D)], axis=1)
        heads.append(whole.reshape(P, CHUNKS, CHUNK).transpose(1, 0, 2))
    inv_freq = (1.0 / _np.float32(10000.0) ** (_np.arange(0, P, 2, dtype=_np.float32) / _np.float32(P))
                ).astype(_np.float32)
    layout = {
        "x": given["x"],
        "xT": given["x"].reshape(B * P, D).T.reshape(C, P, B * P).transpose(1, 0, 2),
        "seqlens": given["itok_B_207_1644"],
        "adapter": given["itok_B_1_7"],
        "table": given["itok_Bx16_0_63"],
        "coeff": given["condB_coeff"],
        "mask": given["mask_Bx4096x4096_ik1"],
        "codebook": given["condB_codebook"],
        "w0": given["L0_cond_weight"],
        "scale_log": given["L0_cond_scale_log"],
        "loraA": given["L0_cond_lora_A"],
        "loraBT": given["L0_cond_lora_B"].T,
        "w1T": columns(given["L1_cond_weight"]),
        "bias1": given["L1_cond_bias"],
        "a1T": columns(given["L1_cond_lora_a_weights"].reshape(P, D)),
        "b1": given["L1_cond_lora_b_weights"].transpose(0, 2, 1).reshape(P, D),
        "scaling": given["L1_cond_scaling_factors"],
        "wall": _np.concatenate(heads, axis=0),
        "wqn": given["L2_cond_q_norm_w"],
        "wkn": given["L2_cond_k_norm_w"],
        "kv_cache": _np.concatenate([given["L2_cond_k_cache"], given["L2_cond_v_cache"]], axis=3).transpose(0, 2, 1, 3),
        "w3T": columns(given["L3_cond_W"]),
        "bias3": given["L3_cond_b"],
        "invf": inv_freq,
    }
    nc = _bacc.Bacc("TRN2", target_bir_lowering=False, num_devices=1, dynamic_dma_scratch_size=1024)
    arrays, args = {}, {}
    for name, a in layout.items():
        a = _np.ascontiguousarray(a)
        arrays[f"in_{name}"] = a
        args[name] = nc.dram_tensor(f"in_{name}", a.shape, _mybir.dt.from_np(a.dtype), kind="ExternalInput").ap()
    args["out"] = nc.dram_tensor("out", (B, P, D), _mybir.dt.from_np(_np.dtype("float32")),
                                 kind="ExternalOutput").ap()
    program(nc, **args)
    r = _run(nc, [arrays], core_ids=[0])
    return r.results[0]["out"]
```

```python
import concourse.bass as bass
from concourse import mybir
from contextlib import ExitStack
import numpy as np

FP32 = mybir.dt.float32
F32R = mybir.dt.float32r
I32 = mybir.dt.int32
U8 = mybir.dt.uint8
ALU = mybir.AluOpType
ACT = mybir.ActivationFunctionType
AX = mybir.AxisListType

P = 128
B = 8
D = 512
C = D // P
G = 8
R = 4
PAGE = 32
NPAGE = 16
PAGES = 64
CACHE = NPAGE * PAGE
KT = CACHE // P
KEYS = CACHE + P
JT = KEYS // P
STEPS = G * B
QKV = R * P + 2 * P
REGION = C * QKV + R * D
CHUNKS = 8
CHUNK = REGION // CHUNKS
LEAD = 9
EPS = 1e-6
RANK = 16
ADAPTERS = 8
LORA_SCALE = 32.0 / 64.0
MAGIC = 1.5 * 2.0 ** 23
TWO_PI = 2.0 * np.pi
PI_A = 6.28125
PI_B = float(np.float32(0.0019350051879882812))
PI_C = float(np.float32(TWO_PI - PI_A - PI_B))
LN2_A = 0.693359375
LN2_B = float(np.float32(np.log(2.0) - LN2_A))
BELOW_PI = 3.1415925
HALF = KEYS // 2
HUGE = 2.0 ** 93
LOWEST = -3.4e38
BANK = [0, 1, 0, 1, 0]


def wait(engine, semaphore, value):
    if isinstance(value, int) and value <= 0:
        return
    engine.wait_ge(semaphore, value)


def matmul(nc, o, l, r, start, stop):
    return nc.tensor.matmul(o, l, r, start=start, stop=stop)


def passes(nc, o, terms, first=True, last=True):
    for i, (lh, ll, rh, rl) in enumerate(terms):
        matmul(nc, o, lh, rh, first and i == 0, False)
        matmul(nc, o, ll, rh, False, False)
        done = matmul(nc, o, lh, rl, False, last and i == len(terms) - 1)
    return done


def attention(nc, acc, xTs, qA, qB, kA, kB, ident, key_no, late_from, pages, wH, wL, wr, wall, kv_cache,
              w3, w3T, w3_in):
    ctx = ExitStack()
    with ctx:
        def sbuf(name, shape, dt=FP32):
            return ctx.enter_context(nc.sbuf_tensor(name, shape, dt))

        def psum(name, shape):
            return ctx.enter_context(nc.psum_tensor(name, shape, FP32))

        def sem(name):
            return ctx.enter_context(nc.semaphore(name))

        xH = [sbuf(f"xH{i}", [P, C, P], F32R) for i in range(2)]
        xL = [sbuf(f"xL{i}", [P, C, P], F32R) for i in range(2)]
        kv_raw = [sbuf(f"kv_raw{i}", [P, KT, 2, P]) for i in range(2)]
        vH = [sbuf(f"vH{i}", [P, JT, P], F32R) for i in range(2)]
        vL = [sbuf(f"vL{i}", [P, JT, P], F32R) for i in range(2)]
        kH = sbuf("kH", [P, KEYS], F32R)
        kL = sbuf("kL", [P, KEYS], F32R)
        qH = sbuf("qH", [P, R * P], F32R)
        qL = sbuf("qL", [P, R * P], F32R)
        q_u = sbuf("q_u", [P, R, P])
        q_w = sbuf("q_w", [P, R, P])
        kv = [sbuf(f"kv{i}", [P, 2, P]) for i in range(2)]
        k_u = sbuf("k_u", [P, P])
        k_w = sbuf("k_w", [P, P])
        k_rot = sbuf("k_rot", [P, P])
        q_sums = sbuf("q_sums", [P, R])
        k_sum = sbuf("k_sum", [P, 1])
        q_mean = sbuf("q_mean", [P, R])
        k_mean = sbuf("k_mean", [P, 1])
        halves = sbuf("halves", [P, R])
        k_inv = sbuf("k_inv", [P, 1])
        q_inv = [sbuf(f"q_inv{i}", [P, R]) for i in range(2)]
        late = [sbuf(f"late{i}", [P, 2, HALF]) for i in range(2)]
        row_max = sbuf("row_max", [P, R])
        bias = [sbuf(f"bias{i}", [P, R]) for i in range(2)]
        prob = [sbuf(f"prob{i}", [P, R, KEYS]) for i in range(2)]
        den = [sbuf(f"den{i}", [P, R]) for i in range(2)]
        den_inv = [sbuf(f"den_inv{i}", [P, R]) for i in range(2)]
        ptH = [sbuf(f"ptH{i}", [P, R * P], F32R) for i in range(2)]
        ptL = [sbuf(f"ptL{i}", [P, R * P], F32R) for i in range(2)]
        oH = sbuf("oH", [P, R * P], F32R)
        oL = sbuf("oL", [P, R * P], F32R)
        table_out = sbuf("table_out", [P, 1])

        scores = [psum(f"scores{i}", [P, 2, 512]) for i in range(2)]
        turned = [psum(f"turned{i}", [P, R * P]) for i in range(2)]
        p_q = psum("p_q", [P, R * P])
        p_o = psum("p_o", [P, R * P])

        kv_done, q_done, scored = sem("kv_done"), sem("q_done"), sem("scored")
        prob_turned, pv_done, out_done = sem("prob_turned"), sem("pv_done"), sem("out_done")
        cache_turned, q_turned, k_turned = sem("cache_turned"), sem("q_turned"), sem("k_turned")
        late_ok, exp_done, pt_hi, kv_copied, k_sq, q_sq = (sem(x) for x in (
            "late_ok", "exp_done", "pt_hi", "kv_copied", "k_sq", "q_sq"))
        o_hi, cache_hi, q_hi, k_hi, table_in, w_hi = (sem(x) for x in (
            "o_hi", "cache_hi", "q_hi", "k_hi", "table_in", "w_hi"))
        x_hi = sem("x_hi")
        x_lo, q_lo0 = sem("x_lo"), sem("q_lo0")
        row_max_ok, bias_ok, pt_lo, inv_ok = (sem(x) for x in ("row_max_ok", "bias_ok", "pt_lo", "inv_ok"))
        o_lo, q_parts, sums_ok, cache_lo, q_lo, k_lo, added = (sem(x) for x in (
            "o_lo", "q_parts", "sums_ok", "cache_lo", "q_lo", "k_lo", "added"))
        v_hi, v_lo, w_lo, normed, k_parts, k_added = (sem(x) for x in (
            "v_hi", "v_lo", "w_lo", "normed", "k_parts", "k_added"))
        k_mean_ok, k_inv_ok, q_mean_ok, q_inv_ok, k_ready, q_ready, const_ok = (sem(x) for x in (
            "k_mean_ok", "k_inv_ok", "q_mean_ok", "q_inv_ok", "k_ready", "q_ready", "const_ok"))
        act_passed, pool_passed, dve_passed = sem("act_passed"), sem("pool_passed"), sem("dve_passed")
        w_in = sem("w_in")
        kv_in = [sem("kv_in0"), sem("kv_in1")]

        def hold(engine, passed, semaphore, value):
            if isinstance(value, int):
                wait(engine, semaphore, value)
                return
            engine.wait_ge(semaphore, value)
            engine.sem_inc(passed, 1)

        def steps(engine, turn):
            turn(-1, 1, False, False, False, True)
            turn(0, 0, False, False, True, True)
            turn(1, 1, False, True, True, True)
            with engine.Fori(1, STEPS // 2 - 1) as i:
                turn(i * 2, 0, True, True, True, True)
                turn(i * 2 + 1, 1, True, True, True, True)
            turn(STEPS - 2, 0, True, True, True, True)
            turn(STEPS - 1, 1, True, True, True, False)
            turn(STEPS, 0, True, True, False, False)
            turn(STEPS + 1, 1, True, False, False, False)

        block = ctx.enter_context(nc.Block())

        @block.sync
        def _(sp):
            heads_of_pages = kv_cache.rearrange("n g s d -> (n g) s d")

            def load_pages(m, p):
                b, g = m % B, m // B
                _, numbers = nc.values_load_multi_w_load_instructions(
                    pages[0:1, bass.ds(b * NPAGE, NPAGE)], engines=(mybir.EngineType.SP,), min_val=0,
                    max_val=PAGES - 1, skip_runtime_bounds_check_because="they were clamped to the cache on the chip")
                wait(sp, cache_turned, m - 1)
                wait(sp, v_lo, m - 1)
                for j in range(NPAGE):
                    rows = slice(PAGE * (j % 4), PAGE * (j % 4 + 1))
                    sp.dma_start(kv_raw[p][rows, j // 4, :, :],
                                 heads_of_pages[bass.ds(numbers[j] * G + g, 1), :, :].rearrange(
                                     "o s (a d) -> (o s) a d", a=2)).then_inc(kv_in[p], 16)

            def load_weights(m):
                wait(sp, w_lo, m - LEAD)
                sp.dma_start(wr[:, :], wall[bass.ds(m % (G * CHUNKS), 1), :, :].rearrange("o p n -> (o p) n")
                             ).then_inc(w_in, 16)

            def turn(n, p):
                load_pages(n + 2, p)
                load_weights(n + LEAD + 1)

            load_weights(LEAD)
            load_pages(0, 0)
            load_pages(1, 1)
            turn(0, 0)
            sp.dma_start(w3[:, :, :], w3T).then_inc(w3_in, 16)
            with sp.Fori(0, (STEPS - 4) // 2) as i:
                turn(i * 2 + 1, 1)
                turn(i * 2 + 2, 0)
            load_pages(STEPS - 1, 1)
            for p in range(2):
                sp.wait_ge(kv_in[p], 16 * NPAGE * STEPS // 2)

        @block.gpsimd
        def _(pool):
            Gp = nc.gpsimd
            Gp.memset(halves[:, :], -0.5).then_inc(const_ok, 1)
            pool.wait_ge(const_ok, 1)

            def rounded(o, full):
                return Gp.tensor_scalar(o, full, 1.0, 1.0, ALU.mult, ALU.mult)

            def turn(n, p, outs, ends, works, begins):
                q = 1 - p
                m = n + 1

                def normalise(h):
                    hold(pool, pool_passed, inv_ok, n * R + h + 1)
                    done = Gp.tensor_scalar(prob[p][:, h, :], prob[p][:, h, :], den_inv[p][:, h:h + 1], 1.0,
                                            ALU.mult, ALU.mult)
                    if h == R - 1:
                        done.then_inc(normed, 1)

                if works:
                    if outs:
                        hold(pool, pool_passed, pv_done, (n - 1) * JT)
                    hold(pool, pool_passed, kv_in[p], 16 * NPAGE * (n // 2 + 1))
                    rounded(vH[p][:, KT, :], kv[p][:, 1, :]).then_inc(v_hi, 1)
                    rounded(vH[p][:, 0:KT, :], kv_raw[p][:, :, 1, :]).then_inc(v_hi, 1)
                    hold(pool, pool_passed, v_hi, (n + 1) * 2)
                    Gp.tensor_tensor(vL[p][:, KT, :], kv[p][:, 1, :], vH[p][:, KT, :].bitcast(FP32), ALU.subtract)
                    Gp.tensor_tensor(vL[p][:, 0:KT, :], kv_raw[p][:, :, 1, :], vH[p][:, 0:KT, :].bitcast(FP32),
                                     ALU.subtract).then_inc(v_lo, 1)
                if begins:
                    row = bass.ds(m % B, 1)
                    a = kA[:, row, :].rearrange("p o d -> p (o d)")
                    b_ = kB[:, row, :].rearrange("p o d -> p (o d)")
                    hold(pool, pool_passed, k_sq, m + 1)
                    Gp.tensor_scalar(k_mean[:, :], k_sum[:, :], 1.0 / P, EPS, ALU.mult, ALU.add).then_inc(k_mean_ok, 1)
                    hold(pool, pool_passed, k_turned, m)
                    Gp.tensor_tensor(k_u[:, :], kv[q][:, 0, :], a, ALU.mult).then_inc(k_parts, 1)
                    Gp.tensor_tensor(k_w[:, 0:64], kv[q][:, 0, 64:P], b_[:, 0:64], ALU.mult).then_inc(k_parts, 1)
                    Gp.tensor_tensor(k_w[:, 64:P], kv[q][:, 0, 0:64], b_[:, 64:P], ALU.mult).then_inc(k_parts, 1)
                    hold(pool, pool_passed, k_mean_ok, m + 1)
                    Gp.tensor_tensor(k_inv[:, :], k_mean[:, :], halves[:, 0:1], ALU.pow).then_inc(k_inv_ok, 1)
                    hold(pool, pool_passed, k_parts, (m + 1) * 3)
                    Gp.tensor_tensor(k_u[:, :], k_u[:, :], k_w[:, :], ALU.add).then_inc(k_added, 1)
                    hold(pool, pool_passed, k_added, m + 1)
                    hold(pool, pool_passed, k_inv_ok, m + 1)
                    Gp.tensor_scalar(k_rot[:, :], k_u[:, :], k_inv[:, 0:1], 1.0, ALU.mult, ALU.mult
                                     ).then_inc(k_ready, 1)
                if works:
                    normalise(0)
                    normalise(1)
                    if not isinstance(n, int) or n < STEPS - 2:
                        at = bass.ds(((n + LEAD) % (2 * CHUNKS)) * CHUNK, CHUNK)
                        hold(pool, pool_passed, w_hi, n + 1)
                        Gp.tensor_tensor(wL[:, at], wr[:, :], wH[:, at].bitcast(FP32), ALU.subtract).then_inc(w_lo, 1)
                    normalise(2)
                if begins:
                    hold(pool, pool_passed, q_parts, m + 1)
                    Gp.tensor_tensor(q_u[:, :, :], q_u[:, :, :], q_w[:, :, :], ALU.add).then_inc(q_ready, 1)
                if works:
                    normalise(3)
                if begins:
                    hold(pool, pool_passed, sums_ok, m + 1)
                    Gp.tensor_scalar(q_mean[:, :], q_sums[:, :], 1.0, P * EPS, ALU.mult, ALU.add).then_inc(q_mean_ok, 1)
                    hold(pool, pool_passed, q_mean_ok, m + 1)
                    Gp.tensor_tensor(q_inv[q][:, :], q_mean[:, :], halves[:, :], ALU.pow).then_inc(q_inv_ok, 1)

            steps(pool, turn)

        @block.scalar
        def _(act):
            A = nc.scalar
            def place_row(m, parity):
                hold(act, act_passed, q_done, m - 1)
                A.copy(xH[parity][:, :, :], xTs[:, :, bass.ds((m % B) * P, P)]).then_inc(x_hi, 1)

            def turn(n, p, outs, ends, works, begins):
                q = 1 - p
                m = n + 1

                def prob_part(s, parity, j):
                    act.wait_ge(prob_turned, s * JT + j + 1)
                    wait(act, pv_done, s * JT + j - 1)
                    A.copy(ptH[(parity + j) % 2][:, :], turned[BANK[j]][:, :]).then_inc(pt_hi, 1)

                def soft(h):
                    act.wait_ge(bias_ok, n * R + h + 1)
                    if h == 0:
                        wait(act, prob_turned, (n - 1) * JT)
                    A.activation(prob[p][:, h, :].rearrange("p (a k) -> p a k", a=2), scores[h % 2][:, :, 0:HALF],
                                 ACT.Exp, bias=bias[p][:, h:h + 1], scale=q_inv[p][:, h:h + 1],
                                 accum_out=den[p][:, h:h + 1]).then_inc(exp_done, 1)

                if begins and (not isinstance(m, int) or m + 1 < STEPS):
                    place_row(m + 1, p)
                if works:
                    soft(0)
                if ends:
                    prob_part(n - 1, q, 0)
                    prob_part(n - 1, q, 1)
                if begins:
                    act.wait_ge(kv_done, m + 1)
                    wait(act, v_lo, m - 1)
                    wait(act, k_added, m)
                    A.copy(kv[q][:, :, :], p_q[:, 0:2 * P].rearrange("p (a d) -> p a d", a=2)).then_inc(kv_copied, 1)
                    wait(act, k_mean_ok, m)
                    act.wait_ge(kv_copied, m + 1)
                    A.activation(k_w[:, :], kv[q][:, 0, :], ACT.Square, accum_out=k_sum[:, :]).then_inc(k_sq, 1)
                if works:
                    soft(1)
                    if not isinstance(n, int) or n < STEPS - 2:
                        at = bass.ds(((n + LEAD) % (2 * CHUNKS)) * CHUNK, CHUNK)
                        hold(act, act_passed, w_in, 16 * (n + 1))
                        A.copy(wH[:, at], wr[:, :]).then_inc(w_hi, 1)
                if begins:
                    hold(act, act_passed, row_max_ok, n * R)
                    A.activation(late[q][:, :, :], key_no[:, :, :], ACT.Relu, bias=late_from[:, bass.ds(m % B, 1)],
                                 scale=HUGE).then_inc(late_ok, 1)
                if works:
                    soft(2)
                if ends:
                    prob_part(n - 1, q, 2)
                if works:
                    soft(3)
                if ends:
                    prob_part(n - 1, q, 3)
                    prob_part(n - 1, q, 4)
                if begins:
                    act.wait_ge(cache_turned, m + 1)
                    wait(act, scored, m * R)
                    A.copy(kH[:, 0:CACHE], scores[0][:, 1, :]).then_inc(cache_hi, 1)
                    act.wait_ge(k_turned, m + 1)
                    A.copy(kH[:, CACHE:KEYS], scores[0][:, 0, 0:P]).then_inc(k_hi, 1)
                    act.wait_ge(q_turned, m + 1)
                    A.copy(qH[:, :], turned[1][:, :]).then_inc(q_hi, 1)
                    act.wait_ge(q_parts, m + 1)
                    A.activation(p_q[:, :], p_q[:, :], ACT.Square).then_inc(q_sq, 1)
                if ends:
                    act.wait_ge(pv_done, n * JT)
                    wait(act, out_done, n - 1)
                    A.copy(oH[:, :], p_o[:, :]).then_inc(o_hi, 1)

            place_row(0, 0)
            A.activation(table_out[:, :], ident[:, 0:1], ACT.Exp).then_inc(table_in, 1)
            steps(act, turn)

        @block.vector
        def _(dve):
            V = nc.vector

            def rest(o, full, high):
                return V.tensor_tensor(o, full, high.bitcast(FP32), ALU.subtract)

            def low_row(m, parity):
                dve.wait_ge(x_hi, m + 1)
                rest(xL[parity][:, :, :], xTs[:, :, bass.ds((m % B) * P, P)], xH[parity][:, :, :]).then_inc(x_lo, 1)

            def turn(n, p, outs, ends, works, begins):
                q = 1 - p
                m = n + 1

                def prob_part(s, parity, j):
                    dve.wait_ge(pt_hi, s * JT + j + 1)
                    t = (parity + j) % 2
                    rest(ptL[t][:, :], turned[BANK[j]][:, :], ptH[t][:, :]
                         ).then_inc(pt_lo, 1)

                def masked_max(h):
                    s = scores[h % 2][:, :, 0:HALF]
                    hold(dve, dve_passed, scored, n * R + h + 1)
                    V.tensor_tensor_reduce(out=s, in0=s, in1=late[p][:, :, :], scale=1.0, scalar=LOWEST,
                                           op0=ALU.subtract, op1=ALU.max, accum_out=row_max[:, h:h + 1]
                                           ).then_inc(row_max_ok, 1)
                    if h == 0:
                        hold(dve, dve_passed, q_inv_ok, n + 1)
                    dve.wait_ge(row_max_ok, n * R + h + 1)
                    V.scalar_tensor_tensor(bias[p][:, h:h + 1], row_max[:, h:h + 1], -1.0, q_inv[p][:, h:h + 1],
                                           ALU.mult, ALU.mult).then_inc(bias_ok, 1)

                def inverse(h):
                    dve.wait_ge(exp_done, n * R + h + 1)
                    V.reciprocal(den_inv[p][:, h:h + 1], den[p][:, h:h + 1]).then_inc(inv_ok, 1)

                if works:
                    hold(dve, dve_passed, late_ok, n + 1)
                    masked_max(0)
                if begins and (not isinstance(m, int) or m + 1 < STEPS):
                    low_row(m + 1, p)
                if ends:
                    prob_part(n - 1, q, 0)
                if works:
                    masked_max(1)
                    inverse(0)
                if outs:
                    a = acc[:, bass.ds((n - 2) % B, 1), :].rearrange("p o d -> p (o d)")
                    dve.wait_ge(out_done, n - 1)
                    V.tensor_tensor(a, p_o[:, :], a, ALU.add).then_inc(added, 1)
                if works:
                    masked_max(2)
                if ends:
                    prob_part(n - 1, q, 1)
                if works:
                    inverse(1)
                if ends:
                    prob_part(n - 1, q, 2)
                if works:
                    inverse(2)
                    masked_max(3)
                if begins:
                    row = bass.ds(m % B, 1)
                    heads = p_q[:, :].rearrange("p (h d) -> p h d", h=R)
                    dve.wait_ge(q_done, m + 1)
                    wait(dve, q_turned, m)
                    V.tensor_tensor(q_w[:, :, 0:64], heads[:, :, 64:P], qB[:, row, 0:64].broadcast_to([P, R, 64]),
                                    ALU.mult)
                    V.tensor_tensor(q_w[:, :, 64:P], heads[:, :, 0:64], qB[:, row, 64:P].broadcast_to([P, R, 64]),
                                    ALU.mult)
                    V.tensor_tensor(q_u[:, :, :], heads, qA[:, row, :].broadcast_to([P, R, P]), ALU.mult
                                    ).then_inc(q_parts, 1)
                if works:
                    inverse(3)
                if ends:
                    prob_part(n - 1, q, 3)
                    prob_part(n - 1, q, 4)
                if begins:
                    dve.wait_ge(cache_hi, m + 1)
                    rest(kL[:, 0:CACHE], scores[0][:, 1, :], kH[:, 0:CACHE]).then_inc(cache_lo, 1)
                    dve.wait_ge(k_hi, m + 1)
                    rest(kL[:, CACHE:KEYS], scores[0][:, 0, 0:P], kH[:, CACHE:KEYS]).then_inc(k_lo, 1)
                    dve.wait_ge(q_hi, m + 1)
                    rest(qL[:, 0:P], turned[1][:, 0:P], qH[:, 0:P]).then_inc(q_lo0, 1)
                    rest(qL[:, P:R * P], turned[1][:, P:R * P], qH[:, P:R * P]).then_inc(q_lo, 1)
                    dve.wait_ge(q_sq, m + 1)
                    wait(dve, q_mean_ok, m)
                    V.tensor_reduce(q_sums[:, :], p_q[:, :].rearrange("p (h d) -> p h d", h=R), AX.X, ALU.add
                                    ).then_inc(sums_ok, 1)
                if ends:
                    dve.wait_ge(o_hi, n)
                    rest(oL[:, :], p_o[:, :], oH[:, :]).then_inc(o_lo, 1)

            low_row(0, 0)
            steps(dve, turn)

        @block.tensor
        def _(pe):
            def turn(n, p, outs, ends, works, begins):
                q = 1 - p
                m = n + 1

                def score(h):
                    if h == 0:
                        pe.wait_ge(q_lo0, n + 1)
                        pe.wait_ge(cache_lo, n + 1)
                        pe.wait_ge(k_lo, n + 1)
                    if h == 1:
                        pe.wait_ge(q_lo, n + 1)
                    if not (isinstance(n, int) and n == 0 and h < 2):
                        pe.wait_ge(exp_done, n * R + h - 1)
                    s = slice(h * P, (h + 1) * P)
                    for a in range(2):
                        k = slice(a * HALF, (a + 1) * HALF)
                        last = passes(nc, scores[h % 2][:, a, 0:HALF], [(qH[:, s], qL[:, s], kH[:, k], kL[:, k])])
                    last.then_inc(scored, 1)

                def turn_probs(s, buffer, j):
                    if j == 0:
                        pe.wait_ge(normed, s + 1)
                        wait(pe, pt_lo, s * JT)
                    elif j == 1 and works:
                        pe.wait_ge(q_lo, n + 1)
                    else:
                        pe.wait_ge(pt_lo, s * JT + j - 1)
                    for h in range(R):
                        last = nc.tensor.transpose(turned[BANK[j]][:, h * P:(h + 1) * P],
                                                   prob[buffer][:, h, j * P:(j + 1) * P], ident[:, :])
                    last.then_inc(prob_turned, 1)

                def times_values(j):
                    s = n - 1
                    pe.wait_ge(pt_lo, s * JT + j + 1)
                    if j == 0:
                        pe.wait_ge(v_lo, n)
                        wait(pe, added, n - 1)
                    t = (q + j) % 2
                    passes(nc, p_o[:, :], [(vH[q][:, j, :], vL[q][:, j, :], ptH[t][:, :], ptL[t][:, :])],
                           first=j == 0, last=j == JT - 1).then_inc(pv_done, 1)

                def project_kv():
                    base = ((m // B) % 2) * REGION
                    pe.wait_ge(x_lo, m + 1)
                    wait(pe, w_lo, n)
                    wait(pe, sums_ok, m)
                    for i in range(C):
                        at = bass.ds(base + i * QKV + R * P, 2 * P)
                        last = passes(nc, p_q[:, 0:2 * P], [(xH[q][:, i, :], xL[q][:, i, :], wH[:, at], wL[:, at])],
                                      first=i == 0, last=i == C - 1)
                    last.then_inc(kv_done, 1)

                def project_q():
                    base = ((m // B) % 2) * REGION
                    pe.wait_ge(kv_copied, m + 1)
                    for i in range(C):
                        at = bass.ds(base + i * QKV, R * P)
                        last = passes(nc, p_q[:, :], [(xH[q][:, i, :], xL[q][:, i, :], wH[:, at], wL[:, at])],
                                      first=i == 0, last=i == C - 1)
                    last.then_inc(q_done, 1)

                def project_out(heads):
                    if heads[0] == 0:
                        pe.wait_ge(o_lo, n - 1)
                    base = (((n - 2) // B) % 2) * REGION + C * QKV
                    for h in heads:
                        s = slice(h * P, (h + 1) * P)
                        at = bass.ds(base + h * D, D)
                        last = passes(nc, p_o[:, :], [(oH[:, s], oL[:, s], wH[:, at], wL[:, at])],
                                      first=h == 0, last=h == R - 1)
                    if heads[-1] == R - 1:
                        last.then_inc(out_done, 1)

                def turn_cached_keys():
                    pe.wait_ge(kv_in[q], 16 * NPAGE * (m // 2 + 1))
                    if works:
                        pe.wait_ge(exp_done, n * R + 3)
                    for t in range(KT):
                        last = nc.tensor.transpose(scores[0][:, 1, t * P:(t + 1) * P], kv_raw[q][:, t, 0, :],
                                                   ident[:, :])
                    last.then_inc(cache_turned, 1)

                def turn_new_keys():
                    pe.wait_ge(k_ready, m + 1)
                    nc.tensor.transpose(scores[0][:, 0, 0:P], k_rot[:, :], ident[:, :]).then_inc(k_turned, 1)

                def turn_queries():
                    pe.wait_ge(q_ready, m + 1)
                    if ends:
                        pe.wait_ge(pt_lo, (n - 1) * JT + 4)
                    elif works:
                        pe.wait_ge(q_lo, n + 1)
                    for h in range(R):
                        last = nc.tensor.transpose(turned[1][:, h * P:(h + 1) * P], q_u[:, h, :], ident[:, :])
                    last.then_inc(q_turned, 1)

                if works:
                    score(0)
                if ends:
                    turn_probs(n - 1, q, 1)
                if begins:
                    project_kv()
                if outs:
                    project_out((0, 1))
                if works:
                    score(1)
                if outs:
                    project_out((2, 3))
                if works:
                    score(2)
                if ends:
                    turn_probs(n - 1, q, 2)
                    times_values(0)
                if works:
                    score(3)
                if begins:
                    project_q()
                if ends:
                    times_values(1)
                    turn_probs(n - 1, q, 3)
                    times_values(2)
                    turn_probs(n - 1, q, 4)
                if begins:
                    turn_cached_keys()
                    turn_new_keys()
                if ends:
                    times_values(3)
                if begins:
                    turn_queries()
                if ends:
                    times_values(4)
                if works:
                    turn_probs(n, p, 0)

            steps(pe, turn)


def last_layer(nc, acc, ident, coeffs, minus_one, mask, w3, w3_in, bias3, out):
    ctx = ExitStack()
    with ctx:
        def sbuf(name, shape, dt=FP32):
            return ctx.enter_context(nc.sbuf_tensor(name, shape, dt))

        def psum(name, shape):
            return ctx.enter_context(nc.psum_tensor(name, shape, FP32))

        def sem(name):
            return ctx.enter_context(nc.semaphore(name))

        w3H = sbuf("w3H", [P, C, D], F32R)
        w3L = sbuf("w3L", [P, C, D], F32R)
        bi3 = sbuf("bi3", [P, D])
        raw_mask = [sbuf(f"raw_mask{i}", [P, C, D], I32) for i in range(2)]
        signs = [sbuf(f"signs{i}", [P, C, D], F32R) for i in range(2)]
        row = [sbuf(f"row{i}", [P, D]) for i in range(2)]
        tH = [sbuf(f"tH{i}", [P, C * P], F32R) for i in range(2)]
        tL = [sbuf(f"tL{i}", [P, C * P], F32R) for i in range(2)]
        row_bias = [sbuf(f"row_bias{i}", [P, D]) for i in range(2)]
        part = [sbuf(f"part{i}", [P, D]) for i in range(2)]
        y = [sbuf(f"y{i}", [P, D]) for i in range(2)]
        pT = [psum(f"pT{i}", [P, D]) for i in range(2)]
        pO = [psum(f"pO{i}", [P, D]) for i in range(2)]
        pS = [psum(f"pS{i}", [P, D]) for i in range(2)]
        bias_in, mask_in = sem("bias_in"), [sem("mask_in0"), sem("mask_in1")]
        w3_hi, w3_lo, row_ok, signs_ok, row_bias_ok = (sem(x) for x in (
            "w3_hi", "w3_lo", "row_ok", "signs_ok", "row_bias_ok"))
        row_turned, t_hi, t_lo, o_done, s_done, part_ok, y_ok = (sem(x) for x in (
            "row_turned", "t_hi", "t_lo", "o_done", "s_done", "part_ok", "y_ok"))
        stored = [sem("stored0"), sem("stored1")]
        act_held, pool_held = sem("act_held"), sem("pool_held")
        block = ctx.enter_context(nc.Block())

        def hold(engine, held, semaphore, value):
            if isinstance(value, int):
                wait(engine, semaphore, value)
                return
            engine.wait_ge(semaphore, value)
            engine.sem_inc(held, 1)

        def all_rows(engine, turn):
            turn(0, 0)
            turn(1, 1)
            with engine.Fori(1, B // 2 - 1) as i:
                turn(i * 2, 0)
                turn(i * 2 + 1, 1)
            turn(B - 2, 0)
            turn(B - 1, 1)

        def is_last(b):
            return isinstance(b, int) and b == B - 1

        def acc_row(b):
            return acc[:, bass.ds(b, 1), :].rearrange("p o n -> p (o n)")

        @block.sync
        def _(sp):
            def load(b, p):
                wait(sp, signs_ok, b - 1)
                sp.dma_start(raw_mask[p][:, :, :],
                             mask[bass.ds(b, 1), :, :].rearrange("b (c p) o -> p (b c) o", p=P)
                             ).then_inc(mask_in[p], 16)

            def turn(b, p):
                if not isinstance(b, int) or b + 2 < B:
                    load(b + 2, p)
                sp.wait_ge(y_ok, b + 1)
                sp.dma_start(out[bass.ds(b, 1), :, :].rearrange("b p n -> (b p) n"), y[p][:, :]
                             ).then_inc(stored[p], 16)

            load(0, 0)
            sp.dma_start(bi3[:, :], bias3.rearrange("(o n) -> o n", o=1).broadcast_to([P, D])).then_inc(bias_in, 16)
            load(1, 1)
            all_rows(sp, turn)
            for p in range(2):
                sp.wait_ge(stored[p], 16 * B // 2)
                sp.wait_ge(mask_in[p], 16 * B // 2)

        @block.scalar
        def _(act):
            A = nc.scalar

            def copy_row(b, p):
                hold(act, act_held, row_turned, b - 1)
                A.copy(row[p][:, :], acc_row(b)).then_inc(row_ok, 1)

            def turn(b, p):
                if not is_last(b):
                    copy_row(b + 1, 1 - p)
                act.wait_ge(row_turned, b + 1)
                wait(act, s_done, b - 1)
                A.copy(tH[p][:, :], pT[p][:, :]).then_inc(t_hi, 1)
                act.wait_ge(mask_in[p], 16 * (b // 2 + 1))
                A.activation(signs[p][:, :, :], raw_mask[p][:, :, :], ACT.Identity, bias=minus_one[:, 0:1], scale=2.0
                             ).then_inc(signs_ok, 1)

            copy_row(0, 0)
            act.wait_ge(w3_in, 16)
            A.copy(w3H[:, :, :], w3[:, :, :]).then_inc(w3_hi, 1)
            all_rows(act, turn)

        @block.gpsimd
        def _(pool):
            pool.wait_ge(bias_in, 16)

            def turn(b, p):
                hold(pool, pool_held, part_ok, b - 1)
                nc.gpsimd.tensor_tensor(row_bias[p][:, :], acc_row(b), bi3[:, :], ALU.add).then_inc(row_bias_ok, 1)

            all_rows(pool, turn)

        @block.vector
        def _(dve):
            V = nc.vector

            def low(b, p):
                dve.wait_ge(t_hi, b + 1)
                V.tensor_tensor(tL[p][:, :], pT[p][:, :], tH[p][:, :].bitcast(FP32), ALU.subtract).then_inc(t_lo, 1)

            def turn(b, p):
                if not is_last(b):
                    low(b + 1, 1 - p)
                dve.wait_ge(row_bias_ok, b + 1)
                dve.wait_ge(s_done, b + 1)
                V.scalar_tensor_tensor(part[p][:, :], pS[p][:, :], coeffs[:, bass.ds(b, 1)], row_bias[p][:, :],
                                       ALU.mult, ALU.add).then_inc(part_ok, 1)
                dve.wait_ge(part_ok, b + 1)
                wait(dve, stored[p], 16 * (b // 2))
                V.tensor_tensor(y[p][:, :], pO[p][:, :], part[p][:, :], ALU.add).then_inc(y_ok, 1)

            dve.wait_ge(w3_hi, 1)
            V.tensor_tensor(w3L[:, :, :], w3[:, :, :], w3H[:, :, :].bitcast(FP32), ALU.subtract).then_inc(w3_lo, 1)
            low(0, 0)
            all_rows(dve, turn)

        @block.tensor
        def _(pe):
            def turn_row(b, p):
                pe.wait_ge(row_ok, b + 1)
                wait(pe, t_lo, b - 1)
                for i in range(C):
                    last = nc.tensor.transpose(pT[p][:, i * P:(i + 1) * P], row[p][:, i * P:(i + 1) * P], ident[:, :])
                last.then_inc(row_turned, 1)

            def turn(b, p):
                if not is_last(b):
                    turn_row(b + 1, 1 - p)
                pe.wait_ge(t_lo, b + 1)
                wait(pe, y_ok, b - 1)
                cut = [slice(i * P, (i + 1) * P) for i in range(C)]
                passes(nc, pO[p][:, :], [(tH[p][:, cut[i]], tL[p][:, cut[i]], w3H[:, i, :], w3L[:, i, :])
                                         for i in range(C)]).then_inc(o_done, 1)
                pe.wait_ge(signs_ok, b + 1)
                for i in range(C):
                    matmul(nc, pS[p][:, :], tH[p][:, cut[i]], signs[p][:, i, :], i == 0, False)
                    last = matmul(nc, pS[p][:, :], tL[p][:, cut[i]], signs[p][:, i, :], False, i == C - 1)
                last.then_inc(s_done, 1)

            turn_row(0, 0)
            pe.wait_ge(w3_lo, 1)
            all_rows(pe, turn)


def program(nc, x, xT, seqlens, adapter, table, coeff, mask, codebook, w0, scale_log, loraA, loraBT,
            w1T, bias1, a1T, b1, scaling, wall, wqn, wkn, kv_cache, w3T, bias3, invf, out):
    outer = ExitStack()

    def sbuf(ctx, name, shape, dt=FP32):
        return ctx.enter_context(nc.sbuf_tensor(name, shape, dt))

    def psum(ctx, name, shape, dt=FP32):
        return ctx.enter_context(nc.psum_tensor(name, shape, dt))

    def semaphore(ctx, name):
        return ctx.enter_context(nc.semaphore(name))

    def counted(ctx, *all_names):
        return [semaphore(ctx, n) for n in all_names]

    class Chain:

        def __init__(self, engine, sem):
            self.engine, self.sem, self.n = engine, sem, 0

        def __call__(self, instruction):
            self.n += 1
            instruction.then_inc(self.sem, 1)
            self.engine.wait_ge(self.sem, self.n)

    with outer:
        acc = sbuf(outer, "acc", [P, B, D])
        xTs = sbuf(outer, "xTs", [P, C, B * P])
        qA = sbuf(outer, "qA", [P, B, P])
        qB = sbuf(outer, "qB", [P, B, P])
        kA = sbuf(outer, "kA", [P, B, P])
        kB = sbuf(outer, "kB", [P, B, P])
        ident = sbuf(outer, "ident", [P, P])
        key_no = sbuf(outer, "key_no", [P, 2, HALF])
        late_from = sbuf(outer, "late_from", [P, B])
        pages = sbuf(outer, "pages", [1, B * NPAGE], I32)
        coeffs = sbuf(outer, "coeffs", [P, B])
        minus_one = sbuf(outer, "minus_one", [P, 1])
        w3 = sbuf(outer, "w3", [P, C, D])
        w3_in = semaphore(outer, "w3_in")
        weights = ExitStack()
        wH = sbuf(weights, "wH", [P, 2 * REGION], F32R)
        wL = sbuf(weights, "wL", [P, 2 * REGION], F32R)
        wr0 = sbuf(weights, "wr0", [P, CHUNK])

        prep = ExitStack()
        with prep:
            c1 = prep
            w0TH = sbuf(c1, "w0TH", [P, C, D], F32R)
            w0TL = sbuf(c1, "w0TL", [P, C, D], F32R)
            sel = sbuf(c1, "sel", [P, B])
            toki = sbuf(c1, "toki", [P, 1], I32)
            rowi = sbuf(c1, "rowi", [P, 2], I32)
            rowf = sbuf(c1, "rowf", [P, 2])
            adi = sbuf(c1, "adi", [P, B], I32)
            adf = sbuf(c1, "adf", [P, 3, B])
            scl = sbuf(c1, "scl", [P, 1])
            keyi = sbuf(c1, "keyi", [P, CACHE], I32)
            pgf = sbuf(c1, "pgf", [1, 2, B * NPAGE])
            nwq = sbuf(c1, "nwq", [P, P])
            nwk = sbuf(c1, "nwk", [P, P])
            nn = sbuf(c1, "nn", [P, 2, 64])
            seqf = sbuf(c1, "seqf", [P, B])
            sn = sbuf(c1, "sn", [P, B, 64])
            cs = sbuf(c1, "cs", [P, B, 64])
            setup = ExitStack()
            with setup:
                c = setup
                W = sbuf(c, "W", [P, C, D])
                NR = sbuf(c, "NR", [P, C, D])
                QA = sbuf(c, "QA", [P, C, D])
                DL = sbuf(c, "DL", [P, C, D])
                QB = w3
                QC = sbuf(c, "QC", [P, C, D])
                GT = [sbuf(c, f"GT{i}", [P, C, D], U8) for i in range(3)]
                lA, lB = QC[0:64, 0, :], QC[0:64, 1, :]
                sl = sbuf(c, "sl", [P, C, C])
                ex = sbuf(c, "ex", [P, 6, C * C])
                exi = sbuf(c, "exi", [P, C * C], I32)
                cb = sbuf(c, "cb", [P, 8])
                cbt = sbuf(c, "cbt", [P, 6, 8])
                seqi = sbuf(c, "seqi", [P, B], I32)
                pos = sbuf(c, "pos", [P, B])
                tokf = sbuf(c, "tokf", [P, 1])
                invs = sbuf(c, "invs", [P, 64])
                fr = sbuf(c, "fr", [P, B, 64])
                kk = sbuf(c, "kk", [P, B, 64])
                angle = [sbuf(c, f"angle{i}", [P, B, 64]) for i in range(2)]
                part = cs
                pD = [psum(c, f"pD{i}", [P, D]) for i in range(4)]
                (in_w, in_scale, in_lora, in_x, in_idx, iota_ok, ident_ok, delta_ok, dv, pl, sin_ready, cos_ready, w_tr, w_hi,
                 w_lo, w_eff, trig_in, pos_ok, scaled, cuts, leaves, chosen) = counted(
                    c, "in_w", "in_scale", "in_lora", "in_x", "in_idx", "iota_ok", "ident_ok", "delta_ok", "dv", "pl", "sin_ready",
                    "cos_ready", "w_tr", "w_hi", "w_lo", "w_eff", "trig_in", "pos_ok", "scaled", "cuts", "leaves",
                    "chosen")
                block = c.enter_context(nc.Block())

                def row(ap, n):
                    return ap.rearrange("(o n) -> o n", o=1).broadcast_to([P, n])

                @block.sync
                def _(sp):
                    sp.dma_start(lA, loraA).then_inc(in_lora, 16)
                    sp.dma_start(lB, loraBT).then_inc(in_lora, 16)
                    sp.dma_start(cb[:, :], row(codebook, 8)).then_inc(in_scale, 16)
                    sp.dma_start(sl[:, :, :], scale_log.rearrange("(t p) g o -> p t (g o)", p=P)).then_inc(in_scale, 16)
                    sp.dma_start(W[:, :, :], w0.rearrange("(t p) i -> p t i", p=P)).then_inc(in_w, 16)
                    sp.dma_start(seqi[:, :], row(seqlens, B)).then_inc(in_idx, 16)
                    sp.dma_start(adi[:, :], row(adapter, B)).then_inc(in_idx, 16)
                    sp.dma_start(invs[:, :], row(invf, 64)).then_inc(in_idx, 16)
                    sp.dma_start(nwq[:, :], row(wqn, P)).then_inc(in_idx, 16)
                    sp.dma_start(nwk[:, :], row(wkn, P)).then_inc(in_idx, 16)
                    sp.dma_start(coeffs[:, :], row(coeff, B)).then_inc(in_idx, 16)
                    sp.dma_start(pages[:, :], table.rearrange("(o b) n -> o (b n)", o=1)).then_inc(in_idx, 16)
                    for a in range(ADAPTERS):
                        sp.dma_start(scl[a * RANK:(a + 1) * RANK, :],
                                     scaling[a:a + 1].rearrange("(o n) -> o n", o=1).broadcast_to([RANK, 1])
                                     ).then_inc(in_idx, 16)
                    sp.dma_start(acc[:, :, :], x.rearrange("b s d -> s b d")).then_inc(in_x, 16)
                    sp.dma_start(xTs[:, :, :], xT).then_inc(in_x, 16)
                    sp.wait_ge(in_x, 32)

                IDX = 16 * (7 + ADAPTERS)

                wide = [P, C * C, P]
                g3 = "p t (g i) -> p (t g) i"
                S, K, F, Y, Z, IV = (ex[:, i, :] for i in range(6))
                sc_b = Z.rearrange("p (n o) -> p n o", o=1).broadcast_to(wide)
                inv_b = IV.rearrange("p (n o) -> p n o", o=1).broadcast_to(wide)

                def requantise(engine, do, tiles):
                    k = slice(tiles.start * C, tiles.stop * C)
                    q, nr, d, w = (x[:, tiles, :] for x in (QA, NR, DL, W))
                    do(engine.tensor_tensor(q, q, nr, ALU.subtract))
                    do(engine.tensor_tensor(q, q, nr, ALU.add))
                    do(engine.tensor_tensor(q.rearrange(g3, g=C), q.rearrange(g3, g=C), sc_b[:, k, :], ALU.mult))
                    engine.tensor_tensor(w, q, d, ALU.add).then_inc(w_eff, 1)

                @block.gpsimd
                def _(pool):
                    do = Chain(pool, pl)
                    Gp = nc.gpsimd
                    do(Gp.memset(ident[:, :], 0.0))
                    Gp.affine_select(out=ident[:, :], in_=ident[:, :], compare_op=ALU.not_equal, fill=1.0,
                                     base=0, pattern=[[-1, P]], channel_multiplier=1).then_inc(ident_ok, 1)
                    Gp.iota(toki[:, :], pattern=[[0, 1]], base=0, channel_multiplier=1).then_inc(iota_ok, 1)
                    Gp.iota(keyi[:, :], pattern=[[1, CACHE]], base=0, channel_multiplier=0).then_inc(iota_ok, 1)
                    pool.wait_ge(in_idx, IDX)
                    pool.wait_ge(pos_ok, 1)
                    do(Gp.tensor_tensor(fr[:, :, :], invs[:, :].rearrange("p (o f) -> p o f", o=1).broadcast_to([P, B, 64]),
                                        pos[:, :].rearrange("p (b o) -> p b o", o=1).broadcast_to([P, B, 64]), ALU.mult))
                    for i, (turn, shift) in enumerate(((0.0, 0.0), (0.25, float(np.float32(np.pi / 2))))):
                        ra = angle[i]
                        do(Gp.tensor_scalar(kk[:, :, :], fr[:, :, :], float(1.0 / TWO_PI), turn, ALU.mult, ALU.add))
                        do(Gp.tensor_scalar(kk[:, :, :], kk[:, :, :], 1.0, MAGIC, ALU.mult, ALU.add))
                        do(Gp.tensor_scalar(kk[:, :, :], kk[:, :, :], 1.0, -MAGIC, ALU.mult, ALU.add))
                        for k, (pi_part, full) in enumerate(((PI_A, fr), (PI_B, ra), (PI_C, ra))):
                            do(Gp.tensor_scalar(part[:, :, :], kk[:, :, :], -pi_part, 0.0, ALU.mult, ALU.add))
                            do(Gp.tensor_tensor(ra[:, :, :], part[:, :, :], full[:, :, :], ALU.add))
                        if turn:
                            pool.wait_ge(chosen, 1)
                            requantise(Gp, do, slice(C - 1, C))
                            do(Gp.tensor_scalar(ra[:, :, :], ra[:, :, :], 1.0, shift, ALU.mult, ALU.add))
                        Gp.tensor_scalar(ra[:, :, :], ra[:, :, :], BELOW_PI, -BELOW_PI, ALU.min, ALU.max
                                         ).then_inc(trig_in, 1)

                @block.scalar
                def _(act):
                    for i in range(C):
                        act.wait_ge(delta_ok, i + 1)
                        nc.scalar.activation(DL[:, i, :], pD[i][:, :], ACT.Identity, scale=LORA_SCALE
                                             ).then_inc(scaled, 1)
                    for k, (o, i) in enumerate(((QA, 0), (QB, 2), (QC, 4), (W, 6))):
                        act.wait_ge(cuts, k + 1)
                        nc.scalar.activation(o[:, :, :], o[:, :, :], ACT.Identity, bias=cbt[:, 1, i:i + 1]
                                             ).then_inc(leaves, 1)
                    act.wait_ge(trig_in, 1)
                    nc.scalar.activation(sn[:, :, :], angle[0][:, :, :], ACT.Sin).then_inc(sin_ready, 1)
                    act.wait_ge(trig_in, 2)
                    nc.scalar.activation(cs[:, :, :], angle[1][:, :, :], ACT.Sin).then_inc(cos_ready, 1)
                    for i in range(C):
                        act.wait_ge(w_tr, i + 1)
                        nc.scalar.copy(w0TH[:, i, :], pD[i][:, :]).then_inc(w_hi, 1)

                @block.tensor
                def _(pe):
                    pe.wait_ge(in_lora, 32)
                    for i in range(C):
                        matmul(nc, pD[i][:, :], QC[0:64, 1, i * P:(i + 1) * P], lA, True, True).then_inc(delta_ok, 1)
                    pe.wait_ge(w_eff, 2)
                    pe.wait_ge(ident_ok, 1)
                    for i in range(C):
                        for t in range(C):
                            last = nc.tensor.transpose(pD[i][:, t * P:(t + 1) * P], W[:, t, i * P:(i + 1) * P],
                                                       ident[:, :])
                        last.then_inc(w_tr, 1)

                @block.vector
                def _(dve):
                    do = Chain(dve, dv)
                    V = nc.vector
                    dve.wait_ge(in_scale, 32)
                    do(V.tensor_reduce(cbt[:, 0, 0:1], cb[:, :], AX.X, ALU.max, apply_absolute_value=True))
                    do(V.tensor_scalar(cbt[:, 0, 0:1], cbt[:, 0, 0:1], 1e-8, None, ALU.max))
                    do(V.reciprocal(cbt[:, 0, 1:2], cbt[:, 0, 0:1]))
                    do(V.tensor_scalar(cbt[:, 1, :], cb[:, :], cbt[:, 0, 1:2], None, ALU.mult))
                    do(V.tensor_tensor(cbt[:, 2, 0:7], cbt[:, 1, 0:7], cbt[:, 1, 1:8], ALU.add))
                    do(V.tensor_scalar(cbt[:, 2, 0:7], cbt[:, 2, 0:7], 0.5, None, ALU.mult))
                    do(V.tensor_tensor(cbt[:, 3, 0:7], cbt[:, 1, 1:8], cbt[:, 1, 0:7], ALU.subtract))
                    s_in = sl[:, :, :].rearrange("p t g -> p (t g)")
                    do(V.tensor_scalar(S, s_in, 88.0, -87.0, ALU.min, ALU.max))
                    do(V.tensor_scalar(K, S, float(np.log2(np.e)), None, ALU.mult))
                    do(V.tensor_scalar(K, K, MAGIC, None, ALU.add))
                    do(V.tensor_scalar(K, K, MAGIC, None, ALU.subtract))
                    do(V.scalar_tensor_tensor(F, K, -LN2_A, S, ALU.mult, ALU.add))
                    do(V.scalar_tensor_tensor(F, K, -LN2_B, F, ALU.mult, ALU.add))
                    do(V.tensor_scalar(Y, F, 1.0 / 5040.0, None, ALU.mult))
                    for cf in (720.0, 120.0, 24.0, 6.0, 2.0, 1.0):
                        do(V.scalar_tensor_tensor(Y, Y, 1.0 / cf, F, ALU.add, ALU.mult))
                    do(V.tensor_scalar(Y, Y, 1.0, None, ALU.add))
                    do(V.tensor_scalar(exi[:, :], K, 127.0, None, ALU.add))
                    do(V.tensor_scalar(exi[:, :], exi[:, :], 23, None, ALU.logical_shift_left))
                    do(V.tensor_tensor(Z, Y, exi[:, :].bitcast(FP32), ALU.mult))
                    do(V.reciprocal(IV, Z))
                    dve.wait_ge(in_w, 16)
                    for t in range(C):
                        dve.wait_ge(scaled, t + 1)
                        do(V.tensor_tensor(W[:, t, :], W[:, t, :], DL[:, t, :], ALU.add))
                    dve.wait_ge(in_idx, IDX)
                    dve.wait_ge(iota_ok, 2)
                    do(V.tensor_copy(seqf[:, :], seqi[:, :]))
                    do(V.tensor_copy(tokf[:, :], toki[:, :]))
                    V.tensor_scalar(pos[:, :], seqf[:, :], tokf[:, 0:1], None, ALU.add).then_inc(pos_ok, 1)
                    do(V.tensor_tensor(NR[:, :, :].rearrange(g3, g=C), W[:, :, :].rearrange(g3, g=C), inv_b, ALU.mult))
                    for k, (o, i) in enumerate(((QA, 0), (QB, 2), (QC, 4), (W, 6))):
                        V.tensor_scalar(o[:, :, :], NR[:, :, :], cbt[:, 2, i:i + 1], cbt[:, 3, i:i + 1],
                                        ALU.is_gt, ALU.mult).then_inc(cuts, 1)
                    for g, i in zip(GT, (1, 5, 3)):
                        do(V.tensor_scalar(g[:, :, :], NR[:, :, :], cbt[:, 2, i:i + 1], None, ALU.is_gt))
                    dve.wait_ge(leaves, 2)
                    do(V.copy_predicated(QA[:, :, :], GT[0][:, :, :], QB[:, :, :]))
                    dve.wait_ge(leaves, 4)
                    do(V.copy_predicated(QC[:, :, :], GT[1][:, :, :], W[:, :, :]))
                    V.copy_predicated(QA[:, :, :], GT[2][:, :, :], QC[:, :, :]).then_inc(chosen, 1)
                    dve.wait_ge(chosen, 1)
                    requantise(V, do, slice(0, C - 1))
                    for i in range(C):
                        dve.wait_ge(w_hi, i + 1)
                        V.tensor_tensor(w0TL[:, i, :], pD[i][:, :], w0TH[:, i, :].bitcast(FP32), ALU.subtract
                                        ).then_inc(w_lo, 1)

            dense = ExitStack()
            with dense:
                c = dense
                w1r = w3
                a1r = sbuf(c, "a1r", [P, C, P])
                b1r = sbuf(c, "b1r", [P, D])
                bi1 = sbuf(c, "bi1", [P, D])
                w1H = sbuf(c, "w1H", [P, C, D], F32R)
                w1L = sbuf(c, "w1L", [P, C, D], F32R)
                a1H = sbuf(c, "a1H", [P, C, P], F32R)
                a1L = sbuf(c, "a1L", [P, C, P], F32R)
                b1H = sbuf(c, "b1H", [P, D], F32R)
                b1L = sbuf(c, "b1L", [P, D], F32R)
                wr = [wr0, sbuf(c, "wr1", [P, CHUNK])]
                xsH = [sbuf(c, f"xsH{i}", [P, C, P], F32R) for i in range(2)]
                xsL = [sbuf(c, f"xsL{i}", [P, C, P], F32R) for i in range(2)]
                lo_f = sbuf(c, "lo_f", [P, P])
                loH = sbuf(c, "loH", [P, P], F32R)
                loL = sbuf(c, "loL", [P, P], F32R)
                ys = [sbuf(c, f"ys{i}", [P, D]) for i in range(2)]
                yn = sbuf(c, "yn", [P, D])
                pY = [psum(c, f"pY{i}", [P, D]) for i in range(2)]
                pX = [psum(c, f"pX{i}", [P, D]) for i in range(2)]
                pL = psum(c, "pL", [P, P])
                (small_steps, table_steps, neg_ok) = counted(c, "small_steps", "table_steps", "neg_ok")
                (w1_in, w1_hi, w1_lo, xs_hi, xs_lo, low_done, low_f, low_hi, low_lo, y_done, y_out, y_mid, acc_in,
                 t_done, t_out, c_in0, c_in1, c_hi, c_lo, act_passed) = counted(
                    c, "w1_in", "w1_hi", "w1_lo", "xs_hi", "xs_lo", "low_done", "low_f", "low_hi", "low_lo", "y_done",
                    "y_out", "y_mid", "acc_in", "t_done", "t_out", "c_in0", "c_in1", "c_hi", "c_lo", "act_passed")
                c_in = [c_in0, c_in1]
                block = c.enter_context(nc.Block())

                def rotation_tables(engine, do, A_t, B_t, nw, neg):
                    for o, trig, w in ((A_t[:, :, 0:64], cs, nw[:, 0:64]), (A_t[:, :, 64:P], cs, nw[:, 64:P]),
                                       (B_t[:, :, 0:64], sn, neg), (B_t[:, :, 64:P], sn, nw[:, 0:64])):
                        do(engine.tensor_tensor(o, trig[:, :, :],
                                                w.rearrange("p (o f) -> p o f", o=1).broadcast_to([P, B, 64]),
                                                ALU.mult))

                def rows(engine, body, first, last):
                    while first % 2:
                        body(first, first % B, first % 2)
                        first += 1
                    end = last + 1 - (last + 1 - first) % 2
                    with engine.Fori(0, (end - first) // 2) as i:
                        for p in range(2):
                            body(i * 2 + (first + p), i * 2 + (first + p) % B, p)
                    for n in range(end, last + 1):
                        body(n, n % B, n % 2)

                @block.sync
                def _(sp):
                    sp.dma_start(w1r[:, :, :], w1T).then_inc(w1_in, 16)
                    sp.dma_start(a1r[:, :, :], a1T).then_inc(w1_in, 16)
                    sp.dma_start(b1r[:, :], b1).then_inc(w1_in, 16)
                    sp.dma_start(bi1[:, :], bias1.rearrange("(o n) -> o n", o=1).broadcast_to([P, D])
                                 ).then_inc(w1_in, 16)
                    for m in range(LEAD):
                        wait(sp, c_lo, m - 1)
                        sp.dma_start(wr[m % 2][:, :], wall[m]).then_inc(c_in[m % 2], 16)
                    sp.wait_ge(w1_in, 64)

                @block.gpsimd
                def _(pool):
                    def rounded(o, full):
                        return nc.gpsimd.tensor_scalar(o, full, 1.0, 1.0, ALU.mult, ALU.mult)

                    pool.wait_ge(w1_in, 64)
                    rounded(w1H[:, :, :], w1r[:, :, :]).then_inc(w1_hi, 1)
                    rounded(a1H[:, :, :], a1r[:, :, :]).then_inc(w1_hi, 1)
                    rounded(b1H[:, :], b1r[:, :]).then_inc(w1_hi, 1)
                    pool.wait_ge(w1_hi, 3)
                    nc.gpsimd.tensor_tensor(w1L[:, :, :], w1r[:, :, :], w1H[:, :, :].bitcast(FP32), ALU.subtract
                                            ).then_inc(w1_lo, 1)
                    nc.gpsimd.tensor_tensor(a1L[:, :, :], a1r[:, :, :], a1H[:, :, :].bitcast(FP32), ALU.subtract
                                            ).then_inc(w1_lo, 1)
                    nc.gpsimd.tensor_tensor(b1L[:, :], b1r[:, :], b1H[:, :].bitcast(FP32), ALU.subtract
                                            ).then_inc(w1_lo, 1)
                    for m in range(LEAD):
                        at = slice(m * CHUNK, (m + 1) * CHUNK)
                        pool.wait_ge(c_in[m % 2], 16 * (m // 2 + 1))
                        rounded(wH[:, at], wr[m % 2][:, :]).then_inc(c_hi, 1)
                        pool.wait_ge(c_hi, m + 1)
                        nc.gpsimd.tensor_tensor(wL[:, at], wr[m % 2][:, :], wH[:, at].bitcast(FP32), ALU.subtract
                                                ).then_inc(c_lo, 1)
                    do = Chain(pool, table_steps)
                    pool.wait_ge(neg_ok, 2)
                    rotation_tables(nc.gpsimd, do, qA, qB, nwq, nn[:, 0, :])
                    rotation_tables(nc.gpsimd, do, kA, kB, nwk, nn[:, 1, :])

                @block.scalar
                def _(act):
                    def hold(sem, value):
                        if isinstance(value, int) and value <= 0:
                            return
                        act.wait_ge(sem, value)
                        if not isinstance(value, int):
                            act.sem_inc(act_passed, 1)

                    def split_row(n, b, p, layer):
                        hold(y_done, n - 1)
                        if layer == 1:
                            hold(t_out, n - (B - 1))
                        nc.scalar.copy(xsH[p][:, :, :], xTs[:, :, bass.ds(b * P, P)]).then_inc(xs_hi, 1)

                    def finish_row(n, b, p):
                        hold(y_out, n + 1)
                        nc.scalar.copy(acc[:, bass.ds(b, 1), :].rearrange("p o n -> p (o n)"), ys[p][:, :]
                                       ).then_inc(acc_in, 1)
                        hold(t_done, n + 1)
                        nc.scalar.copy(xTs[:, :, bass.ds(b * P, P)], pX[p][:, :].rearrange("p (c t) -> p c t", c=C)
                                       ).then_inc(t_out, 1)

                    def body0(n, b, p):
                        split_row(n + 2, b + 2, p, 0)
                        finish_row(n, b, p)

                    def body1(n, b, p):
                        split_row(n + 2, b + 2, p, 1)
                        finish_row(n, b, p)

                    split_row(0, 0, 0, 0)
                    split_row(1, 1, 1, 0)
                    body0(0, 0, 0)
                    body0(1, 1, 1)
                    rows(act, body0, 2, 5)
                    for n in (6, 7):
                        split_row(n + 2, n + 2 - B, n % 2, 1)
                        finish_row(n, n, n % 2)
                    rows(act, body1, 8, 13)
                    for n in (14, 15):
                        finish_row(n, n - B, n % 2)

                @block.vector
                def _(dve):
                    V = nc.vector

                    def low_part(n, b, p):
                        dve.wait_ge(xs_hi, n + 1)
                        V.tensor_tensor(xsL[p][:, :, :], xTs[:, :, bass.ds(b * P, P)], xsH[p][:, :, :].bitcast(FP32),
                                        ALU.subtract).then_inc(xs_lo, 1)

                    def adapter_part(n, b, p):
                        k = n - B
                        dve.wait_ge(low_done, k + 1)
                        V.tensor_scalar(lo_f[:, :], pL[:, :], sel[:, bass.ds(b, 1)], None, ALU.mult).then_inc(low_f, 1)
                        dve.wait_ge(low_f, k + 1)
                        if not isinstance(n, int) or k >= 1:
                            dve.wait_ge(y_done, n)
                        V.tensor_copy(loH[:, :], lo_f[:, :]).then_inc(low_hi, 1)
                        dve.wait_ge(low_hi, k + 1)
                        V.tensor_tensor(loL[:, :], lo_f[:, :], loH[:, :].bitcast(FP32), ALU.subtract
                                        ).then_inc(low_lo, 1)

                    def sum_row(n, b, p, layer):
                        a = acc[:, bass.ds(b, 1), :].rearrange("p o n -> p (o n)")
                        dve.wait_ge(y_done, n + 1)
                        wait(dve, t_done, n - 1)
                        wait(dve, acc_in, n - 1)
                        if layer == 0:
                            V.tensor_tensor(ys[p][:, :], pY[p][:, :], a, ALU.add).then_inc(y_out, 1)
                        else:
                            V.tensor_tensor(yn[:, :], pY[p][:, :], a, ALU.add).then_inc(y_mid, 1)
                            dve.wait_ge(y_mid, n - B + 1)
                            V.tensor_tensor(ys[p][:, :], yn[:, :], bi1[:, :], ALU.add).then_inc(y_out, 1)

                    low_part(0, 0, 0)
                    low_part(1, 1, 1)
                    do = Chain(dve, small_steps)
                    do(V.tensor_scalar(pgf[:, 0, :], pages[:, :], 0.0, float(PAGES), ALU.is_lt, ALU.mult))
                    do(V.tensor_tensor(pgf[:, 1, :], pgf[:, 0, :], pages[:, :], ALU.add))
                    do(V.tensor_scalar(pages[:, :], pgf[:, 1, :], 0.0, float(PAGES - 1), ALU.max, ALU.min))
                    do(V.tensor_scalar(rowi[:, 0:1], toki[:, :], 4, None, ALU.arith_shift_right))
                    do(V.tensor_copy(rowf[:, 0:1], rowi[:, 0:1]))
                    do(V.tensor_scalar(adf[:, 0, :], adi[:, :], 0.0, float(ADAPTERS), ALU.is_lt, ALU.mult))
                    do(V.tensor_tensor(adf[:, 1, :], adf[:, 0, :], adi[:, :], ALU.add))
                    do(V.tensor_scalar(adf[:, 2, :], adf[:, 1, :], 0.0, float(ADAPTERS - 1), ALU.max, ALU.min))
                    do(V.tensor_scalar(sel[:, :], adf[:, 2, :], rowf[:, 0:1], scl[:, 0:1], ALU.is_equal, ALU.mult))
                    k_flat = key_no[:, :, :].rearrange("p a k -> p (a k)")
                    do(V.memset(k_flat[:, CACHE:KEYS], -2.0 ** 32))
                    do(V.tensor_copy(k_flat[:, 0:CACHE], keyi[:, :]))
                    do(V.tensor_scalar(late_from[:, :], seqf[:, :], -HUGE, 0.5 * HUGE, ALU.mult, ALU.add))
                    do(V.memset(minus_one[:, :], -1.0))
                    V.tensor_scalar(nn[:, 0, :], nwq[:, 64:P], -1.0, None, ALU.mult).then_inc(neg_ok, 1)
                    V.tensor_scalar(nn[:, 1, :], nwk[:, 64:P], -1.0, None, ALU.mult).then_inc(neg_ok, 1)
                    for n in (0, 1):
                        sum_row(n, n, n, 0)
                        low_part(n + 2, n + 2, n)

                    def body0(n, b, p):
                        sum_row(n, b, p, 0)
                        low_part(n + 2, b + 2, p)
                    rows(dve, body0, 2, 5)
                    sum_row(6, 6, 0, 0)
                    low_part(8, 0, 0)
                    sum_row(7, 7, 1, 0)
                    adapter_part(8, 0, 0)
                    low_part(9, 1, 1)
                    sum_row(8, 0, 0, 1)
                    adapter_part(9, 1, 1)
                    low_part(10, 2, 0)

                    def body1(n, b, p):
                        sum_row(n, b, p, 1)
                        adapter_part(n + 1, b + 1, 1 - p)
                        low_part(n + 2, b + 2, p)
                    rows(dve, body1, 9, 13)
                    sum_row(14, 6, 0, 1)
                    adapter_part(15, 7, 1)
                    sum_row(15, 7, 1, 1)

                @block.tensor
                def _(pe):
                    def produce(n, b, p, layer):
                        pe.wait_ge(xs_lo, n + 1)
                        wait(pe, y_out, n - 1)
                        if layer == 0:
                            passes(nc, pY[p][:, :], [(xsH[p][:, i, :], xsL[p][:, i, :], w0TH[:, i, :], w0TL[:, i, :])
                                                  for i in range(C)]).then_inc(y_done, 1)
                            return
                        k = n - B
                        wait(pe, low_f, k)
                        passes(nc, pL[:, :], [(a1H[:, i, :], a1L[:, i, :], xsH[p][:, i, :], xsL[p][:, i, :])
                                           for i in range(C)]).then_inc(low_done, 1)
                        for i in range(C):
                            matmul(nc, pY[p][:, :], xsH[p][:, i, :], w1H[:, i, :], i == 0, False)
                            matmul(nc, pY[p][:, :], xsL[p][:, i, :], w1H[:, i, :], False, False)
                            matmul(nc, pY[p][:, :], xsH[p][:, i, :], w1L[:, i, :], False, False)
                        pe.wait_ge(low_lo, k + 1)
                        matmul(nc, pY[p][:, :], loH[:, :], b1H[:, :], False, False)
                        matmul(nc, pY[p][:, :], loL[:, :], b1H[:, :], False, False)
                        matmul(nc, pY[p][:, :], loH[:, :], b1L[:, :], False, True).then_inc(y_done, 1)

                    def turn(n, b, p):
                        pe.wait_ge(y_out, n + 1)
                        wait(pe, t_out, n - 1)
                        for i in range(C):
                            last = nc.tensor.transpose(pX[p][:, i * P:(i + 1) * P], ys[p][:, i * P:(i + 1) * P],
                                                       ident[:, :])
                        last.then_inc(t_done, 1)

                    produce(0, 0, 0, 0)
                    produce(1, 1, 1, 0)
                    for n in (0, 1):
                        turn(n, n, n)
                        produce(n + 2, n + 2, n, 0)

                    def body0(n, b, p):
                        turn(n, b, p)
                        produce(n + 2, b, p, 0)
                    rows(pe, body0, 2, 5)
                    pe.wait_ge(w1_lo, 3)
                    for n in (6, 7):
                        turn(n, n, n % 2)
                        produce(n + 2, n, n % 2, 1)

                    def body1(n, b, p):
                        turn(n, b, p)
                        produce(n + 2, b, p, 1)
                    body1(8, 0, 0)
                    body1(9, 1, 1)
                    rows(pe, body1, 10, 13)
                    turn(14, 6, 0)
                    turn(15, 7, 1)

        attention(nc, acc, xTs, qA, qB, kA, kB, ident, key_no, late_from, pages, wH, wL, wr0, wall,
                  kv_cache, w3, w3T, w3_in)
        weights.close()
        last_layer(nc, acc, ident, coeffs, minus_one, mask, w3, w3_in, bias3, out)


def kernel(**inputs):
    import numpy as _np
    import concourse.bacc as _bacc
    from concourse import mybir as _mybir
    from concourse.bass_utils import run_bass_kernel_spmd as _run

    given = {k: _np.asarray(v) for k, v in inputs.items()}

    def columns(w):
        return w.T.reshape(C, P, w.shape[0]).transpose(1, 0, 2)

    wq, wk, wv = (columns(given[f"L2_cond_W{n}"]) for n in "qkv")
    wo = given["L2_cond_Wo"].T.reshape(G, R, P, D).transpose(0, 2, 1, 3)
    heads = []
    for g in range(G):
        qkv = _np.concatenate([wq[:, :, g * R * P:(g + 1) * R * P], wk[:, :, g * P:(g + 1) * P],
                               wv[:, :, g * P:(g + 1) * P]], axis=2).reshape(P, C * QKV)
        whole = _np.concatenate([qkv, wo[g].reshape(P, R * D)], axis=1)
        heads.append(whole.reshape(P, CHUNKS, CHUNK).transpose(1, 0, 2))
    inv_freq = (1.0 / _np.float32(10000.0) ** (_np.arange(0, P, 2, dtype=_np.float32) / _np.float32(P))
                ).astype(_np.float32)
    layout = {
        "x": given["x"],
        "xT": given["x"].reshape(B * P, D).T.reshape(C, P, B * P).transpose(1, 0, 2),
        "seqlens": given["itok_B_207_1644"],
        "adapter": given["itok_B_1_7"],
        "table": given["itok_Bx16_0_63"],
        "coeff": given["condB_coeff"],
        "mask": given["mask_Bx4096x4096_ik1"],
        "codebook": given["condB_codebook"],
        "w0": given["L0_cond_weight"],
        "scale_log": given["L0_cond_scale_log"],
        "loraA": given["L0_cond_lora_A"],
        "loraBT": given["L0_cond_lora_B"].T,
        "w1T": columns(given["L1_cond_weight"]),
        "bias1": given["L1_cond_bias"],
        "a1T": columns(given["L1_cond_lora_a_weights"].reshape(P, D)),
        "b1": given["L1_cond_lora_b_weights"].transpose(0, 2, 1).reshape(P, D),
        "scaling": given["L1_cond_scaling_factors"],
        "wall": _np.concatenate(heads, axis=0),
        "wqn": given["L2_cond_q_norm_w"],
        "wkn": given["L2_cond_k_norm_w"],
        "kv_cache": _np.concatenate([given["L2_cond_k_cache"], given["L2_cond_v_cache"]], axis=3).transpose(0, 2, 1, 3),
        "w3T": columns(given["L3_cond_W"]),
        "bias3": given["L3_cond_b"],
        "invf": inv_freq,
    }
    nc = _bacc.Bacc("TRN2", target_bir_lowering=False, num_devices=1, dynamic_dma_scratch_size=1024)
    arrays, args = {}, {}
    for name, a in layout.items():
        a = _np.ascontiguousarray(a)
        arrays[f"in_{name}"] = a
        args[name] = nc.dram_tensor(f"in_{name}", a.shape, _mybir.dt.from_np(a.dtype), kind="ExternalInput").ap()
    args["out"] = nc.dram_tensor("out", (B, P, D), _mybir.dt.from_np(_np.dtype("float32")),
                                 kind="ExternalOutput").ap()
    program(nc, **args)
    r = _run(nc, [arrays], core_ids=[0])
    return r.results[0]["out"]
```
